# Optimizing a Trainium2 kernel written in Bass

```python
import numpy as np
import jax
import jax.numpy as jnp

def _softmax(x, axis=-1):
    return jax.nn.softmax(x, axis=axis)

def _gelu(x):
    return jax.nn.gelu(x, approximate=True)

def _silu(x):
    return jax.nn.silu(x)

def _sigmoid(x):
    return jax.nn.sigmoid(x)

def _layernorm(x, axis=-1, eps=1e-05):
    m = jnp.mean(x, axis=axis, keepdims=True)
    v = jnp.var(x, axis=axis, keepdims=True)
    return (x - m) / jnp.sqrt(v + eps)

def _scatter_add(tgt, idx, src, axis=0):
    return tgt.at[idx].add(src)

def _segment_sum(src, seg, n):
    return jax.ops.segment_sum(src, seg, n)
kernel_name = 'mk_gnn_resnorm_d4_gnn_r32_dee1c2'

def setup_inputs(seed: int=0):
    np.random.seed(seed)
    _w = jnp.asarray

    def _rec_inputs():
        import jax
        import jax.numpy as jnp
        _gk = jax.random.key(seed)
        x = -0.0002117 + 1 * jax.random.normal(jax.random.fold_in(_gk, 1), (3125, 256), jnp.float32)
        _s = jax.random.randint(jax.random.fold_in(_gk, 2), (25000,), 0, 3125, jnp.int32)
        _d = jax.random.randint(jax.random.fold_in(_gk, 3), (25000,), 0, 3125, jnp.int32)
        _loop = jnp.arange(3125, dtype=jnp.int32)
        src = jnp.concatenate([_s, _d, _loop])
        dst = jnp.concatenate([_d, _s, _loop])
        _o = jnp.argsort(dst, stable=True)
        src = src[_o]
        dst = dst[_o]
        edge_attr_8 = -0.00019784 + 0.999804 * jax.random.normal(jax.random.fold_in(_gk, 12), (53125, 8), jnp.float32)
        edge_type_16 = jax.random.randint(jax.random.fold_in(_gk, 14), (53125,), 0, 16, jnp.int32)
        edge_weight = jax.random.uniform(jax.random.fold_in(_gk, 15), (53125,), jnp.float32, 0.0, 1)
        return (x, src, dst, edge_attr_8, edge_type_16, edge_weight)
    x, src, dst, edge_attr_8, edge_type_16, edge_weight = _rec_inputs()

    def _L0_gnn_setup():
        import jax, jax.numpy as jnp
        import numpy as np
        N_NODES = 3125
        N_EDGES = 100000
        D_IN = 256
        D_OUT = 256
        key = jax.random.key(seed)
        k1, k2, k3, k4, k5 = jax.random.split(key, 5)
        X = jax.random.normal(k1, (N_NODES, D_IN), dtype=jnp.float32)
        edge_row = jax.random.randint(k2, (N_EDGES,), 0, N_NODES, dtype=jnp.int32)
        edge_col = jax.random.randint(k3, (N_EDGES,), 0, N_NODES, dtype=jnp.int32)
        edge_val = jax.random.uniform(k4, (N_EDGES,), dtype=jnp.float32)
        W = jax.random.normal(k5, (D_OUT, D_IN), dtype=jnp.float32) * (6.0 / (D_IN + D_OUT)) ** 0.5
        b = jnp.zeros((D_OUT,), dtype=jnp.float32)
        return {'X': X, 'edge_row': edge_row, 'edge_col': edge_col, 'edge_val': edge_val, 'W': W, 'b': b}
    _L0_gnn_all = _L0_gnn_setup()
    _L0_gnn_in = {k: v for k, v in _L0_gnn_all.items() if k in ('W', 'b')}
    del _L0_gnn_all

    def _L1_gnn_setup():
        import jax, jax.numpy as jnp
        import numpy as np
        N = 3125
        E = 25000
        FEAT = 256
        HEADS = 8
        HEAD_DIM = FEAT // HEADS
        SCALING = HEAD_DIM ** (-0.5)
        key = jax.random.key(seed)
        ks = jax.random.split(key, 8)
        w_scale = (2.0 / (FEAT + FEAT)) ** 0.5
        return {'nfeat': jax.random.normal(ks[0], (N, FEAT), dtype=jnp.float32), 'attn_bias': jax.random.normal(ks[1], (E, HEADS), dtype=jnp.float32), 'Wq': jax.random.normal(ks[2], (FEAT, FEAT), dtype=jnp.float32) * w_scale, 'Wk': jax.random.normal(ks[3], (FEAT, FEAT), dtype=jnp.float32) * w_scale, 'Wv': jax.random.normal(ks[4], (FEAT, FEAT), dtype=jnp.float32) * w_scale, 'Wo': jax.random.normal(ks[5], (FEAT, FEAT), dtype=jnp.float32) * w_scale, 'src': jax.random.randint(ks[6], (E,), 0, N, dtype=jnp.int32), 'dst': jax.random.randint(ks[7], (E,), 0, N, dtype=jnp.int32)}
    _L1_gnn_all = _L1_gnn_setup()
    _L1_gnn_in = {k: v for k, v in _L1_gnn_all.items() if k in ('Wq', 'Wk', 'Wv', 'Wo')}
    del _L1_gnn_all

    def _L2_gnn_setup():
        import jax, jax.numpy as jnp
        import numpy as np
        N_NODES = 50000
        N_EDGES = 25000
        HDIM = 256
        NUMRELS = 16

        def _gru_cell(x, h, w_ih, w_hh, b_ih, b_hh):
            gi = x @ w_ih.T + b_ih
            gh = h @ w_hh.T + b_hh
            i_r, i_z, i_n = jnp.split(gi, 3, axis=-1)
            h_r, h_z, h_n = jnp.split(gh, 3, axis=-1)
            r = jax.nn.sigmoid(i_r + h_r)
            z = jax.nn.sigmoid(i_z + h_z)
            n = jnp.tanh(i_n + r * h_n)
            return (1.0 - z) * n + z * h
        key = jax.random.key(seed)
        ks = jax.random.split(key, 9)
        h = jax.random.normal(ks[0], (N_NODES, HDIM), dtype=jnp.float32)
        relvectors = jax.random.normal(ks[1], (NUMRELS, HDIM), dtype=jnp.float32)
        s = 1.0 / np.sqrt(HDIM)
        w_ih = jax.random.uniform(ks[2], (3 * HDIM, HDIM), minval=-s, maxval=s, dtype=jnp.float32)
        w_hh = jax.random.uniform(ks[3], (3 * HDIM, HDIM), minval=-s, maxval=s, dtype=jnp.float32)
        b_ih = jax.random.uniform(ks[4], (3 * HDIM,), minval=-s, maxval=s, dtype=jnp.float32)
        b_hh = jax.random.uniform(ks[5], (3 * HDIM,), minval=-s, maxval=s, dtype=jnp.float32)
        edge_src = jax.random.randint(ks[6], (N_EDGES,), 0, N_NODES, dtype=jnp.int32)
        edge_dst = jax.random.randint(ks[7], (N_EDGES,), 0, N_NODES, dtype=jnp.int32)
        edge_rel = jax.random.randint(ks[8], (N_EDGES,), 0, NUMRELS, dtype=jnp.int32)
        return {'h': h, 'relvectors': relvectors, 'w_ih': w_ih, 'w_hh': w_hh, 'b_ih': b_ih, 'b_hh': b_hh, 'edge_src': edge_src, 'edge_dst': edge_dst, 'edge_rel': edge_rel}
    _L2_gnn_all = _L2_gnn_setup()
    _L2_gnn_in = {k: v for k, v in _L2_gnn_all.items() if k in ('relvectors', 'w_ih', 'w_hh', 'b_ih', 'b_hh')}
    del _L2_gnn_all

    def _L3_gnn_setup():
        import jax, jax.numpy as jnp
        import numpy as np
        N_NODES = 50000

        def gcn_conv(x, src, dst, W, b):
            N = x.shape[0]
            h = x @ W
            ones = jnp.ones(dst.shape, dtype=h.dtype)
            deg = jax.ops.segment_sum(ones, dst, num_segments=N) + 1.0
            dinv = jax.lax.rsqrt(deg)
            norm = dinv[src] * dinv[dst]
            agg = jax.ops.segment_sum(h[src] * norm[:, None], dst, num_segments=N)
            agg = agg + h * (dinv * dinv)[:, None]
            return agg + b
        key = jax.random.key(seed)
        ks = jax.random.split(key, 8)
        in_dim, mid_dim, out_dim, fc_mid, proj_dim = (256, 128, 64, 128, 256)
        n_edges = 25000
        x = jax.random.normal(ks[0], (N_NODES, in_dim), dtype=jnp.float32)
        edge_index = jax.random.randint(ks[1], (2, n_edges), 0, N_NODES, dtype=jnp.int64)

        def glorot(k, fan_in, fan_out):
            lim = np.sqrt(6.0 / (fan_in + fan_out)).astype(np.float32)
            return jax.random.uniform(k, (fan_in, fan_out), jnp.float32, -lim, lim)
        return {'x': x, 'edge_index': edge_index, 'W1': glorot(ks[2], in_dim, mid_dim), 'b1': jnp.zeros((mid_dim,), jnp.float32), 'W2': glorot(ks[3], mid_dim, out_dim), 'b2': jnp.zeros((out_dim,), jnp.float32), 'fc1_w': glorot(ks[4], out_dim, fc_mid), 'fc1_b': jnp.zeros((fc_mid,), jnp.float32), 'fc2_w': glorot(ks[5], fc_mid, proj_dim), 'fc2_b': jnp.zeros((proj_dim,), jnp.float32)}
    _L3_gnn_all = _L3_gnn_setup()
    _L3_gnn_in = {k: v for k, v in _L3_gnn_all.items() if k in ('W1', 'b1', 'W2', 'b2', 'fc1_w', 'fc1_b', 'fc2_w', 'fc2_b')}
    del _L3_gnn_all
    return {'x': x, 'src': src, 'dst': dst, 'edge_attr_8': edge_attr_8, 'edge_type_16': edge_type_16, 'edge_weight': edge_weight, 'L0_gnn_W': _L0_gnn_in['W'], 'L0_gnn_b': _L0_gnn_in['b'], 'L1_gnn_Wq': _L1_gnn_in['Wq'], 'L1_gnn_Wk': _L1_gnn_in['Wk'], 'L1_gnn_Wv': _L1_gnn_in['Wv'], 'L1_gnn_Wo': _L1_gnn_in['Wo'], 'L2_gnn_relvectors': _L2_gnn_in['relvectors'], 'L2_gnn_w_ih': _L2_gnn_in['w_ih'], 'L2_gnn_w_hh': _L2_gnn_in['w_hh'], 'L2_gnn_b_ih': _L2_gnn_in['b_ih'], 'L2_gnn_b_hh': _L2_gnn_in['b_hh'], 'L3_gnn_W1': _L3_gnn_in['W1'], 'L3_gnn_b1': _L3_gnn_in['b1'], 'L3_gnn_W2': _L3_gnn_in['W2'], 'L3_gnn_b2': _L3_gnn_in['b2'], 'L3_gnn_fc1_w': _L3_gnn_in['fc1_w'], 'L3_gnn_fc1_b': _L3_gnn_in['fc1_b'], 'L3_gnn_fc2_w': _L3_gnn_in['fc2_w'], 'L3_gnn_fc2_b': _L3_gnn_in['fc2_b']}

def reference(x, src, dst, edge_attr_8, edge_type_16, edge_weight, L0_gnn_W, L0_gnn_b, L1_gnn_Wq, L1_gnn_Wk, L1_gnn_Wv, L1_gnn_Wo, L2_gnn_relvectors, L2_gnn_w_ih, L2_gnn_w_hh, L2_gnn_b_ih, L2_gnn_b_hh, L3_gnn_W1, L3_gnn_b1, L3_gnn_W2, L3_gnn_b2, L3_gnn_fc1_w, L3_gnn_fc1_b, L3_gnn_fc2_w, L3_gnn_fc2_b):
    import jax
    import jax.numpy as jnp

    def _L0_gnn_ref(X, edge_row, edge_col, edge_val, W, b):
        import jax, jax.numpy as jnp
        import numpy as np
        N_NODES = 3125
        N_EDGES = 100000
        D_IN = 256
        D_OUT = 256
        msgs = edge_val[:, None] * X[edge_col]
        h = jax.ops.segment_sum(msgs, edge_row, num_segments=N_NODES)
        return h @ W.T + b

    def _L1_gnn_ref(nfeat, attn_bias, Wq, Wk, Wv, Wo, src, dst):
        import jax, jax.numpy as jnp
        import numpy as np
        N = 3125
        E = 25000
        FEAT = 256
        HEADS = 8
        HEAD_DIM = FEAT // HEADS
        SCALING = HEAD_DIM ** (-0.5)
        n = nfeat.shape[0]
        q = (nfeat @ Wq.T).reshape(n, HEADS, HEAD_DIM) / SCALING
        k = (nfeat @ Wk.T).reshape(n, HEADS, HEAD_DIM)
        v = (nfeat @ Wv.T).reshape(n, HEADS, HEAD_DIM)
        attn = jnp.einsum('ehd,ehd->eh', k[src], q[dst])
        attn = attn + attn_bias
        m = jax.ops.segment_max(attn, dst, num_segments=n)
        a = jnp.exp(attn - m[dst])
        s = jax.ops.segment_sum(a, dst, num_segments=n)
        a = a / s[dst]
        out = jax.ops.segment_sum(v[src] * a[:, :, None], dst, num_segments=n)
        return out.reshape(n, FEAT) @ Wo.T

    def _L2_gnn_ref(h, relvectors, w_ih, w_hh, b_ih, b_hh, edge_src, edge_dst, edge_rel):
        import jax, jax.numpy as jnp
        import numpy as np
        N_NODES = 50000
        N_EDGES = 25000
        HDIM = 256
        NUMRELS = 16

        def _gru_cell(x, h, w_ih, w_hh, b_ih, b_hh):
            gi = x @ w_ih.T + b_ih
            gh = h @ w_hh.T + b_hh
            i_r, i_z, i_n = jnp.split(gi, 3, axis=-1)
            h_r, h_z, h_n = jnp.split(gh, 3, axis=-1)
            r = jax.nn.sigmoid(i_r + h_r)
            z = jax.nn.sigmoid(i_z + h_z)
            n = jnp.tanh(i_n + r * h_n)
            return (1.0 - z) * n + z * h
        msg = h[edge_src] + relvectors[edge_rel]
        red = jax.ops.segment_sum(msg, edge_dst, num_segments=h.shape[0])
        return _gru_cell(red, h, w_ih, w_hh, b_ih, b_hh)

    def _L3_gnn_ref(x, edge_index, W1, b1, W2, b2, fc1_w, fc1_b, fc2_w, fc2_b):
        import jax, jax.numpy as jnp
        import numpy as np
        N_NODES = 50000

        def gcn_conv(x, src, dst, W, b):
            N = x.shape[0]
            h = x @ W
            ones = jnp.ones(dst.shape, dtype=h.dtype)
            deg = jax.ops.segment_sum(ones, dst, num_segments=N) + 1.0
            dinv = jax.lax.rsqrt(deg)
            norm = dinv[src] * dinv[dst]
            agg = jax.ops.segment_sum(h[src] * norm[:, None], dst, num_segments=N)
            agg = agg + h * (dinv * dinv)[:, None]
            return agg + b
        src, dst = (edge_index[0], edge_index[1])
        h = jax.nn.relu(gcn_conv(x, src, dst, W1, b1))
        h = jax.nn.relu(gcn_conv(h, src, dst, W2, b2))
        h = h @ fc1_w + fc1_b
        h = h @ fc2_w + fc2_b
        return h
    edge_index = jnp.stack([src, dst])
    x = _layernorm(x + _L0_gnn_ref(x, src, dst, edge_weight, L0_gnn_W, L0_gnn_b), axis=-1)
    x = _layernorm(x + _L1_gnn_ref(x, edge_attr_8, L1_gnn_Wq, L1_gnn_Wk, L1_gnn_Wv, L1_gnn_Wo, src, dst), axis=-1)
    x = _layernorm(x + _L2_gnn_ref(x, L2_gnn_relvectors, L2_gnn_w_ih, L2_gnn_w_hh, L2_gnn_b_ih, L2_gnn_b_hh, src, dst, edge_type_16), axis=-1)
    x = _layernorm(x + _L3_gnn_ref(x, edge_index, L3_gnn_W1, L3_gnn_b1, L3_gnn_W2, L3_gnn_b2, L3_gnn_fc1_w, L3_gnn_fc1_b, L3_gnn_fc2_w, L3_gnn_fc2_b), axis=-1)
    return x

_drawn_inputs = setup_inputs


def setup_inputs(seed=0):
    import zlib

    import numpy as np

    out = dict(_drawn_inputs(seed))
    spreads = {'L0_gnn_b': (0.0, 0.1),
     'L3_gnn_b1': (0.0, 0.299),
     'L3_gnn_b2': (0.0, 0.1),
     'L3_gnn_fc1_b': (0.0, 0.1),
     'L3_gnn_fc2_b': (0.0, 0.1)}
    factors = {'L2_gnn_b_ih': 8.0, 'L2_gnn_b_hh': 8.0}
    for name, (base, spread) in spreads.items():
        noise = np.random.default_rng([zlib.crc32(name.encode()), seed]).standard_normal(out[name].shape)
        drawn = base * np.exp(spread * noise) if base else spread * noise
        out[name] = jnp.asarray(drawn.astype(out[name].dtype))
    for name, factor in factors.items():
        out[name] = (out[name] * factor).astype(out[name].dtype)
    return out
```

```python
from contextlib import ExitStack

import concourse.bass as bass
from concourse import mybir

F32 = mybir.dt.float32
I32 = mybir.dt.int32
ALU = mybir.AluOpType
ACT = mybir.ActivationFunctionType
AX = mybir.AxisListType

P = 128
EPS = 1e-5
BIG = float(2**100)
RECW = 13
R_SRC, R_DST, R_TYPE, R_W, R_POS, R_BIAS = 0, 1, 2, 3, 4, 5
U = 8
PR = 4
GRP = 16


class Link:

    def __init__(self, eng, sem, done=0, turn=None, per_turn=0):
        self.eng, self.sem, self.done, self.turn, self.per_turn, self.n = eng, sem, done, turn, per_turn, 0

    def __call__(self, ins):
        self.n += 1
        ins.then_inc(self.sem, 1)
        at = self.done + self.n
        self.eng.wait_ge(self.sem, at if self.turn is None else self.turn * self.per_turn + at)

    def end(self):
        assert self.turn is None or self.n == self.per_turn, (self.n, self.per_turn)


def gnn_kernel(nc, x, src, dst, edge_attr, edge_type, edge_weight, w0, b0, wq, wk, wv, wo, rel,
               w_ih, w_hh, b_ih, b_hh, w1, b1, w2, b2, fc1_w, fc1_b, fc2_w, fc2_b, out, debug=None):
    N, D = x.shape
    E, H = edge_attr.shape
    NREL = rel.shape[0]
    D1, D2, DF = w1.shape[1], w2.shape[1], fc1_w.shape[1]
    DH = D // H
    NB = -(-N // P)
    NLAST = N - (NB - 1) * P
    EC = E // P
    EREST = E - EC * P
    T = -(-(-(-E // P) + NB - 1) // GRP) * GRP
    TURNS = T // U
    SCALE = float(DH) ** 0.5
    assert D == 256 and H * GRP == P and EREST < P

    tab_rec = nc.dram_tensor("tab_rec", (E + P, RECW), I32, kind="Internal").ap()
    MW = D + 1
    tab_m = nc.dram_tensor("tab_m", (E + P, MW), F32, kind="Internal").ap()
    tab_k = nc.dram_tensor("tab_k", (NB * P, D), F32, kind="Internal").ap()
    tab_v = nc.dram_tensor("tab_v", (NB * P, D), F32, kind="Internal").ap()
    tab_x = nc.dram_tensor("tab_x", (NB * P, D), F32, kind="Internal").ap()
    tab_h1 = nc.dram_tensor("tab_h1", (NB * P, D1), F32, kind="Internal").ap()
    tab_h2 = nc.dram_tensor("tab_h2", (NB * P, D2), F32, kind="Internal").ap()

    with ExitStack() as ctx:
        def sb(name, shape, dt=F32):
            return ctx.enter_context(nc.sbuf_tensor(name, shape, dt))

        def sem(name):
            return ctx.enter_context(nc.semaphore(name))

        X = sb("X", [P, NB * D])
        ACCW = 272
        acc = sb("acc", [P, NB * ACCW])
        Q = sb("Q", [P, NB * D])
        S = sb("S", [P, T * H])
        rec = sb("rec", [P, T * RECW], I32)
        recf = rec[:, :].bitcast(F32)
        rec3 = rec[:, :].rearrange("p (t c) -> p t c", c=RECW)
        recf3 = recf.rearrange("p (t c) -> p t c", c=RECW)
        NWT = 10 + 2 * (3 * D // P)
        WT = sb("WT", [P, 2, NWT * P])
        W1 = sb("W1", [P, 2, D1])
        W2 = sb("W2", [P, D2])
        FC1 = sb("FC1", [D2, DF])
        FC2 = sb("FC2", [P, D])
        REL = sb("REL", [NREL, D])
        BO = {}
        o = 0
        for n, w in (("b0", D), ("ih", 3 * D), ("hh", 3 * D), ("fc1", DF), ("fc2", D), ("b1", D1), ("b2", D2)):
            BO[n] = o
            o += w
        brow = sb("brow", [1, o])
        b12 = sb("b12", [P, D1 + D2])
        wnat = Q[:, 0:NWT * D].rearrange("p (r n) -> p r n", n=D)
        G = sb("G", [P, U, D + 4])
        oh = sb("oh", [P, PR, P])
        ohT = sb("ohT", [P, 2, P])
        tyf = sb("tyf", [P, PR, NREL])
        work = sb("work", [P, 2, 264])
        idx = sb("idx", [P, U], I32)
        prod = sb("prod", [P, 2, D])
        small_t = sb("small_t", [P, T])
        sg_row = sb("sg_row", [1, T])
        epsb = sb("epsb", [P, 1])
        ident = sb("ident", [P, P])
        ones = sb("ones", [P, P])
        iota_i = sb("iota_i", [P, 512], I32)
        iota_f = sb("iota_f", [P, 512])
        dstl = sb("dstl", [P, T])
        bs_row = [sb(f"bs_row{k}", [1, T], I32) for k in range(2)]
        as_row = [sb(f"as_row{k}", [1, T], I32) for k in range(2)]
        offs = sb("offs", [P, T])
        cnt = sb("cnt", [P, NB])
        cntn = [sb(f"cntn{k}", [P, NB]) for k in range(2)]
        place = sb("place", [P, NB])
        triP = sb("triP", [P, P])
        small = sb("small", [P, 16])
        smalli = sb("smalli", [P, 4], I32)
        tri = sb("tri", [NB, NB])
        past = sb("past", [NB, T])
        mx = sb("mx", [P, NB * H])
        dinv = sb("dinv", [P, NB])
        A = sb("A", [P, D])
        AT = sb("AT", [P, 2, P])
        XS = sb("XS", [P, D])
        XT = sb("XT", [P, 2, P])
        Y = sb("Y", [P, D])
        KV = sb("KV", [P, 2 * D])
        gru = sb("gru", [P, 3 * D])
        stats = sb("stats", [P, 8])
        mv = sb("mv", [P, 4])
        sg = sb("sg", [P, P])
        dg = sb("dg", [P, P])
        sT = sb("sT", [P, P])
        dT = sb("dT", [P, P + 2])
        fl = sb("fl", [P, P])
        la = sb("la", [P, P])
        ms = sb("ms", [P, P])
        mrow = sb("mrow", [P, GRP, H + 1])
        padr = sb("padr", [P, RECW], I32)
        rest = acc[:, (EC + 1) * RECW:]
        recs = acc[:, 0:(EC + 1) * RECW].bitcast(I32).rearrange("p (t c) -> p t c", c=RECW)
        recsf = acc[:, 0:(EC + 1) * RECW].rearrange("p (t c) -> p t c", c=RECW)
        in_src = S[:, 0:EC + 1].bitcast(I32)
        in_dst = S[:, EC + 1:2 * (EC + 1)].bitcast(I32)
        in_typ = S[:, 2 * (EC + 1):3 * (EC + 1)].bitcast(I32)
        in_w = S[:, 3 * (EC + 1):4 * (EC + 1)]
        in_att = rec[:, 0:(EC + 1) * H].bitcast(F32)
        junk = S[:, 4 * (EC + 1):5 * (EC + 1)]
        tile_of = S[:, 5 * (EC + 1):6 * (EC + 1)]
        pos = S[:, 6 * (EC + 1):7 * (EC + 1)]
        run_to = rest[:, 0:EC + 1]
        in_it = rest[:, EC + 1:2 * (EC + 1)].bitcast(I32)
        ones_t = rest[:, 2 * (EC + 1):3 * (EC + 1)]

        PS = [ctx.enter_context(nc.psum_tensor(f"PS{i}", [P, 512], F32)) for i in range(8)]

        block_sems = {}

        def s_(name):
            if name not in block_sems:
                block_sems[name] = sem(name)
            return block_sems[name]

        ld_w, ld_x, ld_e = s_("ld_w"), s_("ld_x"), s_("ld_e")
        blank, consts = s_("blank"), s_("consts")
        wt_t, wt_c = s_("wt_t"), s_("wt_c")
        recs_done, rec_out, rec_in = s_("recs_done"), s_("rec_out"), s_("rec_in")
        v_set, pe_set = s_("v_set"), s_("pe_set")
        tabs = s_("tabs")
        N_W = 5 * 1 + 2 + 5 + 7
        passed = sem("passed")
        block = ctx.enter_context(nc.Block())

        def rows(ap, n):
            return ap.rearrange("(a n) -> a n", a=1)

        class Pass:

            def __init__(self, name, table, width, weighted=False):
                self.name, self.table, self.w, self.weighted = name, table, width, weighted
                self.idx = sem(name + "_idx")
                self.rows = ROWS
                self.used = sem(name + "_used")
                self.oh = sem(name + "_oh") if name not in ("keys", "vals") else None
                self.added = sem(name + "_added")

        NORMS = ["n1", "n2", "n3", "n5"]
        ROWS = [sem(f"rows{u}") for u in range(U)]
        pm = Pass("send", tab_m, MW)
        p0 = Pass("take", tab_m, D)
        pk = Pass("keys", tab_k, D)
        pv = Pass("vals", tab_v, D)
        p2 = Pass("msgs", tab_x, D)
        pc1 = Pass("gcn1", tab_h1, D1)
        pc2 = Pass("gcn2", tab_h2, D2)
        ORDER = [pm, pk, pv, p2, pc1, pc2]
        for n, p in enumerate(ORDER):
            p.base = 16 * TURNS * n
        p0.rows, p0.base = [sem(f"taken{u}") for u in range(U)], 0

        def settle(eng):
            eng.sem_inc(passed, 1)

        @block.gpsimd
        def _(pool):
            pool.memset(ident[:, :], 0.0).then_inc(blank, 1)
            pool.memset(tri[:, :], 1.0).then_inc(blank, 1)
            pool.memset(triP[:, :], 1.0).then_inc(blank, 1)
            pool.memset(ones[:, :], 1.0).then_inc(consts, 1)
            pool.iota(iota_i[:, :], [[1, 512]], base=0, channel_multiplier=0).then_inc(blank, 1)
            pool.wait_ge(blank, 4)
            pool.affine_select(out=ident[:, :], in_=ident[:, :], compare_op=ALU.not_equal, fill=1.0, base=0,
                               pattern=[[-1, P]], channel_multiplier=1).then_inc(consts, 1)
            pool.affine_select(out=tri[:, :], in_=tri[:, :], compare_op=ALU.is_ge, fill=0.0, base=0,
                               pattern=[[1, NB]], channel_multiplier=-1).then_inc(consts, 1)
            pool.tensor_copy(iota_f[:, :], iota_i[:, :]).then_inc(consts, 1)

            pool.wait_ge(blank, 4)
            pool.affine_select(out=triP[:, :], in_=triP[:, :], compare_op=ALU.is_gt, fill=0.0, base=0,
                               pattern=[[1, P]], channel_multiplier=-1).then_inc(consts, 1)

            with pool.Fori(0, TURNS) as i:
                for u in range(U):
                    if u % (U // 2) == 0:
                        pool.wait_ge(pm.idx, i * 2 + (u // (U // 2) + 1))
                    pool.wait_ge(pm.oh, i * U + (u + 1))
                    settle(pool)
                    pool.indirect_dma_start(tab_m[0:E, :], bass.IndirectOffsetOnAxis(ap=idx[:, u:u + 1], axis=0),
                                            G[:, u, :MW], None, bounds_check=E - 1, oob_is_err=False
                                            ).then_inc(pm.rows[u], 16)

            def gathers(p, ready, count):
                pool.wait_ge(ready, count)
                with pool.Fori(0, TURNS) as i:
                    for u in range(U):
                        if u % (U // 2) == 0:
                            pool.wait_ge(p.idx, i * 2 + (u // (U // 2) + 1))
                        pool.wait_ge(p.used, i * U + (u + 1))
                        settle(pool)
                        pool.indirect_dma_start(G[:, u, :p.w], None, p.table,
                                                bass.IndirectOffsetOnAxis(ap=idx[:, u:u + 1], axis=0)
                                                ).then_inc(p.rows[u], 16)

            gathers(pk, tabs, 16 * 2 * NB)
            gathers(pv, tabs, 16 * 2 * NB)
            gathers(p2, tabs, 16 * 3 * NB)
            gathers(pc1, tabs, 16 * 4 * NB)
            gathers(pc2, tabs, 16 * 5 * NB)

        @block.sync
        def _(sp):
            sp.wait_ge(v_set, 1)
            nx = (NB - 1) * P
            sp.dma_start(X[:, 0:(NB - 1) * D].rearrange("p (b n) -> p b n", n=D),
                         x[0:nx, :].rearrange("(b p) n -> p b n", p=P)).then_inc(ld_x, 16)
            sp.dma_start(X[0:NLAST, (NB - 1) * D:NB * D], x[nx:N, :]).then_inc(ld_x, 16)
            for to, of in ((in_dst, dst), (in_src, src), (in_typ, edge_type), (in_w, edge_weight)):
                sp.dma_start(to[:, 0:EC], of[0:EC * P].rearrange("(p t) -> p t", t=EC)).then_inc(ld_e, 16)
                sp.dma_start(to[0:EREST, EC:EC + 1],
                             of[EC * P:E].rearrange("(p t) -> p t", t=1)).then_inc(ld_e, 16)
            sp.dma_start(in_att[:, 0:EC * H], edge_attr[0:EC * P, :].rearrange("(p t) h -> p (t h)", t=EC)
                         ).then_inc(ld_e, 16)
            sp.dma_start(in_att[0:EREST, EC * H:(EC + 1) * H], edge_attr[EC * P:E, :]).then_inc(ld_e, 16)
            sp.wait_ge(recs_done, 2)
            sp.dma_start(tab_rec[0:EC * P, :].rearrange("(p t) c -> p t c", t=EC), recs[:, 0:EC, :]
                         ).then_inc(rec_out, 16)
            sp.dma_start(tab_rec[EC * P:E, :], recs[0:EREST, EC, :]).then_inc(rec_out, 16)
            sp.dma_start(tab_rec[E:E + P, :], padr[:, :]).then_inc(rec_out, 16)
            sp.wait_ge(s_("pad_m"), 1)
            sp.dma_start(tab_m[E:E + P, :], G[:, 0, 0:MW]).then_inc(rec_out, 16)
            sp.wait_ge(rec_out, 64)
            sp.wait_ge(v_set, 3)
            with sp.Fori(0, T) as t:
                first = sp.value_load(as_row[0][0:1, bass.ds(t, 1)], min_val=0, max_val=E)
                sp.dma_start(rec[:, bass.ds(t * RECW, RECW)], tab_rec[bass.ds(first, P), :]).then_inc(rec_in, 16)
            sp.sem_inc(pm.used, U)
            with sp.Fori(0, TURNS) as i:
                for u in range(U):
                    sp.wait_ge(pm.rows[u], i * 16 + 16)
                    sp.sem_inc(pm.used, 1)
            with sp.Fori(0, TURNS) as i:
                for u in range(U):
                    first = sp.value_load(as_row[1][0:1, bass.ds(i * U + u, 1)], min_val=0, max_val=E)
                    sp.wait_ge(p0.used, i * U + (u + 1))
                    sp.dma_start(G[:, u, 0:MW], tab_m[bass.ds(first, P), :]).then_inc(p0.rows[u], 16)

            def store(ready, table, of):
                with sp.Fori(0, NB) as b:
                    sp.wait_ge(ready, b + 1)
                    for tb, o in zip(table, of):
                        sp.dma_start(tb[bass.ds(b * P, P), :], o).then_inc(tabs, 16)

            store(s_("n1_kv"), (tab_k, tab_v), (KV[:, 0:D], KV[:, D:2 * D]))
            store(s_("n2_x"), (tab_x,), (XS[:, :],))
            store(s_("n3_h"), (tab_h1,), (KV[:, 0:D1],))
            store(s_("n4_h"), (tab_h2,), (KV[:, 0:D2],))
            sp.wait_ge(s_("n5_done"), 1)
            sp.dma_start(out[0:nx, :].rearrange("(b p) n -> p b n", p=P),
                         X[:, 0:(NB - 1) * D].rearrange("p (b n) -> p b n", n=D)).then_inc(s_("out"), 16)
            sp.dma_start(out[nx:N, :], X[0:NLAST, (NB - 1) * D:NB * D]).then_inc(s_("out"), 16)
            sp.wait_ge(s_("out"), 32)

        WMATS = [(w0, D), (wq, D), (wk, D), (wv, D), (wo, D), (w_ih, 3 * D), (w_hh, 3 * D)]
        WCOL = {}
        o = 0
        for n, (_, r) in zip(("w0", "wq", "wk", "wv", "wo", "ih", "hh"), WMATS):
            WCOL[n] = o
            o += r

        @block.scalar
        def _(act):
            r = 0
            for w, n in WMATS:
                act.dma_start(wnat[:, r:r + n // P, :], w.rearrange("(r p) n -> p r n", p=P)).then_inc(ld_w, 16)
                r += n // P
            act.dma_start(W1[:, :, :], w1.rearrange("(c p) n -> p c n", p=P)).then_inc(ld_w, 16)
            act.dma_start(W2[:, :], w2).then_inc(ld_w, 16)
            act.dma_start(FC1[:, :], fc1_w).then_inc(ld_w, 16)
            act.dma_start(FC2[:, :], fc2_w).then_inc(ld_w, 16)
            act.dma_start(REL[:, :], rel).then_inc(ld_w, 16)
            for n, b in (("b0", b0), ("ih", b_ih), ("hh", b_hh), ("fc1", fc1_b), ("fc2", fc2_b), ("b1", b1), ("b2", b2)):
                act.dma_start(brow[:, BO[n]:BO[n] + b.shape[0]], rows(b, b.shape[0])).then_inc(ld_w, 16)
            for r in range(NWT):
                act.wait_ge(wt_t, r + 1)
                act.copy(WT[:, :, r * P:(r + 1) * P],
                         PS[r % 4][:, 0:2 * P].rearrange("p (c n) -> p c n", c=2)).then_inc(wt_c, 1)
            act.wait_ge(wt_t, NWT + 1)
            act.copy(b12[:, :], PS[4][:, 0:D1 + D2]).then_inc(wt_c, 1)

            def window(p, i, h, field=R_SRC):
                n = U // 2
                act.wait_ge(p.used, i * U + (n * h + n))
                act.copy(idx[:, n * h:n * h + n],
                         rec[:, bass.ds(i * (U * RECW) + n * h * RECW, n * RECW)]
                         .rearrange("p (t c) -> p t c", c=RECW)[:, :, field]).then_inc(p.idx, 1)

            def windows(p):
                with act.Fori(0, TURNS) as i:
                    window(p, i, 0)
                    window(p, i, 1)

            def norm_std(l, name, b):
                act.wait_ge(s_("var"), b + (NORMS.index(name) * NB + 1))
                act.activation(mv[:, 2:3], mv[:, 1:2], ACT.Sqrt, bias=epsb[:, 0:1]).then_inc(s_("std"), 1)

            def turned(p, i, u, first):
                act.wait_ge(s_(p.name + "_ohT"), i * U + (u + 1))
                act.wait_ge(s_(p.name + "_sel"), i * U + (u + 1))
                act.copy(ohT[:, u % 2, :], PS[u % 2][:, 0:P]).then_inc(s_(p.name + "_ohTc"), 1)

            act.wait_ge(s_("places"), 1)
            with act.Fori(0, TURNS) as i:
                window(pm, i, 0, R_POS)
                window(pm, i, 1, R_POS)
                for u in range(U):
                    turned(pm, i, u, None)
            with act.Fori(0, NB) as b:
                act.wait_ge(s_("n1_free"), b + 1)
                act.copy(A[:, :], acc[:, bass.ds(b * ACCW, D)]).then_inc(s_("n1_a"), 1)
                act.wait_ge(s_("n1_aT"), b + 1)
                act.copy(AT[:, :, :], PS[0][:, 0:D].rearrange("p (c n) -> p c n", c=2)).then_inc(s_("n1_aTc"), 1)
                norm_std(None, "n1", b)
                act.wait_ge(s_("n1_xT"), b + 1)
                act.copy(XT[:, :, :], PS[2][:, 0:D].rearrange("p (c n) -> p c n", c=2)).then_inc(s_("n1_xTc"), 1)
                act.wait_ge(s_("n1_qkv"), b + 1)
                act.mul(Q[:, bass.ds(b * D, D)], PS[3][:, 0:D], SCALE).then_inc(s_("n1_q"), 1)
                act.copy(KV[:, :], PS[4][:, 0:2 * D]).then_inc(s_("n1_kv"), 1)
                act.wait_ge(tabs, b * 32 + 32)

            with act.Fori(0, TURNS) as i:
                window(pk, i, 0)
                window(pk, i, 1)
                for u in range(U):
                    turned(pk, i, u, None)
            with act.Fori(0, T // GRP) as g:
                act.wait_ge(s_("m_sg"), g + 1)
                act.copy(S[:, bass.ds(g * P, P)], sg[:, :]).then_inc(s_("m_s"), 1)
                act.wait_ge(s_("m_T"), g * 2 + 1)
                act.copy(sT[:, :], PS[0][:, 0:P]).then_inc(s_("m_Tc"), 1)
                act.copy(dT[:, 1:P + 1], PS[1][:, 0:P]).then_inc(s_("m_Tc"), 1)
                act.wait_ge(s_("m_T"), g * 2 + 2)
                act.copy(mrow[:, :, 0:H], PS[2][:, 0:P].rearrange("p (t h) -> p t h", h=H)).then_inc(s_("m_row"), 1)
                act.copy(mrow[:, :, H:H + 1], PS[3][:, 0:P].rearrange("p (t h) -> p t h", h=H)[:, :, 0:1]
                         ).then_inc(s_("m_row"), 1)
            with act.Fori(0, TURNS) as i:
                window(pv, i, 0)
                window(pv, i, 1)
                for u in range(U):
                    turned(pv, i, u, None)
                    act.wait_ge(s_("vals_d"), i * U + (u + 1))
                    act.activation(work[:, u % 2, D:D + H], work[:, u % 2, D:D + H], ACT.Exp
                                   ).then_inc(s_("vals_e"), 1)
            with act.Fori(0, NB) as b:
                act.wait_ge(s_("n2_aT"), b + 1)
                act.copy(AT[:, :, :], PS[0][:, 0:D].rearrange("p (c n) -> p c n", c=2)).then_inc(s_("n2_aTc"), 1)
                norm_std(None, "n2", b)
            windows(p2)
            act.wait_ge(s_("n3_deg"), 1)
            act.activation(dinv[:, :], dinv[:, :], ACT.Sqrt).then_inc(s_("n3_degs"), 1)
            with act.Fori(0, NB) as b:
                act.wait_ge(s_("n3_cT"), b + 1)
                act.copy(AT[0:NREL, 0, :], PS[0][0:NREL, 0:P]).then_inc(s_("n3_cTc"), 1)
                act.wait_ge(s_("n3_aT"), b + 1)
                act.copy(AT[:, :, :], PS[0][:, 0:D].rearrange("p (c n) -> p c n", c=2)).then_inc(s_("n3_aTc"), 1)
                act.copy(XT[:, :, :], PS[2][:, 0:D].rearrange("p (c n) -> p c n", c=2)).then_inc(s_("n3_aTc"), 1)
                act.wait_ge(s_("n3_g"), b + 1)
                act.activation(gru[:, 0:2 * D], PS[3][:, 0:2 * D], ACT.Sigmoid).then_inc(s_("n3_rz"), 1)
                act.wait_ge(s_("n3_t"), b + 1)
                act.activation(gru[:, 2 * D:3 * D], A[:, :], ACT.Tanh).then_inc(s_("n3_n"), 1)
                norm_std(None, "n3", b)
                act.wait_ge(s_("n3_xT"), b + 1)
                act.copy(XT[:, :, :], PS[2][:, 0:D].rearrange("p (c n) -> p c n", c=2)).then_inc(s_("n3_xTc"), 1)
            windows(pc1)
            with act.Fori(0, NB) as b:
                act.wait_ge(s_("n4_aT"), b + 1)
                act.copy(AT[:, 0, :], PS[0][:, 0:P]).then_inc(s_("n4_aTc"), 1)
            windows(pc2)
            with act.Fori(0, NB) as b:
                act.wait_ge(s_("n5_aT"), b + 1)
                act.copy(AT[0:D2, 0, :], PS[0][0:D2, 0:P]).then_inc(s_("n5_aTc"), 1)
                act.wait_ge(s_("n5_f1"), b + 1)
                act.copy(KV[:, 0:DF], PS[1][:, 0:DF]).then_inc(s_("n5_f1c"), 1)
                act.wait_ge(s_("n5_fT"), b + 1)
                act.copy(XT[:, 0, :], PS[2][:, 0:P]).then_inc(s_("n5_fTc"), 1)
                norm_std(None, "n5", b)

        @block.tensor
        def _(pe):
            pe.wait_ge(consts, 5)
            pe.wait_ge(ld_w, 16 * 19)
            for r in range(NWT):
                if r >= 4:
                    pe.wait_ge(wt_c, r - 3)
                pe.transpose(PS[r % 4][:, 0:P], wnat[:, r, 0:P], ident[:, :])
                pe.transpose(PS[r % 4][:, P:2 * P], wnat[:, r, P:2 * P], ident[:, :]).then_inc(wt_t, 1)
            pe.matmul(PS[4][:, 0:D1 + D2], ones[0:1, :], brow[:, BO["b1"]:BO["b1"] + D1 + D2],
                      start=True, stop=True).then_inc(wt_t, 1)
            for k in range(2):
                pe.wait_ge(s_("v_cnt"), k + 1)
                pe.matmul(PS[5][0:NB, 0:1], cntn[k][:, :], ones[:, 0:1], start=True, stop=True).then_inc(pe_set, 1)
                pe.wait_ge(s_("v_nt"), 2 * k + 1)
                pe.matmul(PS[5][0:NB, 8:9], tri[:, :], small[0:NB, 1:2], start=True, stop=True).then_inc(pe_set, 1)
                pe.wait_ge(s_("v_nt"), 2 * k + 2)
                pe.wait_ge(wt_c, NWT + 1)
                pe.matmul(PS[6][0:1, 0:T], ones[0:NB, 0:1], past[:, :], start=True, stop=True)
                pe.matmul(PS[7][0:1, 0:T], small[0:NB, 2:3], past[:, :], start=True, stop=True)
                pe.matmul(PS[4][:, 0:T], ones[0:NB, :], past[:, :], start=True, stop=True).then_inc(pe_set, 1)
            pe.wait_ge(v_set, 3)
            pe.matmul(PS[4][:, 0:NB], triP[:, :], cntn[1][:, :], start=True, stop=True)
            pe.matmul(PS[5][:, 0:NB], ones[:, :], cntn[1][:, :], start=True, stop=True).then_inc(pe_set, 1)

            def bias(ps, name, n, off=0):
                pe.matmul(ps, ones[0:1, :], brow[:, BO[name] + off:BO[name] + off + n], start=True, stop=False)

            def times(ps, aT, name, off, n, start, stop=True):
                c0 = WCOL[name] + off
                for c in range(2):
                    last = pe.matmul(ps, aT[:, c, :], WT[:, c, c0:c0 + n],
                                     start=(start and c == 0), stop=(stop and c == 1))
                return last

            def turn2(ps, a):
                pe.transpose(ps[:, 0:P], a[:, 0:P], ident[:, :])
                return pe.transpose(ps[:, P:2 * P], a[:, P:2 * P], ident[:, :])

            def sums(p, types=False):
                pe.sem_inc(p.used, U)
                with pe.Fori(0, TURNS) as i:
                    for u in range(U):
                        pe.wait_ge(p.oh, i * U + (u + 1))
                        pe.wait_ge(p.rows[u], i * 16 + (p.base + 16))
                        pe.wait_ge(p.added, i * U + (u + 1))
                        last = pe.matmul(PS[4 + u % PR][:, 0:p.w], oh[:, u % PR, :], G[:, u, :p.w],
                                         start=True, stop=True)
                        if types:
                            last = pe.matmul(PS[4 + u % PR][:, D:D + NREL], oh[:, u % PR, :], tyf[:, u % PR, :],
                                             start=True, stop=True)
                        last.then_inc(p.used, 1)

            def chosen(p, i, u):
                pe.wait_ge(s_(p.name + "_1h"), i * U + (u + 1))
                pe.transpose(PS[u % 2][:, 0:P], oh[:, u % PR, :], ident[:, :]).then_inc(s_(p.name + "_ohT"), 1)
                pe.wait_ge(s_(p.name + "_ohTc"), i * U + (u + 1))

            pe.wait_ge(s_("places"), 1)
            pe.wait_ge(ld_x, 32)
            pe.sem_inc(s_("send_sel"), 2)
            with pe.Fori(0, TURNS) as i:
                for u in range(U):
                    tile = pe.value_load(bs_row[0][0:1, bass.ds(i * U + u, 1)], min_val=0, max_val=NB - 1)
                    chosen(pm, i, u)
                    pe.wait_ge(pm.added, i * U + (u + 1))
                    pe.matmul(PS[4 + u % PR][:, 0:D], ohT[:, u % 2, :], X[:, bass.ds(tile * D, D)],
                              start=True, stop=True).then_inc(s_("send_sel"), 1)
            sums(p0)
            with pe.Fori(0, NB) as b:
                pe.wait_ge(s_("n1_a"), b + 1)
                turn2(PS[0], A).then_inc(s_("n1_aT"), 1)
                pe.wait_ge(s_("n1_aTc"), b + 1)
                bias(PS[1][:, 0:D], "b0", D)
                times(PS[1][:, 0:D], AT, "w0", 0, D, False).then_inc(s_("n1_h"), 1)
                pe.wait_ge(s_("n1_ln"), b + 1)
                turn2(PS[2], XS).then_inc(s_("n1_xT"), 1)
                pe.wait_ge(s_("n1_xTc"), b + 1)
                times(PS[3][:, 0:D], XT, "wq", 0, D, True)
                times(PS[4][:, 0:D], XT, "wk", 0, D, True)
                times(PS[4][:, D:2 * D], XT, "wv", 0, D, True).then_inc(s_("n1_qkv"), 1)

            pe.wait_ge(s_("n1_kv"), NB)
            pe.sem_inc(s_("keys_sel"), 2)
            with pe.Fori(0, TURNS) as i:
                for u in range(U):
                    tile = pe.value_load(bs_row[0][0:1, bass.ds(i * U + u, 1)], min_val=0, max_val=NB - 1)
                    chosen(pk, i, u)
                    pe.wait_ge(pk.added, i * U + (u + 1))
                    pe.matmul(PS[4 + u % PR][:, 0:D], ohT[:, u % 2, :], Q[:, bass.ds(tile * D, D)],
                              start=True, stop=True).then_inc(s_("keys_sel"), 1)
            pe.sem_inc(s_("m_mm"), PR)
            with pe.Fori(0, T // GRP) as g:
                pe.wait_ge(s_("m_sg"), g + 1)
                pe.wait_ge(s_("m_dg"), g + 1)
                pe.transpose(PS[0][:, 0:P], sg[:, :], ident[:, :])
                pe.transpose(PS[1][:, 0:P], dg[:, :], ident[:, :]).then_inc(s_("m_T"), 1)
                pe.wait_ge(s_("m_ms"), g + 1)
                pe.transpose(PS[2][:, 0:P], ms[:, :], ident[:, :])
                pe.transpose(PS[3][:, 0:P], la[:, :], ident[:, :]).then_inc(s_("m_T"), 1)
                pe.wait_ge(s_("m_row"), g * 2 + 2)
                for u in range(GRP):
                    pe.wait_ge(s_("m_oh"), g * GRP + (u + 1))
                    pe.wait_ge(s_("m_added"), g * GRP + (u + 1))
                    pe.matmul(PS[4 + u % PR][:, 0:H + 1], oh[:, u % PR, :], mrow[:, u, :],
                              start=True, stop=True).then_inc(s_("m_mm"), 1)
            pe.sem_inc(s_("vals_sel"), 2)
            pe.sem_inc(pv.used, U)
            with pe.Fori(0, TURNS) as i:
                for u in range(U):
                    tile = pe.value_load(bs_row[0][0:1, bass.ds(i * U + u, 1)], min_val=0, max_val=NB - 1)
                    chosen(pv, i, u)
                    pe.matmul(PS[2 + u % 2][:, 0:H], ohT[:, u % 2, :], mx[:, bass.ds(tile * H, H)],
                              start=True, stop=True).then_inc(s_("vals_sel"), 1)
                    pe.wait_ge(s_("vals_vp"), i * U + (u + 1))
                    pe.wait_ge(pv.added, i * U + (u + 1))
                    pe.matmul(PS[4 + u % PR][:, 0:D + H], oh[:, u % PR, :], work[:, u % 2, :],
                              start=True, stop=True).then_inc(pv.used, 1)
            with pe.Fori(0, NB) as b:
                pe.wait_ge(s_("n2_a"), b + 1)
                turn2(PS[0], A).then_inc(s_("n2_aT"), 1)
                pe.wait_ge(s_("n2_aTc"), b + 1)
                times(PS[1][:, 0:D], AT, "wo", 0, D, True).then_inc(s_("n2_h"), 1)
            sums(p2, types=True)
            with pe.Fori(0, NB) as b:
                pe.wait_ge(s_("n3_c"), b + 1)
                pe.transpose(PS[0][0:NREL, 0:P], Y[:, 0:NREL], ident[:, :]).then_inc(s_("n3_cT"), 1)
                pe.wait_ge(s_("n3_cTc"), b + 1)
                pe.matmul(PS[1][:, 0:D], AT[0:NREL, 0, :], REL[:, :], start=True, stop=True).then_inc(s_("n3_r"), 1)
                pe.wait_ge(s_("n3_a"), b + 1)
                turn2(PS[0], A)
                turn2(PS[2], XS).then_inc(s_("n3_aT"), 1)
                pe.wait_ge(s_("n3_aTc"), b * 2 + 2)
                bias(PS[3][:, 0:2 * D], "ih", 2 * D)
                pe.matmul(PS[3][:, 0:2 * D], ones[0:1, :], brow[:, BO["hh"]:BO["hh"] + 2 * D], start=False, stop=False)
                times(PS[3][:, 0:2 * D], AT, "ih", 0, 2 * D, False, stop=False)
                times(PS[3][:, 0:2 * D], XT, "hh", 0, 2 * D, False)
                bias(PS[4][:, 0:D], "ih", D, 2 * D)
                times(PS[4][:, 0:D], AT, "ih", 2 * D, D, False)
                bias(PS[5][:, 0:D], "hh", D, 2 * D)
                times(PS[5][:, 0:D], XT, "hh", 2 * D, D, False).then_inc(s_("n3_g"), 1)
                pe.wait_ge(s_("n3_ln"), b + 1)
                turn2(PS[2], XS).then_inc(s_("n3_xT"), 1)
                pe.wait_ge(s_("n3_xTc"), b + 1)
                for c in range(2):
                    last = pe.matmul(PS[1][:, 0:D1], XT[:, c, :], W1[:, c, :], start=(c == 0), stop=(c == 1))
                last.then_inc(s_("n3_h1"), 1)
            sums(pc1)
            with pe.Fori(0, NB) as b:
                pe.wait_ge(s_("n4_a"), b + 1)
                pe.transpose(PS[0][:, 0:P], A[:, 0:D1], ident[:, :]).then_inc(s_("n4_aT"), 1)
                pe.wait_ge(s_("n4_aTc"), b + 1)
                pe.matmul(PS[1][:, 0:D2], AT[:, 0, :], W2[:, :], start=True, stop=True).then_inc(s_("n4_h2"), 1)
            sums(pc2)
            with pe.Fori(0, NB) as b:
                pe.wait_ge(s_("n5_a"), b + 1)
                settle(pe)
                pe.transpose(PS[0][0:D2, 0:P], A[:, 0:D2], ident[:, :]).then_inc(s_("n5_aT"), 1)
                pe.wait_ge(s_("n5_aTc"), b + 1)
                bias(PS[1][:, 0:DF], "fc1", DF)
                pe.matmul(PS[1][:, 0:DF], AT[0:D2, 0, :], FC1[:, :], start=False, stop=True).then_inc(s_("n5_f1"), 1)
                pe.wait_ge(s_("n5_f1c"), b + 1)
                pe.transpose(PS[2][:, 0:P], KV[:, 0:DF], ident[:, :]).then_inc(s_("n5_fT"), 1)
                pe.wait_ge(s_("n5_fTc"), b + 1)
                bias(PS[3][:, 0:D], "fc2", D)
                pe.matmul(PS[3][:, 0:D], XT[:, 0, :], FC2[:, :], start=False, stop=True).then_inc(s_("n5_f2"), 1)

        @block.vector
        def _(dve):
            lk = s_("v_link")
            link = Link(dve, lk)
            NOEDGE = 1 << 20
            link(dve.memset(in_dst[:, EC:EC + 1], NOEDGE))
            link(dve.memset(in_src[:, EC:EC + 1], NOEDGE))
            link(dve.memset(in_typ[:, EC:EC + 1], 0))
            link(dve.memset(in_w[:, EC:EC + 1], 0.0))
            link(dve.memset(in_att[:, EC * H:(EC + 1) * H], 0.0))
            link(dve.memset(padr[:, :], 0))
            link(dve.memset(padr[:, R_DST:R_DST + 1].bitcast(F32), float(NOEDGE)))
            link(dve.memset(epsb[:, :], EPS))
            link(dve.memset(dT[:, :], -1.0))
            link(dve.memset(mx[:, :], -BIG))
            dve.memset(X[:, (NB - 1) * D:NB * D], 0.0).then_inc(v_set, 1)
            dve.wait_ge(ld_e, 160)
            link(dve.tensor_copy(recs[:, :, R_SRC], in_src))
            link(dve.tensor_copy(recsf[:, :, R_DST], in_dst))
            link(dve.tensor_copy(recsf[:, :, R_TYPE], in_typ))
            link(dve.tensor_copy(recsf[:, :, R_W], in_w))
            dve.tensor_copy(recsf[:, :, R_BIAS:], in_att.rearrange("p (t h) -> p t h", h=H)).then_inc(recs_done, 1)
            dve.wait_ge(recs_done, 1)
            for k, field in ((0, in_dst), (1, in_src)):
                link(dve.tensor_copy(in_it, field))
                link(dve.tensor_scalar(in_it, in_it, 7, None, ALU.arith_shift_right))
                link(dve.tensor_copy(tile_of, in_it))
                for b in range(NB):
                    link(dve.tensor_scalar(junk, tile_of, float(b), None, ALU.is_equal, ALU.add,
                                           accum_out=cntn[k][:, b:b + 1]))
                dve.sem_inc(s_("v_cnt"), 1)
            link(dve.memset(G[:, 0, :], float(NOEDGE)))
            dve.sem_inc(s_("pad_m"), 1)
            for k in range(2):
                dve.wait_ge(pe_set, 3 * k + 1)
                link(dve.tensor_scalar(smalli[0:NB, 0:1], PS[5][0:NB, 0:1], float(P - 1), None, ALU.add))
                link(dve.tensor_scalar(smalli[0:NB, 1:2], smalli[0:NB, 0:1], 7, None, ALU.arith_shift_right))
                link(dve.tensor_copy(small[0:NB, 1:2], smalli[0:NB, 1:2]))
                dve.scalar_tensor_tensor(small[0:NB, 2:3], small[0:NB, 1:2], float(-P), PS[5][0:NB, 0:1],
                                         ALU.mult, ALU.add).then_inc(s_("v_nt"), 1)
                dve.wait_ge(pe_set, 3 * k + 2)
                dve.wait_ge(consts, 5)
                link(dve.tensor_copy(small[0:NB, 3:4], PS[5][0:NB, 8:9]))
                dve.tensor_scalar(past[:, :], iota_f[0:NB, 0:T], small[0:NB, 3:4], None, ALU.is_ge
                                  ).then_inc(s_("v_nt"), 1)
                dve.wait_ge(pe_set, 3 * k + 3)
                link(dve.tensor_scalar(bs_row[k][:, :], PS[6][0:1, 0:T], float(NB - 1), None, ALU.min))
                link(dve.scalar_tensor_tensor(sg_row[:, :], iota_f[0:1, 0:T], float(P), PS[7][0:1, 0:T],
                                              ALU.mult, ALU.add))
                link(dve.tensor_scalar(as_row[k][:, :], sg_row[:, :], float(E), None, ALU.min))
                link(dve.tensor_scalar((dstl, offs)[k][:, :], PS[4][:, 0:T], float(NB - 1), -float(P),
                                       ALU.min, ALU.mult))
            dve.sem_inc(v_set, 2)
            dve.wait_ge(pe_set, 7)
            link(dve.tensor_copy(cnt[:, :], PS[5][:, 0:NB]))
            link(dve.tensor_tensor_scan(place[:, :], ones[:, 0:NB], cnt[:, :], -1.0, ALU.mult, ALU.add))
            link(dve.tensor_tensor(place[:, :], place[:, :], cnt[:, :], ALU.subtract))
            link(dve.tensor_tensor(place[:, :], place[:, :], PS[4][:, 0:NB], ALU.add))
            link(dve.memset(ones_t, 1.0))
            link(dve.memset(pos, 0.0))
            for b in range(NB):
                link(dve.tensor_scalar(junk, tile_of, float(b), None, ALU.is_equal))
                link(dve.tensor_tensor_scan(run_to, ones_t, junk, place[:, b:b + 1], ALU.mult, ALU.add))
                link(dve.tensor_tensor(run_to, run_to, junk, ALU.mult))
                link(dve.tensor_tensor(pos, pos, run_to, ALU.add))
            dve.tensor_copy(recs[:, :, R_POS], pos).then_inc(recs_done, 1)
            dve.wait_ge(rec_in, 16 * T)
            dve.wait_ge(v_set, 3)
            link(dve.tensor_tensor(dstl[:, :], dstl[:, :], recf3[:, :, R_DST], ALU.add))
            link(dve.memset(acc[:, :], 0.0))
            link(dve.tensor_scalar(small_t[:, :], dstl[:, :], 0.0, None, ALU.is_ge))
            link(dve.scalar_tensor_tensor(small_t[:, :], dstl[:, :], float(P), small_t[:, :], ALU.is_lt, ALU.mult))
            link(dve.tensor_tensor(recf3[:, :, R_BIAS:], recf3[:, :, R_BIAS:],
                                   small_t[:, :, None].to_broadcast([P, T, H]), ALU.mult))
            link(dve.tensor_scalar(small_t[:, :], small_t[:, :], -float(NOEDGE), float(NOEDGE), ALU.mult, ALU.add))
            link(dve.tensor_tensor(rec3[:, :, R_POS], rec3[:, :, R_POS], small_t[:, :], ALU.add))
            dve.sem_inc(s_("places"), 1)
            done = link.n

            def onehot(p, i, u, t, ready, used, used_at, weighted=False):
                dve.wait_ge(used, used_at)
                dve.tensor_scalar(oh[:, u % PR, :], iota_f[:, 0:P], dstl[:, bass.ds(t, 1)],
                                  recf[:, bass.ds(t * RECW + R_W, 1)] if weighted else None,
                                  ALU.is_equal, *([ALU.mult] if weighted else [])).then_inc(ready, 1)

            def add_up(p, i, u, w, k=0):
                tile = dve.value_load(bs_row[k][0:1, bass.ds(i * U + u, 1)], min_val=0, max_val=NB - 1)
                to = acc[:, bass.ds(tile * ACCW, w)]
                dve.wait_ge(p.used, i * U + (u + 1 + U))
                dve.wait_ge(p.added, i * U + (u + PR))
                dve.tensor_tensor(to, to, PS[4 + u % PR][:, 0:w], ALU.add).then_inc(p.added, 1)

            LAG = 2

            def sums(p, types=False):
                dve.sem_inc(p.added, PR)
                with dve.Fori(0, TURNS) as i:
                    for u in range(U + LAG):
                        if u < U:
                            if types:
                                dve.wait_ge(p.used, i * U + (u + 1 + U - PR))
                                dve.tensor_scalar(tyf[:, u % PR, :], iota_f[:, 0:NREL],
                                                  recf[:, bass.ds(i * (U * RECW) + (u * RECW + R_TYPE), 1)], None,
                                                  ALU.is_equal).then_inc(s_("types"), 1)
                                dve.wait_ge(s_("types"), i * U + (u + 1))
                            onehot(p, i, u, i * U + u, p.oh, p.used, i * U + (u + 1 + U - PR), p.weighted)
                        if u >= LAG:
                            add_up(p, i, u - LAG, p.w + (NREL if types else 0))

            def norm(name, b, lkn, to):
                lkn(dve.bn_stats(stats[:, 0:6], Y[:, :]))
                settle(dve)
                dve.bn_aggr(mv[:, 0:2], stats[:, 0:6]).then_inc(s_("var"), 1)
                dve.wait_ge(s_("std"), b + (NORMS.index(name) * NB + 1))
                lkn(dve.reciprocal(mv[:, 3:4], mv[:, 2:3]))
                return dve.tensor_scalar(to, Y[:, :], mv[:, 0:1], mv[:, 3:4], ALU.subtract, ALU.mult)

            dve.sem_inc(pm.added, PR)
            with dve.Fori(0, TURNS) as i:
                for u in range(U + LAG):
                    if u < U:
                        onehot(pm, i, u, i * U + u, s_("send_1h"), s_("send_sel"), i * U + (u + 1))
                    if u >= LAG:
                        v = u - LAG
                        dve.wait_ge(pm.used, i * U + (v + 1))
                        dve.wait_ge(s_("send_sel"), i * U + (v + 3))
                        dve.tensor_scalar(G[:, v, 0:D], PS[4 + v % PR][:, 0:D],
                                          recf[:, bass.ds(i * (U * RECW) + (v * RECW + R_W), 1)], None, ALU.mult
                                          ).then_inc(pm.added, 1)
                        dve.wait_ge(pm.added, i * U + (v + 1 + PR))
                        dve.tensor_scalar(G[:, v, D:MW], rec[:, bass.ds(i * (U * RECW) + (v * RECW + R_SRC), 1)],
                                          1.0, None, ALU.mult).then_inc(pm.oh, 1)
            dve.wait_ge(pm.oh, T)
            dve.sem_inc(p0.added, PR)
            with dve.Fori(0, TURNS) as i:
                for u in range(U + LAG):
                    if u < U:
                        dve.wait_ge(p0.rows[u], i * 16 + (p0.base + 16))
                        dve.wait_ge(p0.used, i * U + (u + 1 + U - PR))
                        dve.tensor_scalar(oh[:, u % PR, :], iota_f[:, 0:P], G[:, u, D:MW],
                                          offs[:, bass.ds(i * U + u, 1)], ALU.subtract, ALU.is_equal
                                          ).then_inc(p0.oh, 1)
                    if u >= LAG:
                        add_up(p0, i, u - LAG, D, 1)
            dve.wait_ge(ld_x, 32)
            dve.wait_ge(p0.added, T + PR)
            dve.sem_inc(s_("n1_free"), 1)
            k1 = s_("n1_link")
            with dve.Fori(0, NB) as b:
                ln = Link(dve, k1, 0, b, 5)
                dve.wait_ge(s_("n1_h"), b + 1)
                ln(dve.tensor_tensor(Y[:, :], X[:, bass.ds(b * D, D)], PS[1][:, 0:D], ALU.add))
                ln(norm("n1", b, ln, XS[:, :]))
                dve.sem_inc(s_("n1_ln"), 1)
                settle(dve)
                ln(dve.tensor_copy(X[:, bass.ds(b * D, D)], XS[:, :]))
                dve.wait_ge(s_("n1_qkv"), b + 1)
                dve.sem_inc(s_("n1_free"), 1)
                ln.end()
            link2 = Link(dve, lk, done)
            link2(dve.memset(acc[:, :], 0.0))
            dve.sem_inc(pk.added, PR)
            dve.sem_inc(pk.used, U)
            kk = s_("keys_link")
            with dve.Fori(0, TURNS) as i:
                for u in range(U + LAG):
                    if u < U:
                        onehot(pk, i, u, i * U + u, s_("keys_1h"), s_("keys_sel"), i * U + (u + 1 + 2 - 2))
                    if u >= LAG:
                        v = u - LAG
                        dve.wait_ge(s_("keys_sel"), i * U + (v + 3))
                        dve.wait_ge(pk.rows[v], i * 16 + (pk.base + 16))
                        dve.tensor_tensor(prod[:, v % 2, :], G[:, v, 0:D], PS[4 + v % PR][:, 0:D], ALU.mult
                                          ).then_inc(kk, 1)
                        dve.wait_ge(kk, i * (2 * U) + (2 * v + 1))
                        dve.tensor_reduce(S[:, bass.ds((i * U + v) * H, H)],
                                          prod[:, v % 2, :].rearrange("p (h d) -> p h d", h=H), AX.X, ALU.add
                                          ).then_inc(kk, 1)
                        dve.wait_ge(kk, i * (2 * U) + (2 * v + 2))
                        dve.sem_inc(pk.added, 1)
                        dve.sem_inc(pk.used, 1)
            dve.sem_inc(s_("m_added"), PR)
            km = s_("m_link")
            with dve.Fori(0, T // GRP) as g:
                ln = Link(dve, km, 0, g, 7)
                settle(dve)
                ln(dve.tensor_copy(dg[:, :].rearrange("p (t h) -> p t h", h=H),
                                   recf[:, bass.ds(g * (GRP * RECW), GRP * RECW)]
                                   .rearrange("p (t c) -> p t c", c=RECW)[:, :, R_DST:R_DST + 1]
                                   .to_broadcast([P, GRP, H])))
                dve.sem_inc(s_("m_dg"), 1)
                ln(dve.tensor_tensor(sg[:, :].rearrange("p (t h) -> p t h", h=H),
                                     S[:, bass.ds(g * P, P)].rearrange("p (t h) -> p t h", h=H),
                                     recf[:, bass.ds(g * (GRP * RECW), GRP * RECW)]
                                     .rearrange("p (t c) -> p t c", c=RECW)[:, :, R_BIAS:], ALU.add))
                dve.sem_inc(s_("m_sg"), 1)
                dve.wait_ge(s_("m_Tc"), g * 2 + 2)
                ln(dve.tensor_tensor(fl[:, :], dT[:, 1:P + 1], dT[:, 0:P], ALU.not_equal))
                ln(dve.tensor_scalar(fl[:, :], fl[:, :], -BIG, None, ALU.mult))
                ln(dve.tensor_tensor(la[:, :], dT[:, 1:P + 1], dT[:, 2:P + 2], ALU.not_equal))
                ln(dve.tensor_tensor_scan(ms[:, :], fl[:, :], sT[:, :], -BIG, ALU.add, ALU.max))
                ln(dve.tensor_tensor(ms[:, :], ms[:, :], la[:, :], ALU.mult))
                dve.sem_inc(s_("m_ms"), 1)
                ln.end()
                for u in range(GRP + LAG):
                    if u < GRP:
                        dve.wait_ge(s_("m_mm"), g * GRP + (u + 1))
                        dve.tensor_scalar(oh[:, u % PR, :], iota_f[:, 0:P], dstl[:, bass.ds(g * GRP + u, 1)], None,
                                          ALU.is_equal).then_inc(s_("m_oh"), 1)
                    if u >= LAG:
                        v = u - LAG
                        tile = dve.value_load(bs_row[0][0:1, bass.ds(g * GRP + v, 1)], min_val=0, max_val=NB - 1)
                        to = mx[:, bass.ds(tile * H, H)]
                        dve.wait_ge(s_("m_mm"), g * GRP + (v + 1 + PR))
                        dve.tensor_scalar(mv[:, 0:1], PS[4 + v % PR][:, H:H + 1], BIG, -BIG, ALU.mult, ALU.add
                                          ).then_inc(s_("m_off"), 1)
                        dve.wait_ge(s_("m_off"), g * GRP + (v + 1))
                        dve.scalar_tensor_tensor(to, PS[4 + v % PR][:, 0:H], mv[:, 0:1], to, ALU.add, ALU.max
                                                 ).then_inc(s_("m_added"), 1)
                        dve.wait_ge(s_("m_added"), g * GRP + (v + 1 + PR))
            dve.sem_inc(pv.added, PR)
            with dve.Fori(0, TURNS) as i:
                for u in range(U):
                    t = i * U + u
                    onehot(pv, i, u, t, s_("vals_1h"), pv.used, i * U + (u + 1 + U - PR))
                    dve.wait_ge(s_("vals_sel"), i * U + (u + 3))
                    dve.wait_ge(pv.used, i * U + (u + 1 + U - 2))
                    dve.tensor_tensor(work[:, u % 2, D:D + H], S[:, bass.ds(t * H, H)], PS[2 + u % 2][:, 0:H],
                                      ALU.subtract).then_inc(s_("vals_d"), 1)
                    dve.wait_ge(s_("vals_e"), i * U + (u + 1))
                    dve.wait_ge(pv.rows[u], i * 16 + (pv.base + 16))
                    dve.tensor_tensor(work[:, u % 2, 0:D].rearrange("p (h d) -> p h d", h=H),
                                      G[:, u, 0:D].rearrange("p (h d) -> p h d", h=H),
                                      work[:, u % 2, D:D + H, None].to_broadcast([P, H, DH]), ALU.mult
                                      ).then_inc(s_("vals_vp"), 1)
                    add_up(pv, i, u, D + H)
            dve.wait_ge(pv.added, T + PR)
            with dve.Fori(0, NB) as b:
                ln = Link(dve, s_("n2_link"), 0, b, 6)
                ln(dve.tensor_scalar(small[:, 0:H], acc[:, bass.ds(b * ACCW + D, H)], 1e-30, None, ALU.max))
                ln(dve.reciprocal(small[:, 8:8 + H], small[:, 0:H]))
                dve.tensor_tensor(A[:, :].rearrange("p (h d) -> p h d", h=H),
                                  acc[:, bass.ds(b * ACCW, D)].rearrange("p (h d) -> p h d", h=H),
                                  small[:, 8:8 + H, None].to_broadcast([P, H, DH]), ALU.mult
                                  ).then_inc(s_("n2_a"), 1)
                dve.wait_ge(s_("n2_h"), b + 1)
                ln(dve.tensor_tensor(Y[:, :], X[:, bass.ds(b * D, D)], PS[1][:, 0:D], ALU.add))
                dve.wait_ge(tabs, b * 16 + 16 * 2 * NB)
                norm("n2", b, ln, XS[:, :]).then_inc(s_("n2_x"), 1)
                dve.wait_ge(s_("n2_x"), b + 1)
                settle(dve)
                ln(dve.tensor_copy(X[:, bass.ds(b * D, D)], XS[:, :]))
                ln.end()
            link2(dve.memset(acc[:, :], 0.0))
            sums(p2, types=True)
            dve.wait_ge(p2.added, T + PR)
            acc3 = acc[:, :].rearrange("p (b w) -> p b w", w=ACCW)
            link2(dve.tensor_reduce(dinv[:, :], acc3[:, :, D:D + NREL], AX.X, ALU.add))
            dve.tensor_scalar(dinv[:, :], dinv[:, :], 1.0, None, ALU.add).then_inc(s_("n3_deg"), 1)
            dve.wait_ge(s_("n3_degs"), 1)
            link2(dve.reciprocal(dinv[:, :], dinv[:, :]))
            dve.wait_ge(tabs, 16 * 3 * NB)
            with dve.Fori(0, NB) as b:
                ln = Link(dve, s_("n3_link"), 0, b, 9)
                xb = X[:, bass.ds(b * D, D)]
                settle(dve)
                dve.tensor_copy(Y[:, 0:NREL], acc[:, bass.ds(b * ACCW + D, NREL)]).then_inc(s_("n3_c"), 1)
                dve.wait_ge(s_("n3_r"), b + 1)
                settle(dve)
                ln(dve.tensor_copy(XS[:, :], xb))
                dve.tensor_tensor(A[:, :], acc[:, bass.ds(b * ACCW, D)], PS[1][:, 0:D], ALU.add
                                  ).then_inc(s_("n3_a"), 1)
                dve.wait_ge(s_("n3_rz"), b + 1)
                ln(dve.tensor_tensor(A[:, :], gru[:, 0:D], PS[5][:, 0:D], ALU.mult))
                dve.tensor_tensor(A[:, :], A[:, :], PS[4][:, 0:D], ALU.add).then_inc(s_("n3_t"), 1)
                dve.wait_ge(s_("n3_n"), b + 1)
                ln(dve.tensor_tensor(Y[:, :], xb, gru[:, 2 * D:3 * D], ALU.subtract))
                ln(dve.tensor_tensor(Y[:, :], Y[:, :], gru[:, D:2 * D], ALU.mult))
                ln(dve.tensor_tensor(Y[:, :], Y[:, :], gru[:, 2 * D:3 * D], ALU.add))
                ln(dve.tensor_tensor(Y[:, :], Y[:, :], xb, ALU.add))
                norm("n3", b, ln, XS[:, :]).then_inc(s_("n3_ln"), 1)
                dve.wait_ge(s_("n3_ln"), b + 1)
                settle(dve)
                ln(dve.tensor_copy(xb, XS[:, :]))
                dve.wait_ge(s_("n3_h1"), b + 1)
                dve.wait_ge(tabs, b * 16 + 16 * 3 * NB)
                dve.tensor_scalar(KV[:, 0:D1], PS[1][:, 0:D1], dinv[:, bass.ds(b, 1)], None, ALU.mult
                                  ).then_inc(s_("n3_h"), 1)
                dve.wait_ge(s_("n3_h"), b + 1)
                settle(dve)
                dve.tensor_copy(Q[:, bass.ds(b * D, D1)], KV[:, 0:D1]).then_inc(s_("n3_hs"), 1)
                ln.end()
            link2(dve.memset(acc[:, :], 0.0))
            sums(pc1)
            dve.wait_ge(pc1.added, T + PR)

            def gcn(name, b, ln, w, boff, last_sem, at):
                ln(dve.tensor_tensor(A[:, 0:w], acc[:, bass.ds(b * ACCW, w)], Q[:, bass.ds(b * D, w)], ALU.add))
                ln(dve.scalar_tensor_tensor(A[:, 0:w], A[:, 0:w], dinv[:, bass.ds(b, 1)],
                                            b12[:, boff:boff + w], ALU.mult, ALU.add))
                dve.tensor_scalar(A[:, 0:w], A[:, 0:w], 0.0, None, ALU.max).then_inc(s_(name + "_a"), 1)

            dve.wait_ge(tabs, 16 * 4 * NB)
            dve.wait_ge(s_("n3_hs"), NB)
            with dve.Fori(0, NB) as b:
                ln = Link(dve, s_("n4_link"), 0, b, 2)
                gcn("n4", b, ln, D1, 0, None, None)
                dve.wait_ge(s_("n4_h2"), b + 1)
                dve.wait_ge(tabs, b * 16 + 16 * 4 * NB)
                dve.tensor_scalar(KV[:, 0:D2], PS[1][:, 0:D2], dinv[:, bass.ds(b, 1)], None, ALU.mult
                                  ).then_inc(s_("n4_h"), 1)
                dve.wait_ge(s_("n4_h"), b + 1)
                settle(dve)
                dve.tensor_copy(Q[:, bass.ds(b * D, D2)], KV[:, 0:D2]).then_inc(s_("n4_hs"), 1)
                ln.end()
            link2(dve.memset(acc[:, :], 0.0))
            sums(pc2)
            dve.wait_ge(pc2.added, T + PR)
            dve.wait_ge(tabs, 16 * 5 * NB)
            dve.wait_ge(s_("n4_hs"), NB)
            with dve.Fori(0, NB) as b:
                ln = Link(dve, s_("n5_link"), 0, b, 6)
                gcn("n5", b, ln, D2, D1, None, None)
                dve.wait_ge(s_("n5_f2"), b + 1)
                ln(dve.tensor_tensor(Y[:, :], X[:, bass.ds(b * D, D)], PS[3][:, 0:D], ALU.add))
                ln(norm("n5", b, ln, X[:, bass.ds(b * D, D)]))
                ln.end()
            dve.sem_inc(s_("n5_done"), 1)


_INS = ['x', 'src', 'dst', 'edge_attr_8', 'edge_type_16', 'edge_weight', 'L0_gnn_W', 'L0_gnn_b', 'L1_gnn_Wq',
        'L1_gnn_Wk', 'L1_gnn_Wv', 'L1_gnn_Wo', 'L2_gnn_relvectors', 'L2_gnn_w_ih', 'L2_gnn_w_hh', 'L2_gnn_b_ih',
        'L2_gnn_b_hh', 'L3_gnn_W1', 'L3_gnn_b1', 'L3_gnn_W2', 'L3_gnn_b2', 'L3_gnn_fc1_w', 'L3_gnn_fc1_b',
        'L3_gnn_fc2_w', 'L3_gnn_fc2_b']


def kernel(**inputs):
    import numpy as _np
    import concourse.bacc as _bacc
    from concourse import mybir as _mybir
    from concourse.bass_utils import run_bass_kernel_spmd as _run

    nc = _bacc.Bacc("TRN2", target_bir_lowering=False, num_devices=1)
    arrays, args = {}, []
    for name in _INS:
        a = _np.ascontiguousarray(inputs[name])
        arrays[f"in_{name}_dram"] = a
        args.append(nc.dram_tensor(f"in_{name}_dram", a.shape, _mybir.dt.from_np(a.dtype), kind="ExternalInput").ap())
    out = nc.dram_tensor("out_0_dram", tuple(inputs['x'].shape), _mybir.dt.float32, kind="ExternalOutput").ap()
    gnn_kernel(nc, *args, out)
    r = _run(nc, [arrays], core_ids=[0])
    return r.results[0]["out_0_dram"]
```

```python
from contextlib import ExitStack

import concourse.bass as bass
from concourse import mybir

F32 = mybir.dt.float32
I32 = mybir.dt.int32
ALU = mybir.AluOpType
ACT = mybir.ActivationFunctionType
AX = mybir.AxisListType

P = 128
EPS = 1e-5
BIG = float(2**100)
RECW = 13
R_SRC, R_DST, R_TYPE, R_W, R_POS, R_BIAS = 0, 1, 2, 3, 4, 5
U = 8
PR = 4
AHEAD = 2 * U
GRP = 16


class Link:

    def __init__(self, eng, sem, done=0, turn=None, per_turn=0):
        self.eng, self.sem, self.done, self.turn, self.per_turn, self.n = eng, sem, done, turn, per_turn, 0

    def __call__(self, ins):
        self.n += 1
        ins.then_inc(self.sem, 1)
        at = self.done + self.n
        self.eng.wait_ge(self.sem, at if self.turn is None else self.turn * self.per_turn + at)

    def end(self):
        assert self.turn is None or self.n == self.per_turn, (self.n, self.per_turn)


def staged(eng, turns, *stages):
    most = max(lead for lead, _ in stages)
    for t in range(-most, 0):
        for lead, stage in stages:
            if t + lead >= 0:
                stage(t + lead, (t + lead) % U, (t + lead) // U)
    with eng.Fori(0, turns - 1) as i:
        for u in range(U):
            for lead, stage in stages:
                v = u + lead
                stage(i * U + v, v % U, i + v // U)
    for t in range((turns - 1) * U, turns * U):
        for lead, stage in stages:
            if t + lead < turns * U:
                stage(t + lead, (t + lead) % U, (t + lead) // U)


def gnn_kernel(nc, x, src, dst, edge_attr, edge_type, edge_weight, w0, b0, wq, wk, wv, wo, rel,
               w_ih, w_hh, b_ih, b_hh, w1, b1, w2, b2, fc1_w, fc1_b, fc2_w, fc2_b, out, debug=None):
    N, D = x.shape
    E, H = edge_attr.shape
    NREL = rel.shape[0]
    D1, D2, DF = w1.shape[1], w2.shape[1], fc1_w.shape[1]
    DH = D // H
    NB = -(-N // P)
    NLAST = N - (NB - 1) * P
    EC = E // P
    EREST = E - EC * P
    T = -(-(-(-E // P) + NB - 1) // GRP) * GRP
    TURNS = T // U
    SCALE = float(DH) ** 0.5
    assert D == 256 and H * GRP == P and EREST < P

    tab_rec = nc.dram_tensor("tab_rec", (E + P, RECW), I32, kind="Internal").ap()
    MW = D + 1
    tab_m = nc.dram_tensor("tab_m", (E + P, MW), F32, kind="Internal").ap()
    tab_k = nc.dram_tensor("tab_k", (NB * P, D), F32, kind="Internal").ap()
    tab_v = nc.dram_tensor("tab_v", (NB * P, D), F32, kind="Internal").ap()
    tab_x = nc.dram_tensor("tab_x", (NB * P, D), F32, kind="Internal").ap()
    tab_h1 = nc.dram_tensor("tab_h1", (NB * P, D1), F32, kind="Internal").ap()
    tab_h2 = nc.dram_tensor("tab_h2", (NB * P, D2), F32, kind="Internal").ap()

    with ExitStack() as ctx:
        def sb(name, shape, dt=F32):
            return ctx.enter_context(nc.sbuf_tensor(name, shape, dt))

        def sem(name):
            return ctx.enter_context(nc.semaphore(name))

        X = sb("X", [P, NB * D])
        ACCW = 272
        acc = sb("acc", [P, NB * ACCW])
        Q = sb("Q", [P, NB * D])
        S = sb("S", [P, T * H])
        rec = sb("rec", [P, T * RECW], I32)
        recf = rec[:, :].bitcast(F32)
        rec3 = rec[:, :].rearrange("p (t c) -> p t c", c=RECW)
        recf3 = recf.rearrange("p (t c) -> p t c", c=RECW)
        NWT = 10 + 2 * (3 * D // P)
        WT = sb("WT", [P, 2, NWT * P])
        W1 = sb("W1", [P, 2, D1])
        W2 = sb("W2", [P, D2])
        FC1 = sb("FC1", [D2, DF])
        FC2 = sb("FC2", [P, D])
        REL = sb("REL", [NREL, D])
        BO = {}
        o = 0
        for n, w in (("b0", D), ("ih", 3 * D), ("hh", 3 * D), ("fc1", DF), ("fc2", D), ("b1", D1), ("b2", D2)):
            BO[n] = o
            o += w
        brow = sb("brow", [1, o])
        b12 = sb("b12", [P, D1 + D2])
        wnat = Q[:, 0:NWT * D].rearrange("p (r n) -> p r n", n=D)
        G = sb("G", [P, U, D + 4])
        oh = sb("oh", [P, U, P])
        ohT = sb("ohT", [P, 4, P])
        tyf = sb("tyf", [P, U, NREL])
        workf = sb("work", [P, 4 * (D + H)])
        work = workf[:, :].rearrange("p (s n) -> p s n", s=4)
        idx = sb("idx", [P, 2, U], I32)
        srci = sb("srci", [P, T + U], I32)
        posi = sb("posi", [P, T + U], I32)
        gru = sb("gru", [P, 4 * D])
        prod = gru[:, :].rearrange("p (s n) -> p s n", s=4)
        small_t = gru[:, 0:T]
        sg_row = gru[0:1, T:2 * T]
        epsb = sb("epsb", [P, 1])
        ident = sb("ident", [P, P])
        ones = sb("ones", [P, P])
        iota_i = workf[:, 0:512].bitcast(I32)
        iota_f = sb("iota_f", [P, 512])
        dstl = sb("dstl", [P, T])
        bs_row = [sb(f"bs_row{k}", [1, T], I32) for k in range(2)]
        as_row = [sb(f"as_row{k}", [1, T], I32) for k in range(2)]
        offs = sb("offs", [P, T])
        cnt = sb("cnt", [P, NB])
        cntn = [sb(f"cntn{k}", [P, NB]) for k in range(2)]
        place = sb("place", [P, NB])
        triP = sb("triP", [P, P])
        small = sb("small", [P, 16])
        smalli = sb("smalli", [P, 4], I32)
        tri = sb("tri", [NB, NB])
        past = workf[0:NB, 512:512 + T]
        mx = sb("mx", [P, NB * H])
        dinv = sb("dinv", [P, NB])
        A = sb("A", [P, D])
        AT = sb("AT", [P, 2, P])
        XS = sb("XS", [P, D])
        XT = sb("XT", [P, 2, P])
        Y = sb("Y", [P, D])
        KV = sb("KV", [P, 2 * D])
        stats = sb("stats", [P, 8])
        mv = sb("mv", [P, 4])
        sg = sb("sg", [P, P])
        dg = sb("dg", [P, P])
        sT = sb("sT", [P, P])
        dT = sb("dT", [P, P + 2])
        fl = sb("fl", [P, P])
        la = sb("la", [P, P])
        ms = sb("ms", [P, P])
        mrow = sb("mrow", [P, GRP, H + 1])
        padr = sb("padr", [P, RECW], I32)
        rest = acc[:, (EC + 1) * RECW:]
        recs = acc[:, 0:(EC + 1) * RECW].bitcast(I32).rearrange("p (t c) -> p t c", c=RECW)
        recsf = acc[:, 0:(EC + 1) * RECW].rearrange("p (t c) -> p t c", c=RECW)
        in_src = S[:, 0:EC + 1].bitcast(I32)
        in_dst = S[:, EC + 1:2 * (EC + 1)].bitcast(I32)
        in_typ = S[:, 2 * (EC + 1):3 * (EC + 1)].bitcast(I32)
        in_w = S[:, 3 * (EC + 1):4 * (EC + 1)]
        in_att = rec[:, 0:(EC + 1) * H].bitcast(F32)
        junk = S[:, 4 * (EC + 1):5 * (EC + 1)]
        tile_of = S[:, 5 * (EC + 1):6 * (EC + 1)]
        pos = S[:, 6 * (EC + 1):7 * (EC + 1)]
        run_to = rest[:, 0:EC + 1]
        in_it = rest[:, EC + 1:2 * (EC + 1)].bitcast(I32)
        ones_t = rest[:, 2 * (EC + 1):3 * (EC + 1)]

        PS = [ctx.enter_context(nc.psum_tensor(f"PS{i}", [P, 512], F32)) for i in range(8)]

        block_sems = {}

        def s_(name):
            if name not in block_sems:
                block_sems[name] = sem(name)
            return block_sems[name]

        ld_w, ld_x, ld_e = s_("ld_w"), s_("ld_x"), s_("ld_e")
        blank, consts = s_("blank"), s_("consts")
        wt_t, wt_c = s_("wt_t"), s_("wt_c")
        recs_done, rec_out, rec_in = s_("recs_done"), s_("rec_out"), s_("rec_in")
        v_set, pe_set = s_("v_set"), s_("pe_set")
        tabs = s_("tabs")
        N_W = 5 * 1 + 2 + 5 + 7
        passed = sem("passed")
        block = ctx.enter_context(nc.Block())

        def rows(ap, n):
            return ap.rearrange("(a n) -> a n", a=1)

        class Pass:

            def __init__(self, name, table, width):
                self.name, self.table, self.w = name, table, width
                self.rows = ROWS
                self.used = sem(name + "_used")
                self.oh = sem(name + "_oh") if name not in ("keys", "vals") else None
                self.added = sem(name + "_added") if name != "keys" else None

        NORMS = ["n1", "n2", "n3", "n5"]
        ROWS = [sem(f"rows{u}") for u in range(U)]
        IDX = [sem(f"idx{w}") for w in range(2)]
        pm = Pass("send", tab_m, MW)
        p0 = Pass("take", tab_m, D)
        pk = Pass("keys", tab_k, D)
        pv = Pass("vals", tab_v, D)
        p2 = Pass("msgs", tab_x, D)
        pc1 = Pass("gcn1", tab_h1, D1)
        pc2 = Pass("gcn2", tab_h2, D2)
        ORDER = [pm, pk, pv, p2, pc1, pc2]
        for n, p in enumerate(ORDER):
            p.base = 16 * TURNS * n
            p.wins = [16 * (TURNS // 2 * n + (n > 0)), 16 * (TURNS // 2 * n)]
        p0.rows, p0.base = [sem(f"taken{u}") for u in range(U)], 0

        def settle(eng):
            eng.sem_inc(passed, 1)

        @block.gpsimd
        def _(pool):
            pool.memset(ident[:, :], 0.0).then_inc(blank, 1)
            pool.memset(tri[:, :], 1.0).then_inc(blank, 1)
            pool.memset(triP[:, :], 1.0).then_inc(blank, 1)
            pool.memset(ones[:, :], 1.0).then_inc(consts, 1)
            pool.iota(iota_i, [[1, 512]], base=0, channel_multiplier=0).then_inc(blank, 1)
            pool.wait_ge(blank, 4)
            pool.affine_select(out=ident[:, :], in_=ident[:, :], compare_op=ALU.not_equal, fill=1.0, base=0,
                               pattern=[[-1, P]], channel_multiplier=1).then_inc(consts, 1)
            pool.affine_select(out=tri[:, :], in_=tri[:, :], compare_op=ALU.is_ge, fill=0.0, base=0,
                               pattern=[[1, NB]], channel_multiplier=-1).then_inc(consts, 1)
            pool.tensor_copy(iota_f[:, :], iota_i).then_inc(consts, 1)

            pool.wait_ge(blank, 4)
            pool.affine_select(out=triP[:, :], in_=triP[:, :], compare_op=ALU.is_gt, fill=0.0, base=0,
                               pattern=[[1, P]], channel_multiplier=-1).then_inc(consts, 1)

            with pool.Fori(0, TURNS // 2) as i:
                for u in range(2 * U):
                    if u % U == 0:
                        pool.wait_ge(IDX[u // U], i * 16 + (pm.wins[u // U] + 16))
                    pool.wait_ge(pm.added, i * (2 * U) + (u + 1 + PR))
                    pool.wait_ge(pm.oh, i * (2 * U) + (u + 1))
                    settle(pool)
                    pool.indirect_dma_start(tab_m[0:E, :],
                                            bass.IndirectOffsetOnAxis(ap=idx[:, u // U, u % U:u % U + 1], axis=0),
                                            G[:, u % U, :MW], None, bounds_check=E - 1, oob_is_err=False
                                            ).then_inc(pm.rows[u % U], 16)

            def gathers(p, ready, count):
                pool.wait_ge(ready, count)
                with pool.Fori(0, TURNS // 2) as i:
                    for u in range(2 * U):
                        if u % U == 0:
                            pool.wait_ge(IDX[u // U], i * 16 + (p.wins[u // U] + 16))
                        pool.wait_ge(p.used, i * (2 * U) + (u + 1 + AHEAD - U))
                        settle(pool)
                        pool.indirect_dma_start(G[:, u % U, :p.w], None, p.table,
                                                bass.IndirectOffsetOnAxis(ap=idx[:, u // U, u % U:u % U + 1], axis=0)
                                                ).then_inc(p.rows[u % U], 16)

            gathers(pk, tabs, 16 * 2 * NB)
            gathers(pv, tabs, 16 * 2 * NB)
            gathers(p2, tabs, 16 * 3 * NB)
            gathers(pc1, tabs, 16 * 4 * NB)
            gathers(pc2, tabs, 16 * 5 * NB)

        def rec_loads(eng, begin, end):
            with eng.Fori(begin, end) as i:
                first = [eng.value_load(as_row[0][0:1, bass.ds(i * U + u, 1)], min_val=0, max_val=E)
                         for u in range(U)]
                for u in range(U):
                    eng.dma_start(rec[:, bass.ds(i * (U * RECW) + u * RECW, RECW)],
                                  tab_rec[bass.ds(first[u], P), :]).then_inc(rec_in, 16)

        @block.sync
        def _(sp):
            sp.wait_ge(v_set, 1)
            nx = (NB - 1) * P
            sp.dma_start(X[:, 0:(NB - 1) * D].rearrange("p (b n) -> p b n", n=D),
                         x[0:nx, :].rearrange("(b p) n -> p b n", p=P)).then_inc(ld_x, 16)
            sp.dma_start(X[0:NLAST, (NB - 1) * D:NB * D], x[nx:N, :]).then_inc(ld_x, 16)
            for to, of in ((in_dst, dst), (in_src, src), (in_typ, edge_type), (in_w, edge_weight)):
                sp.dma_start(to[:, 0:EC], of[0:EC * P].rearrange("(p t) -> p t", t=EC)).then_inc(ld_e, 16)
                sp.dma_start(to[0:EREST, EC:EC + 1],
                             of[EC * P:E].rearrange("(p t) -> p t", t=1)).then_inc(ld_e, 16)
            sp.dma_start(in_att[:, 0:EC * H], edge_attr[0:EC * P, :].rearrange("(p t) h -> p (t h)", t=EC)
                         ).then_inc(ld_e, 16)
            sp.dma_start(in_att[0:EREST, EC * H:(EC + 1) * H], edge_attr[EC * P:E, :]).then_inc(ld_e, 16)
            sp.wait_ge(recs_done, 2)
            sp.dma_start(tab_rec[0:EC * P, :].rearrange("(p t) c -> p t c", t=EC), recs[:, 0:EC, :]
                         ).then_inc(rec_out, 16)
            sp.dma_start(tab_rec[EC * P:E, :], recs[0:EREST, EC, :]).then_inc(rec_out, 16)
            sp.dma_start(tab_rec[E:E + P, :], padr[:, :]).then_inc(rec_out, 16)
            sp.wait_ge(s_("pad_m"), 1)
            sp.dma_start(tab_m[E:E + P, :], G[:, 0, 0:MW]).then_inc(rec_out, 16)
            sp.wait_ge(rec_out, 64)
            sp.wait_ge(v_set, 3)
            rec_loads(sp, 0, TURNS // 2)

            def window(p, of, i, w):
                sp.wait_ge(p.used, i * (2 * U) + (U * w + U))
                sp.dma_start(idx[:, w, :], of[:, bass.ds(i * (2 * U) + U * w, U)]).then_inc(IDX[w], 16)

            def windows(p):
                with sp.Fori(0, TURNS // 2) as i:
                    window(p, srci, i, 0)
                    window(p, srci, i, 1)

            sp.wait_ge(s_("places"), 1)
            sp.sem_inc(pm.used, AHEAD)
            window(pm, posi, 0, 0)
            with sp.Fori(0, TURNS // 2) as i:
                for w in range(2):
                    window(pm, posi, i + w, 1 - w)
                    for u in range(U):
                        sp.wait_ge(pm.rows[u], i * 32 + (16 * w + 16))
                        sp.sem_inc(pm.used, 1)
            with sp.Fori(0, TURNS) as i:
                first = [sp.value_load(as_row[1][0:1, bass.ds(i * U + u, 1)], min_val=0, max_val=E)
                         for u in range(U)]
                for u in range(U):
                    sp.wait_ge(p0.used, i * U + (u + 1 + AHEAD - U))
                    sp.dma_start(G[:, u, 0:MW], tab_m[bass.ds(first[u], P), :]).then_inc(p0.rows[u], 16)

            def store(ready, table, of):
                with sp.Fori(0, NB) as b:
                    sp.wait_ge(ready, b + 1)
                    for tb, o in zip(table, of):
                        sp.dma_start(tb[bass.ds(b * P, P), :], o).then_inc(tabs, 16)

            store(s_("n1_kv"), (tab_k, tab_v), (KV[:, 0:D], KV[:, D:2 * D]))
            windows(pk)
            windows(pv)
            store(s_("n2_x"), (tab_x,), (XS[:, :],))
            windows(p2)
            store(s_("n3_h"), (tab_h1,), (KV[:, 0:D1],))
            windows(pc1)
            store(s_("n4_h"), (tab_h2,), (KV[:, 0:D2],))
            windows(pc2)
            sp.wait_ge(s_("n5_done"), 1)
            sp.dma_start(out[0:nx, :].rearrange("(b p) n -> p b n", p=P),
                         X[:, 0:(NB - 1) * D].rearrange("p (b n) -> p b n", n=D)).then_inc(s_("out"), 16)
            sp.dma_start(out[nx:N, :], X[0:NLAST, (NB - 1) * D:NB * D]).then_inc(s_("out"), 16)
            sp.wait_ge(s_("out"), 32)

        WMATS = [(w0, D), (wq, D), (wk, D), (wv, D), (wo, D), (w_ih, 3 * D), (w_hh, 3 * D)]
        WCOL = {}
        o = 0
        for n, (_, r) in zip(("w0", "wq", "wk", "wv", "wo", "ih", "hh"), WMATS):
            WCOL[n] = o
            o += r

        @block.scalar
        def _(act):
            r = 0
            for w, n in WMATS:
                act.dma_start(wnat[:, r:r + n // P, :], w.rearrange("(r p) n -> p r n", p=P)).then_inc(ld_w, 16)
                r += n // P
            act.dma_start(W1[:, :, :], w1.rearrange("(c p) n -> p c n", p=P)).then_inc(ld_w, 16)
            act.dma_start(W2[:, :], w2).then_inc(ld_w, 16)
            act.dma_start(FC1[:, :], fc1_w).then_inc(ld_w, 16)
            act.dma_start(FC2[:, :], fc2_w).then_inc(ld_w, 16)
            act.dma_start(REL[:, :], rel).then_inc(ld_w, 16)
            for n, b in (("b0", b0), ("ih", b_ih), ("hh", b_hh), ("fc1", fc1_b), ("fc2", fc2_b), ("b1", b1), ("b2", b2)):
                act.dma_start(brow[:, BO[n]:BO[n] + b.shape[0]], rows(b, b.shape[0])).then_inc(ld_w, 16)
            for r in range(NWT):
                act.wait_ge(wt_t, r + 1)
                act.copy(WT[:, :, r * P:(r + 1) * P],
                         PS[r % 4][:, 0:2 * P].rearrange("p (c n) -> p c n", c=2)).then_inc(wt_c, 1)
            act.wait_ge(wt_t, NWT + 1)
            act.copy(b12[:, :], PS[4][:, 0:D1 + D2]).then_inc(wt_c, 1)

            act.wait_ge(rec_out, 64)
            act.wait_ge(v_set, 3)
            rec_loads(act, TURNS // 2, TURNS)

            def norm_std(l, name, b):
                act.wait_ge(s_("var"), b + (NORMS.index(name) * NB + 1))
                act.activation(mv[:, 2:3], mv[:, 1:2], ACT.Sqrt, bias=epsb[:, 0:1]).then_inc(s_("std"), 1)

            def turned(name):
                def stage(t, r, turn):
                    act.wait_ge(s_(name + "_ohT"), t + 1)
                    act.wait_ge(s_(name + "_sel"), t + (1 + U - 4))
                    act.copy(ohT[:, r % 4, :], PS[r % 2][:, 0:P]).then_inc(s_(name + "_ohTc"), 1)
                return stage

            act.wait_ge(s_("places"), 1)
            act.sem_inc(s_("send_ohTc"), 2)
            staged(act, TURNS, (0, turned("send")))
            with act.Fori(0, NB) as b:
                act.wait_ge(s_("n1_free"), b + 1)
                act.copy(A[:, :], acc[:, bass.ds(b * ACCW, D)]).then_inc(s_("n1_a"), 1)
                act.wait_ge(s_("n1_aT"), b + 1)
                act.copy(AT[:, :, :], PS[0][:, 0:D].rearrange("p (c n) -> p c n", c=2)).then_inc(s_("n1_aTc"), 1)
                norm_std(None, "n1", b)
                act.wait_ge(s_("n1_xT"), b + 1)
                act.copy(XT[:, :, :], PS[2][:, 0:D].rearrange("p (c n) -> p c n", c=2)).then_inc(s_("n1_xTc"), 1)
                act.wait_ge(s_("n1_qkv"), b + 1)
                act.mul(Q[:, bass.ds(b * D, D)], PS[3][:, 0:D], SCALE).then_inc(s_("n1_q"), 1)
                act.copy(KV[:, :], PS[4][:, 0:2 * D]).then_inc(s_("n1_kv"), 1)
                act.wait_ge(tabs, b * 32 + 32)

            act.sem_inc(s_("keys_ohTc"), 2)
            staged(act, TURNS, (0, turned("keys")))
            with act.Fori(0, T // GRP) as g:
                act.wait_ge(s_("m_sg"), g + 1)
                act.copy(S[:, bass.ds(g * P, P)], sg[:, :]).then_inc(s_("m_s"), 1)
                act.wait_ge(s_("m_T"), g * 2 + 1)
                act.copy(sT[:, :], PS[0][:, 0:P]).then_inc(s_("m_Tc"), 1)
                act.copy(dT[:, 1:P + 1], PS[1][:, 0:P]).then_inc(s_("m_Tc"), 1)
                act.wait_ge(s_("m_T"), g * 2 + 2)
                act.copy(mrow[:, :, 0:H], PS[2][:, 0:P].rearrange("p (t h) -> p t h", h=H)).then_inc(s_("m_row"), 1)
                act.copy(mrow[:, :, H:H + 1], PS[3][:, 0:P].rearrange("p (t h) -> p t h", h=H)[:, :, 0:1]
                         ).then_inc(s_("m_row"), 1)
            def exponentials(t, r, turn):
                act.wait_ge(s_("vals_d"), t + 3)
                act.activation(work[:, r % 4, D:D + H], work[:, r % 4, D:D + H], ACT.Exp
                               ).then_inc(s_("vals_e"), 1)

            act.sem_inc(s_("vals_ohTc"), 2)
            staged(act, TURNS, (1, turned("vals")), (0, exponentials))
            with act.Fori(0, NB) as b:
                act.wait_ge(s_("n2_aT"), b + 1)
                act.copy(AT[:, :, :], PS[0][:, 0:D].rearrange("p (c n) -> p c n", c=2)).then_inc(s_("n2_aTc"), 1)
                norm_std(None, "n2", b)
            act.wait_ge(s_("n3_deg"), 1)
            act.activation(dinv[:, :], dinv[:, :], ACT.Sqrt).then_inc(s_("n3_degs"), 1)
            with act.Fori(0, NB) as b:
                act.wait_ge(s_("n3_cT"), b + 1)
                act.copy(AT[0:NREL, 0, :], PS[0][0:NREL, 0:P]).then_inc(s_("n3_cTc"), 1)
                act.wait_ge(s_("n3_aT"), b + 1)
                act.copy(AT[:, :, :], PS[0][:, 0:D].rearrange("p (c n) -> p c n", c=2)).then_inc(s_("n3_aTc"), 1)
                act.copy(XT[:, :, :], PS[2][:, 0:D].rearrange("p (c n) -> p c n", c=2)).then_inc(s_("n3_aTc"), 1)
                act.wait_ge(s_("n3_g"), b + 1)
                act.activation(gru[:, 0:2 * D], PS[3][:, 0:2 * D], ACT.Sigmoid).then_inc(s_("n3_rz"), 1)
                act.wait_ge(s_("n3_t"), b + 1)
                act.activation(gru[:, 2 * D:3 * D], A[:, :], ACT.Tanh).then_inc(s_("n3_n"), 1)
                norm_std(None, "n3", b)
                act.wait_ge(s_("n3_xT"), b + 1)
                act.copy(XT[:, :, :], PS[2][:, 0:D].rearrange("p (c n) -> p c n", c=2)).then_inc(s_("n3_xTc"), 1)
            with act.Fori(0, NB) as b:
                act.wait_ge(s_("n4_aT"), b + 1)
                act.copy(AT[:, 0, :], PS[0][:, 0:P]).then_inc(s_("n4_aTc"), 1)
            with act.Fori(0, NB) as b:
                act.wait_ge(s_("n5_aT"), b + 1)
                act.copy(AT[0:D2, 0, :], PS[0][0:D2, 0:P]).then_inc(s_("n5_aTc"), 1)
                act.wait_ge(s_("n5_f1"), b + 1)
                act.copy(KV[:, 0:DF], PS[1][:, 0:DF]).then_inc(s_("n5_f1c"), 1)
                act.wait_ge(s_("n5_fT"), b + 1)
                act.copy(XT[:, 0, :], PS[2][:, 0:P]).then_inc(s_("n5_fTc"), 1)
                norm_std(None, "n5", b)

        @block.tensor
        def _(pe):
            pe.wait_ge(consts, 5)
            pe.wait_ge(ld_w, 16 * 19)
            for r in range(NWT):
                if r >= 4:
                    pe.wait_ge(wt_c, r - 3)
                pe.transpose(PS[r % 4][:, 0:P], wnat[:, r, 0:P], ident[:, :])
                pe.transpose(PS[r % 4][:, P:2 * P], wnat[:, r, P:2 * P], ident[:, :]).then_inc(wt_t, 1)
            pe.matmul(PS[4][:, 0:D1 + D2], ones[0:1, :], brow[:, BO["b1"]:BO["b1"] + D1 + D2],
                      start=True, stop=True).then_inc(wt_t, 1)
            for k in range(2):
                pe.wait_ge(s_("v_cnt"), k + 1)
                pe.matmul(PS[5][0:NB, 0:1], cntn[k][:, :], ones[:, 0:1], start=True, stop=True).then_inc(pe_set, 1)
                pe.wait_ge(s_("v_nt"), 2 * k + 1)
                pe.matmul(PS[5][0:NB, 8:9], tri[:, :], small[0:NB, 1:2], start=True, stop=True).then_inc(pe_set, 1)
                pe.wait_ge(s_("v_nt"), 2 * k + 2)
                pe.wait_ge(wt_c, NWT + 1)
                pe.matmul(PS[6][0:1, 0:T], ones[0:NB, 0:1], past, start=True, stop=True)
                pe.matmul(PS[7][0:1, 0:T], small[0:NB, 2:3], past, start=True, stop=True)
                pe.matmul(PS[4][:, 0:T], ones[0:NB, :], past, start=True, stop=True).then_inc(pe_set, 1)
            pe.wait_ge(v_set, 3)
            pe.matmul(PS[4][:, 0:NB], triP[:, :], cntn[1][:, :], start=True, stop=True)
            pe.matmul(PS[5][:, 0:NB], ones[:, :], cntn[1][:, :], start=True, stop=True).then_inc(pe_set, 1)

            def bias(ps, name, n, off=0):
                pe.matmul(ps, ones[0:1, :], brow[:, BO[name] + off:BO[name] + off + n], start=True, stop=False)

            def times(ps, aT, name, off, n, start, stop=True):
                c0 = WCOL[name] + off
                for c in range(2):
                    last = pe.matmul(ps, aT[:, c, :], WT[:, c, c0:c0 + n],
                                     start=(start and c == 0), stop=(stop and c == 1))
                return last

            def turn2(ps, a):
                pe.transpose(ps[:, 0:P], a[:, 0:P], ident[:, :])
                return pe.transpose(ps[:, P:2 * P], a[:, P:2 * P], ident[:, :])

            def sums(p, types=False):
                def add(t, r, turn):
                    pe.wait_ge(p.oh, t * 2 + 2 if types else t + 1)
                    pe.wait_ge(p.rows[r], turn * 16 + (p.base + 16))
                    pe.wait_ge(p.added, t + 1)
                    last = pe.matmul(PS[4 + r % PR][:, 0:p.w], oh[:, r, :], G[:, r, :p.w], start=True, stop=True)
                    if types:
                        last = pe.matmul(PS[4 + r % PR][:, D:D + NREL], oh[:, r, :], tyf[:, r, :],
                                         start=True, stop=True)
                    last.then_inc(p.used, 1)

                pe.sem_inc(p.used, AHEAD)
                staged(pe, TURNS, (0, add))

            def turns(name):
                def stage(t, r, turn):
                    pe.wait_ge(s_(name + "_1h"), t + 1)
                    pe.wait_ge(s_(name + "_ohTc"), t + 1)
                    pe.transpose(PS[r % 2][:, 0:P], oh[:, r, :], ident[:, :]).then_inc(s_(name + "_ohT"), 1)
                return stage

            def tile_at(t):
                return pe.value_load(bs_row[0][0:1, bass.ds(t, 1)], min_val=0, max_val=NB - 1)

            def pick_rows(t, r, turn):
                tile = tile_at(t)
                pe.wait_ge(s_("send_ohTc"), t + 3)
                pe.wait_ge(pm.added, t + 1)
                pe.matmul(PS[4 + r % PR][:, 0:D], ohT[:, r % 4, :], X[:, bass.ds(tile * D, D)],
                          start=True, stop=True).then_inc(s_("send_sel"), 1)

            pe.wait_ge(s_("places"), 1)
            pe.wait_ge(ld_x, 32)
            pe.sem_inc(s_("send_sel"), U)
            staged(pe, TURNS, (1, turns("send")), (0, pick_rows))
            sums(p0)
            with pe.Fori(0, NB) as b:
                pe.wait_ge(s_("n1_a"), b + 1)
                turn2(PS[0], A).then_inc(s_("n1_aT"), 1)
                pe.wait_ge(s_("n1_aTc"), b + 1)
                bias(PS[1][:, 0:D], "b0", D)
                times(PS[1][:, 0:D], AT, "w0", 0, D, False).then_inc(s_("n1_h"), 1)
                pe.wait_ge(s_("n1_ln"), b + 1)
                turn2(PS[2], XS).then_inc(s_("n1_xT"), 1)
                pe.wait_ge(s_("n1_xTc"), b + 1)
                times(PS[3][:, 0:D], XT, "wq", 0, D, True)
                times(PS[4][:, 0:D], XT, "wk", 0, D, True)
                times(PS[4][:, D:2 * D], XT, "wv", 0, D, True).then_inc(s_("n1_qkv"), 1)

            pe.wait_ge(s_("n1_kv"), NB)
            def pick_queries(t, r, turn):
                tile = tile_at(t)
                pe.wait_ge(s_("keys_ohTc"), t + 3)
                pe.wait_ge(pk.used, t + (1 + AHEAD - PR))
                pe.matmul(PS[4 + r % PR][:, 0:D], ohT[:, r % 4, :], Q[:, bass.ds(tile * D, D)],
                          start=True, stop=True).then_inc(s_("keys_sel"), 1)

            pe.sem_inc(s_("keys_sel"), U)
            staged(pe, TURNS, (1, turns("keys")), (0, pick_queries))
            pe.sem_inc(s_("m_mm"), PR)
            with pe.Fori(0, T // GRP) as g:
                pe.wait_ge(s_("m_sg"), g + 1)
                pe.wait_ge(s_("m_dg"), g + 1)
                pe.transpose(PS[0][:, 0:P], sg[:, :], ident[:, :])
                pe.transpose(PS[1][:, 0:P], dg[:, :], ident[:, :]).then_inc(s_("m_T"), 1)
                pe.wait_ge(s_("m_ms"), g + 1)
                pe.transpose(PS[2][:, 0:P], ms[:, :], ident[:, :])
                pe.transpose(PS[3][:, 0:P], la[:, :], ident[:, :]).then_inc(s_("m_T"), 1)
                pe.wait_ge(s_("m_row"), g * 2 + 2)
                for u in range(GRP):
                    pe.wait_ge(s_("m_oh"), g * GRP + (u + 1))
                    pe.wait_ge(s_("m_added"), g * GRP + (u + 1))
                    pe.matmul(PS[4 + u % PR][:, 0:H + 1], oh[:, u % PR, :], mrow[:, u, :],
                              start=True, stop=True).then_inc(s_("m_mm"), 1)
            def pick_max(t, r, turn):
                tile = tile_at(t)
                pe.wait_ge(s_("vals_ohTc"), t + 3)
                pe.wait_ge(s_("vals_d"), t + 1)
                pe.matmul(PS[2 + r % 2][:, 0:H], ohT[:, r % 4, :], mx[:, bass.ds(tile * H, H)],
                          start=True, stop=True).then_inc(s_("vals_sel"), 1)

            def sum_values(t, r, turn):
                pe.wait_ge(s_("vals_vp"), t + 1)
                pe.wait_ge(pv.added, t + 1)
                pe.matmul(PS[4 + r % PR][:, 0:D + H], oh[:, r, :], work[:, r % 4, :],
                          start=True, stop=True).then_inc(pv.used, 1)

            pe.sem_inc(s_("vals_sel"), U)
            pe.sem_inc(pv.used, AHEAD)
            staged(pe, TURNS, (3, turns("vals")), (2, pick_max), (0, sum_values))
            with pe.Fori(0, NB) as b:
                pe.wait_ge(s_("n2_a"), b + 1)
                turn2(PS[0], A).then_inc(s_("n2_aT"), 1)
                pe.wait_ge(s_("n2_aTc"), b + 1)
                times(PS[1][:, 0:D], AT, "wo", 0, D, True).then_inc(s_("n2_h"), 1)
            sums(p2, types=True)
            with pe.Fori(0, NB) as b:
                pe.wait_ge(s_("n3_c"), b + 1)
                pe.transpose(PS[0][0:NREL, 0:P], Y[:, 0:NREL], ident[:, :]).then_inc(s_("n3_cT"), 1)
                pe.wait_ge(s_("n3_cTc"), b + 1)
                pe.matmul(PS[1][:, 0:D], AT[0:NREL, 0, :], REL[:, :], start=True, stop=True).then_inc(s_("n3_r"), 1)
                pe.wait_ge(s_("n3_a"), b + 1)
                turn2(PS[0], A)
                turn2(PS[2], XS).then_inc(s_("n3_aT"), 1)
                pe.wait_ge(s_("n3_aTc"), b * 2 + 2)
                bias(PS[3][:, 0:2 * D], "ih", 2 * D)
                pe.matmul(PS[3][:, 0:2 * D], ones[0:1, :], brow[:, BO["hh"]:BO["hh"] + 2 * D], start=False, stop=False)
                times(PS[3][:, 0:2 * D], AT, "ih", 0, 2 * D, False, stop=False)
                times(PS[3][:, 0:2 * D], XT, "hh", 0, 2 * D, False)
                bias(PS[4][:, 0:D], "ih", D, 2 * D)
                times(PS[4][:, 0:D], AT, "ih", 2 * D, D, False)
                bias(PS[5][:, 0:D], "hh", D, 2 * D)
                times(PS[5][:, 0:D], XT, "hh", 2 * D, D, False).then_inc(s_("n3_g"), 1)
                pe.wait_ge(s_("n3_ln"), b + 1)
                turn2(PS[2], XS).then_inc(s_("n3_xT"), 1)
                pe.wait_ge(s_("n3_xTc"), b + 1)
                for c in range(2):
                    last = pe.matmul(PS[1][:, 0:D1], XT[:, c, :], W1[:, c, :], start=(c == 0), stop=(c == 1))
                last.then_inc(s_("n3_h1"), 1)
            sums(pc1)
            with pe.Fori(0, NB) as b:
                pe.wait_ge(s_("n4_a"), b + 1)
                pe.transpose(PS[0][:, 0:P], A[:, 0:D1], ident[:, :]).then_inc(s_("n4_aT"), 1)
                pe.wait_ge(s_("n4_aTc"), b + 1)
                pe.matmul(PS[1][:, 0:D2], AT[:, 0, :], W2[:, :], start=True, stop=True).then_inc(s_("n4_h2"), 1)
            sums(pc2)
            with pe.Fori(0, NB) as b:
                pe.wait_ge(s_("n5_a"), b + 1)
                settle(pe)
                pe.transpose(PS[0][0:D2, 0:P], A[:, 0:D2], ident[:, :]).then_inc(s_("n5_aT"), 1)
                pe.wait_ge(s_("n5_aTc"), b + 1)
                bias(PS[1][:, 0:DF], "fc1", DF)
                pe.matmul(PS[1][:, 0:DF], AT[0:D2, 0, :], FC1[:, :], start=False, stop=True).then_inc(s_("n5_f1"), 1)
                pe.wait_ge(s_("n5_f1c"), b + 1)
                pe.transpose(PS[2][:, 0:P], KV[:, 0:DF], ident[:, :]).then_inc(s_("n5_fT"), 1)
                pe.wait_ge(s_("n5_fTc"), b + 1)
                bias(PS[3][:, 0:D], "fc2", D)
                pe.matmul(PS[3][:, 0:D], XT[:, 0, :], FC2[:, :], start=False, stop=True).then_inc(s_("n5_f2"), 1)

        @block.vector
        def _(dve):
            lk = s_("v_link")
            link = Link(dve, lk)
            NOEDGE = 1 << 20
            link(dve.memset(in_dst[:, EC:EC + 1], NOEDGE))
            link(dve.memset(in_src[:, EC:EC + 1], NOEDGE))
            link(dve.memset(in_typ[:, EC:EC + 1], 0))
            link(dve.memset(in_w[:, EC:EC + 1], 0.0))
            link(dve.memset(in_att[:, EC * H:(EC + 1) * H], 0.0))
            link(dve.memset(padr[:, :], 0))
            link(dve.memset(padr[:, R_DST:R_DST + 1].bitcast(F32), float(NOEDGE)))
            link(dve.memset(epsb[:, :], EPS))
            link(dve.memset(dT[:, :], -1.0))
            link(dve.memset(mx[:, :], -BIG))
            dve.memset(X[:, (NB - 1) * D:NB * D], 0.0).then_inc(v_set, 1)
            dve.wait_ge(ld_e, 160)
            link(dve.tensor_copy(recs[:, :, R_SRC], in_src))
            link(dve.tensor_copy(recsf[:, :, R_DST], in_dst))
            link(dve.tensor_copy(recsf[:, :, R_TYPE], in_typ))
            link(dve.tensor_copy(recsf[:, :, R_W], in_w))
            dve.tensor_copy(recsf[:, :, R_BIAS:], in_att.rearrange("p (t h) -> p t h", h=H)).then_inc(recs_done, 1)
            dve.wait_ge(recs_done, 1)
            for k, field in ((0, in_dst), (1, in_src)):
                link(dve.tensor_copy(in_it, field))
                link(dve.tensor_scalar(in_it, in_it, 7, None, ALU.arith_shift_right))
                link(dve.tensor_copy(tile_of, in_it))
                for b in range(NB):
                    link(dve.tensor_scalar(junk, tile_of, float(b), None, ALU.is_equal, ALU.add,
                                           accum_out=cntn[k][:, b:b + 1]))
                dve.sem_inc(s_("v_cnt"), 1)
            link(dve.memset(G[:, 0, :], float(NOEDGE)))
            dve.sem_inc(s_("pad_m"), 1)
            for k in range(2):
                dve.wait_ge(pe_set, 3 * k + 1)
                link(dve.tensor_scalar(smalli[0:NB, 0:1], PS[5][0:NB, 0:1], float(P - 1), None, ALU.add))
                link(dve.tensor_scalar(smalli[0:NB, 1:2], smalli[0:NB, 0:1], 7, None, ALU.arith_shift_right))
                link(dve.tensor_copy(small[0:NB, 1:2], smalli[0:NB, 1:2]))
                dve.scalar_tensor_tensor(small[0:NB, 2:3], small[0:NB, 1:2], float(-P), PS[5][0:NB, 0:1],
                                         ALU.mult, ALU.add).then_inc(s_("v_nt"), 1)
                dve.wait_ge(pe_set, 3 * k + 2)
                dve.wait_ge(consts, 5)
                link(dve.tensor_copy(small[0:NB, 3:4], PS[5][0:NB, 8:9]))
                dve.tensor_scalar(past, iota_f[0:NB, 0:T], small[0:NB, 3:4], None, ALU.is_ge
                                  ).then_inc(s_("v_nt"), 1)
                dve.wait_ge(pe_set, 3 * k + 3)
                link(dve.tensor_scalar(bs_row[k][:, :], PS[6][0:1, 0:T], float(NB - 1), None, ALU.min))
                link(dve.scalar_tensor_tensor(sg_row[:, :], iota_f[0:1, 0:T], float(P), PS[7][0:1, 0:T],
                                              ALU.mult, ALU.add))
                link(dve.tensor_scalar(as_row[k][:, :], sg_row[:, :], float(E), None, ALU.min))
                link(dve.tensor_scalar((dstl, offs)[k][:, :], PS[4][:, 0:T], float(NB - 1), -float(P),
                                       ALU.min, ALU.mult))
            dve.sem_inc(v_set, 2)
            dve.wait_ge(pe_set, 7)
            link(dve.tensor_copy(cnt[:, :], PS[5][:, 0:NB]))
            link(dve.tensor_tensor_scan(place[:, :], ones[:, 0:NB], cnt[:, :], -1.0, ALU.mult, ALU.add))
            link(dve.tensor_tensor(place[:, :], place[:, :], cnt[:, :], ALU.subtract))
            link(dve.tensor_tensor(place[:, :], place[:, :], PS[4][:, 0:NB], ALU.add))
            link(dve.memset(ones_t, 1.0))
            link(dve.memset(pos, 0.0))
            for b in range(NB):
                link(dve.tensor_scalar(junk, tile_of, float(b), None, ALU.is_equal))
                link(dve.tensor_tensor_scan(run_to, ones_t, junk, place[:, b:b + 1], ALU.mult, ALU.add))
                link(dve.tensor_tensor(run_to, run_to, junk, ALU.mult))
                link(dve.tensor_tensor(pos, pos, run_to, ALU.add))
            dve.tensor_copy(recs[:, :, R_POS], pos).then_inc(recs_done, 1)
            dve.wait_ge(rec_in, 16 * T)
            dve.wait_ge(v_set, 3)
            link(dve.tensor_tensor(dstl[:, :], dstl[:, :], recf3[:, :, R_DST], ALU.add))
            link(dve.memset(acc[:, :], 0.0))
            link(dve.tensor_scalar(small_t[:, :], dstl[:, :], 0.0, None, ALU.is_ge))
            link(dve.scalar_tensor_tensor(small_t[:, :], dstl[:, :], float(P), small_t[:, :], ALU.is_lt, ALU.mult))
            link(dve.tensor_tensor(recf3[:, :, R_BIAS:], recf3[:, :, R_BIAS:],
                                   small_t[:, :, None].to_broadcast([P, T, H]), ALU.mult))
            link(dve.tensor_scalar(small_t[:, :], small_t[:, :], -float(NOEDGE), float(NOEDGE), ALU.mult, ALU.add))
            link(dve.tensor_tensor(rec3[:, :, R_POS], rec3[:, :, R_POS], small_t[:, :], ALU.add))
            link(dve.memset(posi[:, T:], 0))
            link(dve.tensor_copy(posi[:, 0:T], rec3[:, :, R_POS]))
            link(dve.tensor_copy(srci[:, 0:T], rec3[:, :, R_SRC]))
            dve.sem_inc(s_("places"), 1)
            done = link.n

            def onehot(ready, free, ahead):
                def stage(t, r, turn):
                    dve.wait_ge(free, t + (ahead + 1 - U))
                    dve.tensor_scalar(oh[:, r, :], iota_f[:, 0:P], dstl[:, bass.ds(t, 1)], None,
                                      ALU.is_equal).then_inc(ready, 1)
                return stage

            def add_up(p, w, k=0):
                def stage(t, r, turn):
                    tile = dve.value_load(bs_row[k][0:1, bass.ds(t, 1)], min_val=0, max_val=NB - 1)
                    to = acc[:, bass.ds(tile * ACCW, w)]
                    dve.wait_ge(p.used, t + (1 + AHEAD))
                    dve.wait_ge(p.added, t + PR)
                    dve.tensor_tensor(to, to, PS[4 + r % PR][:, 0:w], ALU.add).then_inc(p.added, 1)
                return stage

            def types(t, r, turn):
                dve.wait_ge(p2.used, t + (AHEAD + 1 - U))
                dve.tensor_scalar(tyf[:, r, :], iota_f[:, 0:NREL],
                                  recf[:, bass.ds(t * RECW + R_TYPE, 1)], None, ALU.is_equal).then_inc(p2.oh, 1)

            def sums(p):
                dve.sem_inc(p.added, PR)
                staged(dve, TURNS, (4, onehot(p.oh, p.used, AHEAD)), (0, add_up(p, p.w)))

            def norm(name, b, lkn, to):
                lkn(dve.bn_stats(stats[:, 0:6], Y[:, :]))
                settle(dve)
                dve.bn_aggr(mv[:, 0:2], stats[:, 0:6]).then_inc(s_("var"), 1)
                dve.wait_ge(s_("std"), b + (NORMS.index(name) * NB + 1))
                lkn(dve.reciprocal(mv[:, 3:4], mv[:, 2:3]))
                return dve.tensor_scalar(to, Y[:, :], mv[:, 0:1], mv[:, 3:4], ALU.subtract, ALU.mult)

            def message(t, r, turn):
                dve.wait_ge(pm.used, t + (1 + AHEAD - U))
                dve.wait_ge(s_("send_sel"), t + (1 + U))
                dve.tensor_scalar(G[:, r, 0:D], PS[4 + r % PR][:, 0:D], recf[:, bass.ds(t * RECW + R_W, 1)],
                                  None, ALU.mult).then_inc(pm.added, 1)
                dve.tensor_scalar(G[:, r, D:MW], rec[:, bass.ds(t * RECW + R_SRC, 1)],
                                  1.0, None, ALU.mult).then_inc(pm.oh, 1)

            dve.sem_inc(pm.added, PR)
            staged(dve, TURNS, (4, onehot(s_("send_1h"), s_("send_sel"), U)), (0, message))

            def onehot_src(t, r, turn):
                dve.wait_ge(p0.rows[r], turn * 16 + (p0.base + 16))
                dve.wait_ge(p0.used, t + (AHEAD + 1 - U))
                dve.tensor_scalar(oh[:, r, :], iota_f[:, 0:P], G[:, r, D:MW],
                                  offs[:, bass.ds(t, 1)], ALU.subtract, ALU.is_equal).then_inc(p0.oh, 1)

            dve.wait_ge(pm.oh, T)
            dve.sem_inc(p0.added, PR)
            staged(dve, TURNS, (3, onehot_src), (0, add_up(p0, D, 1)))
            dve.wait_ge(ld_x, 32)
            dve.wait_ge(p0.added, T + PR)
            dve.sem_inc(s_("n1_free"), 1)
            k1 = s_("n1_link")
            with dve.Fori(0, NB) as b:
                ln = Link(dve, k1, 0, b, 5)
                dve.wait_ge(s_("n1_h"), b + 1)
                ln(dve.tensor_tensor(Y[:, :], X[:, bass.ds(b * D, D)], PS[1][:, 0:D], ALU.add))
                ln(norm("n1", b, ln, XS[:, :]))
                dve.sem_inc(s_("n1_ln"), 1)
                settle(dve)
                ln(dve.tensor_copy(X[:, bass.ds(b * D, D)], XS[:, :]))
                dve.wait_ge(s_("n1_qkv"), b + 1)
                dve.sem_inc(s_("n1_free"), 1)
                ln.end()
            link2 = Link(dve, lk, done)
            link2(dve.memset(acc[:, :], 0.0))
            def product(t, r, turn):
                dve.wait_ge(s_("keys_sel"), t + (1 + U))
                dve.wait_ge(pk.rows[r], turn * 16 + (pk.base + 16))
                dve.wait_ge(s_("keys_red"), t + 1)
                dve.tensor_tensor(prod[:, r % 4, :], G[:, r, 0:D], PS[4 + r % PR][:, 0:D], ALU.mult
                                  ).then_inc(pk.used, 1)

            def score(t, r, turn):
                dve.wait_ge(pk.used, t + (1 + AHEAD))
                dve.tensor_reduce(S[:, bass.ds(t * H, H)],
                                  prod[:, r % 4, :].rearrange("p (h d) -> p h d", h=H), AX.X, ALU.add
                                  ).then_inc(s_("keys_red"), 1)

            dve.sem_inc(pk.used, AHEAD)
            dve.sem_inc(s_("keys_red"), 4)
            staged(dve, TURNS, (4, onehot(s_("keys_1h"), s_("keys_sel"), U)), (1, product), (0, score))
            dve.wait_ge(s_("keys_red"), T + 4)
            dve.sem_inc(s_("m_added"), PR)
            km = s_("m_link")
            with dve.Fori(0, T // GRP) as g:
                ln = Link(dve, km, 0, g, 7)
                settle(dve)
                ln(dve.tensor_copy(dg[:, :].rearrange("p (t h) -> p t h", h=H),
                                   recf[:, bass.ds(g * (GRP * RECW), GRP * RECW)]
                                   .rearrange("p (t c) -> p t c", c=RECW)[:, :, R_DST:R_DST + 1]
                                   .to_broadcast([P, GRP, H])))
                dve.sem_inc(s_("m_dg"), 1)
                ln(dve.tensor_tensor(sg[:, :].rearrange("p (t h) -> p t h", h=H),
                                     S[:, bass.ds(g * P, P)].rearrange("p (t h) -> p t h", h=H),
                                     recf[:, bass.ds(g * (GRP * RECW), GRP * RECW)]
                                     .rearrange("p (t c) -> p t c", c=RECW)[:, :, R_BIAS:], ALU.add))
                dve.sem_inc(s_("m_sg"), 1)
                dve.wait_ge(s_("m_Tc"), g * 2 + 2)
                ln(dve.tensor_tensor(fl[:, :], dT[:, 1:P + 1], dT[:, 0:P], ALU.not_equal))
                ln(dve.tensor_scalar(fl[:, :], fl[:, :], -BIG, None, ALU.mult))
                ln(dve.tensor_tensor(la[:, :], dT[:, 1:P + 1], dT[:, 2:P + 2], ALU.not_equal))
                ln(dve.tensor_tensor_scan(ms[:, :], fl[:, :], sT[:, :], -BIG, ALU.add, ALU.max))
                ln(dve.tensor_tensor(ms[:, :], ms[:, :], la[:, :], ALU.mult))
                dve.sem_inc(s_("m_ms"), 1)
                ln.end()
                LAG = 2
                for u in range(GRP + LAG):
                    if u < GRP:
                        dve.wait_ge(s_("m_mm"), g * GRP + (u + 1))
                        dve.tensor_scalar(oh[:, u % PR, :], iota_f[:, 0:P], dstl[:, bass.ds(g * GRP + u, 1)], None,
                                          ALU.is_equal).then_inc(s_("m_oh"), 1)
                    if u >= LAG:
                        v = u - LAG
                        tile = dve.value_load(bs_row[0][0:1, bass.ds(g * GRP + v, 1)], min_val=0, max_val=NB - 1)
                        to = mx[:, bass.ds(tile * H, H)]
                        dve.wait_ge(s_("m_mm"), g * GRP + (v + 1 + PR))
                        dve.tensor_scalar(mv[:, 0:1], PS[4 + v % PR][:, H:H + 1], BIG, -BIG, ALU.mult, ALU.add
                                          ).then_inc(s_("m_off"), 1)
                        dve.wait_ge(s_("m_off"), g * GRP + (v + 1))
                        dve.scalar_tensor_tensor(to, PS[4 + v % PR][:, 0:H], mv[:, 0:1], to, ALU.add, ALU.max
                                                 ).then_inc(s_("m_added"), 1)
                        dve.wait_ge(s_("m_added"), g * GRP + (v + 1 + PR))
            def below(t, r, turn):
                dve.wait_ge(s_("vals_sel"), t + (1 + U))
                dve.wait_ge(pv.used, t + (1 + AHEAD - 4))
                dve.tensor_tensor(work[:, r % 4, D:D + H], S[:, bass.ds(t * H, H)], PS[2 + r % 2][:, 0:H],
                                  ALU.subtract).then_inc(s_("vals_d"), 1)

            def weigh(t, r, turn):
                dve.wait_ge(s_("vals_e"), t + 1)
                dve.wait_ge(pv.rows[r], turn * 16 + (pv.base + 16))
                dve.tensor_tensor(work[:, r % 4, 0:D].rearrange("p (h d) -> p h d", h=H),
                                  G[:, r, 0:D].rearrange("p (h d) -> p h d", h=H),
                                  work[:, r % 4, D:D + H, None].to_broadcast([P, H, DH]), ALU.mult
                                  ).then_inc(s_("vals_vp"), 1)

            dve.sem_inc(pv.added, PR)
            dve.sem_inc(s_("vals_d"), 2)
            staged(dve, TURNS, (6, onehot(s_("vals_1h"), pv.used, AHEAD)), (3, below), (2, weigh),
                   (0, add_up(pv, D + H)))
            dve.wait_ge(pv.added, T + PR)
            with dve.Fori(0, NB) as b:
                ln = Link(dve, s_("n2_link"), 0, b, 6)
                ln(dve.tensor_scalar(small[:, 0:H], acc[:, bass.ds(b * ACCW + D, H)], 1e-30, None, ALU.max))
                ln(dve.reciprocal(small[:, 8:8 + H], small[:, 0:H]))
                dve.tensor_tensor(A[:, :].rearrange("p (h d) -> p h d", h=H),
                                  acc[:, bass.ds(b * ACCW, D)].rearrange("p (h d) -> p h d", h=H),
                                  small[:, 8:8 + H, None].to_broadcast([P, H, DH]), ALU.mult
                                  ).then_inc(s_("n2_a"), 1)
                dve.wait_ge(s_("n2_h"), b + 1)
                ln(dve.tensor_tensor(Y[:, :], X[:, bass.ds(b * D, D)], PS[1][:, 0:D], ALU.add))
                dve.wait_ge(tabs, b * 16 + 16 * 2 * NB)
                norm("n2", b, ln, XS[:, :]).then_inc(s_("n2_x"), 1)
                dve.wait_ge(s_("n2_x"), b + 1)
                settle(dve)
                ln(dve.tensor_copy(X[:, bass.ds(b * D, D)], XS[:, :]))
                ln.end()
            link2(dve.memset(acc[:, :], 0.0))
            dve.sem_inc(p2.added, PR)
            staged(dve, TURNS, (4, types), (4, onehot(p2.oh, p2.used, AHEAD)), (0, add_up(p2, D + NREL)))
            dve.wait_ge(p2.added, T + PR)
            acc3 = acc[:, :].rearrange("p (b w) -> p b w", w=ACCW)
            link2(dve.tensor_reduce(dinv[:, :], acc3[:, :, D:D + NREL], AX.X, ALU.add))
            dve.tensor_scalar(dinv[:, :], dinv[:, :], 1.0, None, ALU.add).then_inc(s_("n3_deg"), 1)
            dve.wait_ge(s_("n3_degs"), 1)
            link2(dve.reciprocal(dinv[:, :], dinv[:, :]))
            dve.wait_ge(tabs, 16 * 3 * NB)
            with dve.Fori(0, NB) as b:
                ln = Link(dve, s_("n3_link"), 0, b, 9)
                xb = X[:, bass.ds(b * D, D)]
                settle(dve)
                dve.tensor_copy(Y[:, 0:NREL], acc[:, bass.ds(b * ACCW + D, NREL)]).then_inc(s_("n3_c"), 1)
                dve.wait_ge(s_("n3_r"), b + 1)
                settle(dve)
                ln(dve.tensor_copy(XS[:, :], xb))
                dve.tensor_tensor(A[:, :], acc[:, bass.ds(b * ACCW, D)], PS[1][:, 0:D], ALU.add
                                  ).then_inc(s_("n3_a"), 1)
                dve.wait_ge(s_("n3_rz"), b + 1)
                ln(dve.tensor_tensor(A[:, :], gru[:, 0:D], PS[5][:, 0:D], ALU.mult))
                dve.tensor_tensor(A[:, :], A[:, :], PS[4][:, 0:D], ALU.add).then_inc(s_("n3_t"), 1)
                dve.wait_ge(s_("n3_n"), b + 1)
                ln(dve.tensor_tensor(Y[:, :], xb, gru[:, 2 * D:3 * D], ALU.subtract))
                ln(dve.tensor_tensor(Y[:, :], Y[:, :], gru[:, D:2 * D], ALU.mult))
                ln(dve.tensor_tensor(Y[:, :], Y[:, :], gru[:, 2 * D:3 * D], ALU.add))
                ln(dve.tensor_tensor(Y[:, :], Y[:, :], xb, ALU.add))
                norm("n3", b, ln, XS[:, :]).then_inc(s_("n3_ln"), 1)
                dve.wait_ge(s_("n3_ln"), b + 1)
                settle(dve)
                ln(dve.tensor_copy(xb, XS[:, :]))
                dve.wait_ge(s_("n3_h1"), b + 1)
                dve.wait_ge(tabs, b * 16 + 16 * 3 * NB)
                dve.tensor_scalar(KV[:, 0:D1], PS[1][:, 0:D1], dinv[:, bass.ds(b, 1)], None, ALU.mult
                                  ).then_inc(s_("n3_h"), 1)
                dve.wait_ge(s_("n3_h"), b + 1)
                settle(dve)
                dve.tensor_copy(Q[:, bass.ds(b * D, D1)], KV[:, 0:D1]).then_inc(s_("n3_hs"), 1)
                ln.end()
            link2(dve.memset(acc[:, :], 0.0))
            sums(pc1)
            dve.wait_ge(pc1.added, T + PR)

            def gcn(name, b, ln, w, boff, last_sem, at):
                ln(dve.tensor_tensor(A[:, 0:w], acc[:, bass.ds(b * ACCW, w)], Q[:, bass.ds(b * D, w)], ALU.add))
                ln(dve.scalar_tensor_tensor(A[:, 0:w], A[:, 0:w], dinv[:, bass.ds(b, 1)],
                                            b12[:, boff:boff + w], ALU.mult, ALU.add))
                dve.tensor_scalar(A[:, 0:w], A[:, 0:w], 0.0, None, ALU.max).then_inc(s_(name + "_a"), 1)

            dve.wait_ge(tabs, 16 * 4 * NB)
            dve.wait_ge(s_("n3_hs"), NB)
            with dve.Fori(0, NB) as b:
                ln = Link(dve, s_("n4_link"), 0, b, 2)
                gcn("n4", b, ln, D1, 0, None, None)
                dve.wait_ge(s_("n4_h2"), b + 1)
                dve.wait_ge(tabs, b * 16 + 16 * 4 * NB)
                dve.tensor_scalar(KV[:, 0:D2], PS[1][:, 0:D2], dinv[:, bass.ds(b, 1)], None, ALU.mult
                                  ).then_inc(s_("n4_h"), 1)
                dve.wait_ge(s_("n4_h"), b + 1)
                settle(dve)
                dve.tensor_copy(Q[:, bass.ds(b * D, D2)], KV[:, 0:D2]).then_inc(s_("n4_hs"), 1)
                ln.end()
            link2(dve.memset(acc[:, :], 0.0))
            sums(pc2)
            dve.wait_ge(pc2.added, T + PR)
            dve.wait_ge(tabs, 16 * 5 * NB)
            dve.wait_ge(s_("n4_hs"), NB)
            with dve.Fori(0, NB) as b:
                ln = Link(dve, s_("n5_link"), 0, b, 6)
                gcn("n5", b, ln, D2, D1, None, None)
                dve.wait_ge(s_("n5_f2"), b + 1)
                ln(dve.tensor_tensor(Y[:, :], X[:, bass.ds(b * D, D)], PS[3][:, 0:D], ALU.add))
                ln(norm("n5", b, ln, X[:, bass.ds(b * D, D)]))
                ln.end()
            dve.sem_inc(s_("n5_done"), 1)


_INS = ['x', 'src', 'dst', 'edge_attr_8', 'edge_type_16', 'edge_weight', 'L0_gnn_W', 'L0_gnn_b', 'L1_gnn_Wq',
        'L1_gnn_Wk', 'L1_gnn_Wv', 'L1_gnn_Wo', 'L2_gnn_relvectors', 'L2_gnn_w_ih', 'L2_gnn_w_hh', 'L2_gnn_b_ih',
        'L2_gnn_b_hh', 'L3_gnn_W1', 'L3_gnn_b1', 'L3_gnn_W2', 'L3_gnn_b2', 'L3_gnn_fc1_w', 'L3_gnn_fc1_b',
        'L3_gnn_fc2_w', 'L3_gnn_fc2_b']


def kernel(**inputs):
    import numpy as _np
    import concourse.bacc as _bacc
    from concourse import mybir as _mybir
    from concourse.bass_utils import run_bass_kernel_spmd as _run

    nc = _bacc.Bacc("TRN2", target_bir_lowering=False, num_devices=1)
    arrays, args = {}, []
    for name in _INS:
        a = _np.ascontiguousarray(inputs[name])
        arrays[f"in_{name}_dram"] = a
        args.append(nc.dram_tensor(f"in_{name}_dram", a.shape, _mybir.dt.from_np(a.dtype), kind="ExternalInput").ap())
    out = nc.dram_tensor("out_0_dram", tuple(inputs['x'].shape), _mybir.dt.float32, kind="ExternalOutput").ap()
    gnn_kernel(nc, *args, out)
    r = _run(nc, [arrays], core_ids=[0])
    return r.results[0]["out_0_dram"]
```

```python
from contextlib import ExitStack

import concourse.bass as bass
from concourse import mybir

F32 = mybir.dt.float32
I32 = mybir.dt.int32
ALU = mybir.AluOpType
ACT = mybir.ActivationFunctionType
AX = mybir.AxisListType

P = 128
EPS = 1e-5
BIG = float(2**100)
RECW = 13
R_SRC, R_DST, R_TYPE, R_W, R_POS, R_BIAS = 0, 1, 2, 3, 4, 5
U = 8
GR = 16
PR = 4
WIN = 4
AHEAD = WIN * U
GRP = 16


class Link:

    def __init__(self, eng, sem, done=0, turn=None, per_turn=0):
        self.eng, self.sem, self.done, self.turn, self.per_turn, self.n = eng, sem, done, turn, per_turn, 0

    def __call__(self, ins):
        self.n += 1
        ins.then_inc(self.sem, 1)
        at = self.done + self.n
        if self.turn is not None:
            at = self.turn * self.per_turn + at
        self.eng.wait_ge(self.sem, at)

    def end(self):
        assert self.turn is None or self.n == self.per_turn, (self.n, self.per_turn)


class Step:

    def __init__(self, base, off):
        self.base, self.off = base, off

    def __mul__(self, k):
        return Step(self.base * k, self.off * k)

    def __add__(self, k):
        return self.base + (self.off + k)

    def __sub__(self, k):
        return self + -k


def ds(start, n):
    return bass.ds(start.base + start.off if isinstance(start, Step) else start, n)


def column(ap, t, width=1, first=0, n=1):
    if isinstance(t, int):
        return ap[:, t * width + first:t * width + first + n]
    return ap[:, t.off * width + first:][:, bass.ds(t.base * width, n)]


def staged(eng, steps, size, *stages, tail=0):
    most = max(lead for lead, _ in stages)
    turns = (steps - most) // size - tail

    def peeled(begin, end):
        for t in range(begin, end):
            for lead, stage in stages:
                if 0 <= t + lead < steps:
                    stage(t + lead, (t + lead) % size, (t + lead) // size)

    peeled(-most, 0)
    with eng.Fori(0, turns) as i:
        for u in range(size):
            for lead, stage in stages:
                v = u + lead
                stage(Step(i * size, v), v % size, Step(i, v // size))
    peeled(turns * size, steps)


def gnn_kernel(nc, x, src, dst, edge_attr, edge_type, edge_weight, w0, b0, wq, wk, wv, wo, rel,
               w_ih, w_hh, b_ih, b_hh, w1, b1, w2, b2, fc1_w, fc1_b, fc2_w, fc2_b, out, debug=None):
    N, D = x.shape
    E, H = edge_attr.shape
    NREL = rel.shape[0]
    D1, D2, DF = w1.shape[1], w2.shape[1], fc1_w.shape[1]
    DH = D // H
    NB = -(-N // P)
    NLAST = N - (NB - 1) * P
    EC = E // P
    EREST = E - EC * P
    T = -(-(-(-E // P) + NB - 1) // GRP) * GRP
    TURNS = T // U
    SCALE = float(DH) ** 0.5
    assert D == 256 and H * GRP == P and EREST < P

    tab_rec = nc.dram_tensor("tab_rec", (E + P, RECW), I32, kind="Internal").ap()
    MW = D + 1
    tab_m = nc.dram_tensor("tab_m", (E + P, MW), F32, kind="Internal").ap()
    tab_k = nc.dram_tensor("tab_k", (NB * P, D), F32, kind="Internal").ap()
    tab_v = nc.dram_tensor("tab_v", (NB * P, D), F32, kind="Internal").ap()
    tab_x = nc.dram_tensor("tab_x", (NB * P, D), F32, kind="Internal").ap()
    tab_h1 = nc.dram_tensor("tab_h1", (NB * P, D1), F32, kind="Internal").ap()
    tab_h2 = nc.dram_tensor("tab_h2", (NB * P, D2), F32, kind="Internal").ap()

    with ExitStack() as ctx:
        def sb(name, shape, dt=F32):
            return ctx.enter_context(nc.sbuf_tensor(name, shape, dt))

        def sem(name):
            return ctx.enter_context(nc.semaphore(name))

        X = sb("X", [P, NB * D])
        ACCW = 272
        acc = sb("acc", [P, NB * ACCW])
        Q = sb("Q", [P, NB * D])
        S = sb("S", [P, T * H])
        rec = sb("rec", [P, T * RECW], I32)
        recf = rec[:, :].bitcast(F32)
        rec3 = rec[:, :].rearrange("p (t c) -> p t c", c=RECW)
        recf3 = recf.rearrange("p (t c) -> p t c", c=RECW)
        NWT = 10 + 2 * (3 * D // P)
        WT = sb("WT", [P, 2, NWT * P])
        W1 = sb("W1", [P, 2, D1])
        W2 = sb("W2", [P, D2])
        FC1 = sb("FC1", [D2, DF])
        FC2 = sb("FC2", [P, D])
        REL = sb("REL", [NREL, D])
        BO = {"ih": 0, "hh": 0, "b0": 0, "fc2": D, "fc1": 2 * D, "b1": 2 * D + DF, "b2": 0}
        BP = {"ih": 0, "hh": 1, "b0": 2, "fc2": 2, "fc1": 2, "b1": 2, "b2": 3}
        assert 2 * D + DF + D1 == 3 * D
        brow = sb("brow", [4, 3 * D])
        pick = sb("pick", [4, 4 * P])
        b12 = sb("b12", [P, D1 + D2])
        wnat = Q[:, 0:NWT * D].rearrange("p (r n) -> p r n", n=D)
        G = sb("G", [P, GR, D + NREL])
        oh = sb("oh", [P, U, P])
        ohT = sb("ohT", [P, 4, P])
        workf = sb("work", [P, 4 * (D + H)])
        work = workf[:, :].rearrange("p (s n) -> p s n", s=4)
        idx = sb("idx", [P, WIN, U], I32)
        srci = sb("srci", [P, T + U], I32)
        posi = sb("posi", [P, T + U], I32)
        gru = sb("gru", [P, 4 * D])
        prod = gru[:, :].rearrange("p (s n) -> p s n", s=4)
        small_t = gru[:, 0:T]
        sg_row = gru[0:1, T:2 * T]
        epsb = sb("epsb", [P, 1])
        local = sb("local", [P, U])
        ident = sb("ident", [P, P])
        ones = sb("ones", [P, P])
        iota_i = workf[:, 0:512].bitcast(I32)
        iota_f = sb("iota_f", [P, 512])
        dstl = sb("dstl", [P, T])
        bs_row = [sb(f"bs_row{k}", [1, T], I32) for k in range(2)]
        as_row = [sb(f"as_row{k}", [1, T], I32) for k in range(2)]
        offs = sb("offs", [P, T])
        cnt = sb("cnt", [P, NB])
        cntn = [sb(f"cntn{k}", [P, NB]) for k in range(2)]
        place = sb("place", [P, NB])
        triP = sb("triP", [P, P])
        small = sb("small", [P, 16])
        smalli = sb("smalli", [P, 4], I32)
        tri = sb("tri", [NB, NB])
        past = workf[0:NB, 512:512 + T]
        top = Q[:, 0:T * H]
        dinv = sb("dinv", [P, NB])
        A = sb("A", [P, D])
        AT = sb("AT", [P, 2, P])
        XS = sb("XS", [P, D])
        XT = sb("XT", [P, 2, P])
        Y = sb("Y", [P, D])
        KV = sb("KV", [P, 2 * D])
        off = sb("off", [P, 4, 4])
        XT2 = sb("XT2", [P, 2, P])
        XI = work[:, 0, 0:D]
        TG = work[:, 1, 0:D]
        cn = work[:, 2, 0:NREL]
        cT = work[0:NREL, 2, P:2 * P]
        stats = sb("stats", [P, 8])
        mv = sb("mv", [P, 4])
        sg = sb("sg", [P, P])
        dg = sb("dg", [P, P])
        sT = sb("sT", [P, P])
        dT = sb("dT", [P, P + 2])
        fl = sb("fl", [P, P])
        la = sb("la", [P, P])
        ms = sb("ms", [P, P])
        mrow = sb("mrow", [P, 2, GRP, H + 1])
        padr = sb("padr", [P, RECW], I32)
        rest = acc[:, (EC + 1) * RECW:]
        recs = acc[:, 0:(EC + 1) * RECW].bitcast(I32).rearrange("p (t c) -> p t c", c=RECW)
        recsf = acc[:, 0:(EC + 1) * RECW].rearrange("p (t c) -> p t c", c=RECW)
        in_src = S[:, 0:EC + 1].bitcast(I32)
        in_dst = S[:, EC + 1:2 * (EC + 1)].bitcast(I32)
        in_typ = S[:, 2 * (EC + 1):3 * (EC + 1)].bitcast(I32)
        in_w = S[:, 3 * (EC + 1):4 * (EC + 1)]
        in_att = rec[:, 0:(EC + 1) * H].bitcast(F32)
        junk = S[:, 4 * (EC + 1):5 * (EC + 1)]
        tile_of = S[:, 5 * (EC + 1):6 * (EC + 1)]
        pos = S[:, 6 * (EC + 1):7 * (EC + 1)]
        run_to = rest[:, 0:EC + 1]
        in_it = rest[:, EC + 1:2 * (EC + 1)].bitcast(I32)
        ones_t = rest[:, 2 * (EC + 1):3 * (EC + 1)]

        PS = [ctx.enter_context(nc.psum_tensor(f"PS{i}", [P, 512], F32)) for i in range(8)]

        block_sems = {}

        def s_(name):
            if name not in block_sems:
                block_sems[name] = sem(name)
            return block_sems[name]

        ld_w, ld_x, ld_e = s_("ld_w"), s_("ld_x"), s_("ld_e")
        blank, consts = s_("blank"), s_("consts")
        wt_t, wt_c = s_("wt_t"), s_("wt_c")
        recs_done, rec_out, rec_in = s_("recs_done"), s_("rec_out"), s_("rec_in")
        v_set, pe_set = s_("v_set"), s_("pe_set")
        tabs = s_("tabs")
        GROUPS = T // GRP
        assert GROUPS % 2 == 0
        passed = sem("passed")
        block = ctx.enter_context(nc.Block())

        def rows(ap, n):
            return ap.rearrange("(a n) -> a n", a=1)

        class Pass:

            def __init__(self, name, table, width):
                self.name, self.table, self.w, self.ring = name, table, width, GR
                self.rows = ROWS
                self.used = sem(name + "_used")
                self.oh = sem(name + "_oh") if name not in ("keys", "vals") else None
                self.added = sem(name + "_added") if name != "keys" else None

        NORMS = ["n1", "n2", "n3", "n5"]
        ROWS = [sem(f"rows{u}") for u in range(GR)]
        IDX = [sem(f"idx{w}") for w in range(WIN)]
        pm = Pass("send", tab_m, MW)
        p0 = Pass("take", tab_m, D)
        pk = Pass("keys", tab_k, D)
        pv = Pass("vals", tab_v, D)
        p2 = Pass("msgs", tab_x, D)
        pc1 = Pass("gcn1", tab_h1, D1)
        pc2 = Pass("gcn2", tab_h2, D2)
        ORDER = [pm, pk, pv, p2, pc1, pc2]
        for n, p in enumerate(ORDER):
            p.base = 16 * (T // GR) * n
            p.wins = [16 * (T // AHEAD * n + (n > 0 and w == 0)) for w in range(WIN)]
        p0.ring, p0.rows, p0.base = U, [sem(f"taken{u}") for u in range(U)], 0

        def wait_old(eng, sem_, count):
            if not isinstance(count, int) or count > 0:
                eng.wait_ge(sem_, count + 0)

        def settle(eng):
            eng.sem_inc(passed, 1)

        @block.gpsimd
        def _(pool):
            pool.memset(ident[:, :], 0.0).then_inc(blank, 1)
            pool.memset(tri[:, :], 1.0).then_inc(blank, 1)
            pool.memset(triP[:, :], 1.0).then_inc(blank, 1)
            pool.memset(pick[:, :], 0.0).then_inc(blank, 1)
            pool.memset(ones[:, :], 1.0).then_inc(consts, 1)
            pool.iota(iota_i, [[1, 512]], base=0, channel_multiplier=0).then_inc(blank, 1)
            pool.wait_ge(blank, 5)
            pool.affine_select(out=ident[:, :], in_=ident[:, :], compare_op=ALU.not_equal, fill=1.0, base=0,
                               pattern=[[-1, P]], channel_multiplier=1).then_inc(consts, 1)
            pool.affine_select(out=tri[:, :], in_=tri[:, :], compare_op=ALU.is_ge, fill=0.0, base=0,
                               pattern=[[1, NB]], channel_multiplier=-1).then_inc(consts, 1)
            pool.tensor_copy(iota_f[:, :], iota_i).then_inc(consts, 1)

            pool.affine_select(out=pick[:, :], in_=pick[:, :], compare_op=ALU.not_equal, fill=1.0, base=0,
                               pattern=[[-1, 4], [0, P]], channel_multiplier=1).then_inc(consts, 1)
            pool.affine_select(out=triP[:, :], in_=triP[:, :], compare_op=ALU.is_gt, fill=0.0, base=0,
                               pattern=[[1, P]], channel_multiplier=-1).then_inc(consts, 1)

            with pool.Fori(0, T // AHEAD) as i:
                for u in range(AHEAD):
                    if u % U == 0:
                        pool.wait_ge(IDX[u // U], i * 16 + (pm.wins[u // U] + 16))
                    pool.wait_ge(pm.added, i * AHEAD + (u + 1 + PR))
                    pool.wait_ge(pm.oh, i * AHEAD + (u + 1))
                    settle(pool)
                    pool.indirect_dma_start(tab_m[0:E, :],
                                            bass.IndirectOffsetOnAxis(ap=idx[:, u // U, u % U:u % U + 1], axis=0),
                                            G[:, u % GR, :MW], None, bounds_check=E - 1, oob_is_err=False
                                            ).then_inc(pm.rows[u % GR], 16)

            def onehot_src(t, r, turn):
                pool.wait_ge(s_("local"), t + 1)
                pool.wait_ge(p0.used, t + (AHEAD + 1 - U))
                settle(pool)
                pool.tensor_scalar(oh[:, r, :], iota_f[:, 0:P], local[:, r:r + 1], None, ALU.is_equal
                                   ).then_inc(p0.oh, 1)

            pool.wait_ge(v_set, 3)
            staged(pool, T, U, (0, onehot_src))

            def gathers(p, ready, count):
                pool.wait_ge(ready, count)
                with pool.Fori(0, T // AHEAD) as i:
                    for u in range(AHEAD):
                        if u % U == 0:
                            pool.wait_ge(IDX[u // U], i * 16 + (p.wins[u // U] + 16))
                        pool.wait_ge(p.used, i * AHEAD + (u + 1 + AHEAD - GR))
                        settle(pool)
                        pool.indirect_dma_start(G[:, u % GR, :p.w], None, p.table,
                                                bass.IndirectOffsetOnAxis(ap=idx[:, u // U, u % U:u % U + 1], axis=0)
                                                ).then_inc(p.rows[u % GR], 16)

            gathers(pk, tabs, 16 * 2 * NB)
            gathers(pv, tabs, 16 * 2 * NB)
            gathers(p2, tabs, 16 * 3 * NB)
            gathers(pc1, tabs, 16 * 4 * NB)
            gathers(pc2, tabs, 16 * 5 * NB)

        def node_tile(eng, k, t):
            return eng.value_load(column(bs_row[k], t)).with_bounds(min_val=0, max_val=NB - 1)

        def first_edge(eng, k, t):
            return eng.value_load(column(as_row[k], t)).with_bounds(min_val=0, max_val=E)

        def rec_loads(eng, begin, end):
            with eng.Fori(begin, end) as i:
                for u in range(U):
                    t = Step(i * U, u)
                    first = first_edge(eng, 0, t)
                    eng.dma_start(column(rec, t, RECW, 0, RECW), tab_rec[bass.ds(first, P), :]).then_inc(rec_in, 16)

        @block.sync
        def _(sp):
            sp.wait_ge(v_set, 1)
            nx = (NB - 1) * P
            sp.dma_start(X[:, 0:(NB - 1) * D].rearrange("p (b n) -> p b n", n=D),
                         x[0:nx, :].rearrange("(b p) n -> p b n", p=P)).then_inc(ld_x, 16)
            sp.dma_start(X[0:NLAST, (NB - 1) * D:NB * D], x[nx:N, :]).then_inc(ld_x, 16)
            for to, of in ((in_dst, dst), (in_src, src), (in_typ, edge_type), (in_w, edge_weight)):
                sp.dma_start(to[:, 0:EC], of[0:EC * P].rearrange("(p t) -> p t", t=EC)).then_inc(ld_e, 16)
                sp.dma_start(to[0:EREST, EC:EC + 1],
                             of[EC * P:E].rearrange("(p t) -> p t", t=1)).then_inc(ld_e, 16)
            sp.dma_start(in_att[:, 0:EC * H], edge_attr[0:EC * P, :].rearrange("(p t) h -> p (t h)", t=EC)
                         ).then_inc(ld_e, 16)
            sp.dma_start(in_att[0:EREST, EC * H:(EC + 1) * H], edge_attr[EC * P:E, :]).then_inc(ld_e, 16)
            sp.wait_ge(recs_done, 2)
            sp.dma_start(tab_rec[0:EC * P, :].rearrange("(p t) c -> p t c", t=EC), recs[:, 0:EC, :]
                         ).then_inc(rec_out, 16)
            sp.dma_start(tab_rec[EC * P:E, :], recs[0:EREST, EC, :]).then_inc(rec_out, 16)
            sp.dma_start(tab_rec[E:E + P, :], padr[:, :]).then_inc(rec_out, 16)
            sp.wait_ge(s_("pad_m"), 1)
            sp.dma_start(tab_m[E:E + P, :], G[:, 0, 0:MW]).then_inc(rec_out, 16)
            sp.wait_ge(rec_out, 64)
            sp.wait_ge(v_set, 3)
            rec_loads(sp, 0, TURNS // 2)

            def window(p, of, i, w):
                sp.wait_ge(p.used, i * AHEAD + (U * w + U))
                sp.dma_start(idx[:, w, :], of[:, ds(i * AHEAD + U * w, U)]).then_inc(IDX[w], 16)

            def windows(p):
                with sp.Fori(0, T // AHEAD) as i:
                    for w in range(WIN):
                        window(p, srci, i, w)

            sp.wait_ge(s_("places"), 1)
            sp.sem_inc(pm.used, AHEAD)
            window(pm, posi, 0, 0)
            with sp.Fori(0, T // AHEAD) as i:
                for w in range(WIN):
                    window(pm, posi, i + (w + 1) // WIN, (w + 1) % WIN)
                    for u in range(w * U, w * U + U):
                        sp.wait_ge(pm.rows[u % GR], i * (16 * AHEAD // GR) + (16 * (u // GR) + 16))
                        sp.sem_inc(pm.used, 1)
            with sp.Fori(0, TURNS) as i:
                for u in range(0, U, 2):
                    first = first_edge(sp, 1, Step(i * U, u))
                    sp.wait_ge(p0.used, i * U + (u + 1 + AHEAD - U))
                    sp.dma_start(G[:, u, 0:MW], tab_m[bass.ds(first, P), :]).then_inc(p0.rows[u], 16)

            def store(ready, table, of):
                with sp.Fori(0, NB) as b:
                    sp.wait_ge(ready, b + 1)
                    for tb, o in zip(table, of):
                        sp.dma_start(tb[ds(b * P, P), :], o).then_inc(tabs, 16)

            store(s_("n1_kv"), (tab_k, tab_v), (KV[:, 0:D], KV[:, D:2 * D]))
            windows(pk)
            windows(pv)
            store(s_("n2_x"), (tab_x,), (XS[:, :],))
            windows(p2)
            store(s_("n3_h"), (tab_h1,), (KV[:, 0:D1],))
            windows(pc1)
            store(s_("n4_h"), (tab_h2,), (KV[:, 0:D2],))
            windows(pc2)
            sp.wait_ge(s_("n5_done"), 1)
            sp.dma_start(out[0:nx, :].rearrange("(b p) n -> p b n", p=P),
                         X[:, 0:(NB - 1) * D].rearrange("p (b n) -> p b n", n=D)).then_inc(s_("out"), 16)
            sp.dma_start(out[nx:N, :], X[0:NLAST, (NB - 1) * D:NB * D]).then_inc(s_("out"), 16)
            sp.wait_ge(s_("out"), 32)

        WMATS = [(w0, D), (wq, D), (wk, D), (wv, D), (wo, D), (w_ih, 3 * D), (w_hh, 3 * D)]
        WCOL = {}
        o = 0
        for n, (_, r) in zip(("w0", "wq", "wk", "wv", "wo", "ih", "hh"), WMATS):
            WCOL[n] = o
            o += r

        @block.scalar
        def _(act):
            r = 0
            for w, n in WMATS:
                act.dma_start(wnat[:, r:r + n // P, :], w.rearrange("(r p) n -> p r n", p=P)).then_inc(ld_w, 16)
                r += n // P
            act.dma_start(W1[:, :, :], w1.rearrange("(c p) n -> p c n", p=P)).then_inc(ld_w, 16)
            act.dma_start(W2[:, :], w2).then_inc(ld_w, 16)
            act.dma_start(FC1[:, :], fc1_w).then_inc(ld_w, 16)
            act.dma_start(FC2[:, :], fc2_w).then_inc(ld_w, 16)
            act.dma_start(REL[:, :], rel).then_inc(ld_w, 16)
            for n, b in (("b0", b0), ("ih", b_ih), ("hh", b_hh), ("fc1", fc1_b), ("fc2", fc2_b), ("b1", b1), ("b2", b2)):
                act.dma_start(brow[BP[n]:BP[n] + 1, BO[n]:BO[n] + b.shape[0]], rows(b, b.shape[0])).then_inc(ld_w, 16)
            for r in range(NWT):
                act.wait_ge(wt_t, r + 1)
                act.copy(WT[:, :, r * P:(r + 1) * P],
                         PS[r % 4][:, 0:2 * P].rearrange("p (c n) -> p c n", c=2)).then_inc(wt_c, 1)
            act.wait_ge(wt_t, NWT + 1)
            act.copy(b12[:, :], PS[4][:, 0:D1 + D2]).then_inc(wt_c, 1)

            act.wait_ge(rec_out, 64)
            act.wait_ge(v_set, 3)
            rec_loads(act, TURNS // 2, TURNS)

            def norm_std(name):
                def stage(b, r, turn):
                    act.wait_ge(s_("var"), b + (NORMS.index(name) * NB + 1))
                    act.activation(mv[:, 2:3], mv[:, 1:2], ACT.Sqrt, bias=epsb[:, 0:1]).then_inc(s_("std"), 1)
                return stage

            def turned(name):
                def stage(t, r, turn):
                    act.wait_ge(s_(name + "_ohT"), t + 1)
                    act.wait_ge(s_(name + "_sel"), t + (1 + U - 4))
                    act.copy(ohT[:, r % 4, :], PS[r % 2][:, 0:P]).then_inc(s_(name + "_ohTc"), 1)
                return stage

            act.wait_ge(s_("places"), 1)
            act.sem_inc(s_("send_ohTc"), 2)
            staged(act, T, U, (0, turned("send")))
            def take_load(t, r, turn):
                if r % 2:
                    first = first_edge(act, 1, t)
                    act.wait_ge(p0.used, t + (1 + AHEAD - U))
                    act.dma_start(G[:, r, 0:MW], tab_m[bass.ds(first, P), :]).then_inc(p0.rows[r], 16)

            def local_nodes(t, r, turn):
                act.wait_ge(p0.rows[r], turn * 16 + (p0.base + 16))
                act.wait_ge(p0.used, t + (1 + AHEAD - U))
                act.activation(local[:, r:r + 1], G[:, r, D:MW], ACT.Identity, bias=column(offs, t)
                               ).then_inc(s_("local"), 1)

            act.wait_ge(pm.used, T + AHEAD)
            staged(act, T, U, (5, take_load), (0, local_nodes))
            def n1_sums(b, r, turn):
                settle(act)
                act.copy(A[:, :], acc[:, ds(b * ACCW, D)]).then_inc(s_("n1_a"), 1)

            def n1_sums_turned(b, r, turn):
                act.wait_ge(s_("n1_aT"), b + 1)
                wait_old(act, s_("n1_h"), b)
                act.copy(AT[:, :, :], PS[0][:, 0:D].rearrange("p (c n) -> p c n", c=2)).then_inc(s_("n1_aTc"), 1)

            def n1_rows_turned(b, r, turn):
                act.wait_ge(s_("n1_xT"), b + 1)
                wait_old(act, s_("n1_qkv"), b)
                act.copy(XT[:, :, :], PS[2][:, 0:D].rearrange("p (c n) -> p c n", c=2)).then_inc(s_("n1_xTc"), 1)

            def n1_out(b, r, turn):
                act.wait_ge(s_("n1_qkv"), b + 1)
                act.mul(Q[:, ds(b * D, D)], PS[3][:, 0:D], SCALE).then_inc(s_("n1_q"), 1)
                wait_old(act, tabs, b * 32)
                act.copy(KV[:, :], PS[4][:, 0:2 * D]).then_inc(s_("n1_kv"), 1)

            act.wait_ge(s_("n1_free"), 1)
            staged(act, NB, 2, (2, norm_std("n1")), (1, n1_out), (4, n1_sums_turned), (5, n1_sums),
                   (2, n1_rows_turned))
            act.sem_inc(s_("keys_ohTc"), 2)
            staged(act, T, U, (0, turned("keys")))
            def scores_turned(g):
                act.wait_ge(s_("m_sg"), g + 1)
                act.copy(S[:, ds(g * P, P)], sg[:, :]).then_inc(s_("m_Tc"), 1)
                act.wait_ge(s_("m_T1"), g + 1)
                if not isinstance(g, int) or g > 0:
                    act.wait_ge(s_("m_ms"), g + 0)
                act.copy(sT[:, :], PS[0][:, 0:P]).then_inc(s_("m_Tc"), 1)
                act.copy(dT[:, 1:P + 1], PS[1][:, 0:P]).then_inc(s_("m_Tc"), 1)

            def maxima_turned(g, slot):
                act.wait_ge(s_("m_T2"), g + 1)
                act.copy(mrow[:, slot, :, 0:H], PS[2][:, 0:P].rearrange("p (t h) -> p t h", h=H)
                         ).then_inc(s_("m_row"), 1)
                act.copy(mrow[:, slot, :, H:H + 1],
                         PS[3][:, 0:P].rearrange("p (t h) -> p t h", h=H)[:, :, 0:1]).then_inc(s_("m_row"), 1)

            def m_act(c, r, turn):
                g = turn * 2 + r // 4
                if r % 4 == 2 and not (isinstance(g, int) and g + 1 >= GROUPS):
                    maxima_turned(g + 1, (r // 4 + 1) % 2)
                if r % 4 == 3 and not (isinstance(g, int) and g + 2 >= GROUPS):
                    scores_turned(g + 2)
                act.wait_ge(s_("m_mm"), c + 3)
                act.wait_ge(s_("m_added"), c + 1)
                act.activation(off[:, r % 4, :], PS[4 + r % PR][:, 0:4 * (H + 1)]
                               .rearrange("p (t h) -> p t h", h=H + 1)[:, :, H], ACT.Copy, bias=-BIG, scale=BIG
                               ).then_inc(s_("m_off"), 1)

            scores_turned(0)
            maxima_turned(0, 0)
            scores_turned(1)
            staged(act, T // 4, 8, (0, m_act), tail=1)
            def exponentials(t, r, turn):
                act.wait_ge(s_("vals_d"), t + 3)
                act.activation(work[:, r % 4, D:D + H], work[:, r % 4, D:D + H], ACT.Exp
                               ).then_inc(s_("vals_e"), 1)

            act.sem_inc(s_("vals_ohTc"), 2)
            staged(act, T, U, (1, turned("vals")), (0, exponentials))
            def n2_turned(b, r, turn):
                act.wait_ge(s_("n2_aT"), b + 1)
                wait_old(act, s_("n2_h"), b)
                act.copy(AT[:, :, :], PS[0][:, 0:D].rearrange("p (c n) -> p c n", c=2)).then_inc(s_("n2_aTc"), 1)

            staged(act, NB, 2, (1, norm_std("n2")), (3, n2_turned))
            act.wait_ge(s_("n3_deg"), 1)
            act.activation(dinv[:, :], dinv[:, :], ACT.Sqrt).then_inc(s_("n3_degs"), 1)
            def n3_counts(b, r, turn):
                settle(act)
                act.copy(cn, acc[:, ds(b * ACCW + D, NREL)]).then_inc(s_("n3_c"), 1)

            def n3_counts_turned(b, r, turn):
                act.wait_ge(s_("n3_cT"), b + 1)
                wait_old(act, s_("n3_aT"), b)
                act.copy(cT, PS[0][0:NREL, 0:P]).then_inc(s_("n3_cTc"), 1)

            def n3_in(b, r, turn):
                settle(act)
                act.copy(A[:, :], acc[:, ds(b * ACCW, D)]).then_inc(s_("n3_a"), 1)
                act.copy(XI, X[:, ds(b * D, D)]).then_inc(s_("n3_a"), 1)

            def n3_in_turned(b, r, turn):
                act.wait_ge(s_("n3_aT"), b + 1)
                wait_old(act, s_("n3_g"), b)
                act.copy(AT[:, :, :], PS[1][:, 0:D].rearrange("p (c n) -> p c n", c=2)).then_inc(s_("n3_aTc"), 1)
                act.copy(XT[:, :, :], PS[1][:, D:2 * D].rearrange("p (c n) -> p c n", c=2)).then_inc(s_("n3_aTc"), 1)

            def n3_gates(b, r, turn):
                act.wait_ge(s_("n3_g"), b + 1)
                wait_old(act, s_("n3_ln"), b)
                act.activation(gru[:, 0:2 * D], PS[(3, 6)[r]][:, 0:2 * D], ACT.Sigmoid).then_inc(s_("n3_rz"), 1)
                act.wait_ge(s_("n3_t"), b + 1)
                act.activation(gru[:, 2 * D:3 * D], TG, ACT.Tanh).then_inc(s_("n3_n"), 1)
                norm_std("n3")(b, r, turn)

            def n3_rows_turned(b, r, turn):
                act.wait_ge(s_("n3_xT"), b + 1)
                wait_old(act, s_("n3_h1"), b)
                act.copy(XT2[:, :, :], PS[5][:, 0:D].rearrange("p (c n) -> p c n", c=2)).then_inc(s_("n3_xTc"), 1)

            staged(act, NB, 2, (2, n3_gates), (5, n3_counts_turned), (6, n3_counts), (4, n3_in_turned), (5, n3_in),
                   (2, n3_rows_turned))
            with act.Fori(0, NB) as b:
                act.wait_ge(s_("n4_aT"), b + 1)
                act.copy(AT[:, 0, :], PS[0][:, 0:P]).then_inc(s_("n4_aTc"), 1)
            def n5_a_turned(b, r, turn):
                act.wait_ge(s_("n5_aT"), b + 1)
                wait_old(act, s_("n5_f1"), b)
                act.copy(AT[0:D2, 0, :], PS[0][0:D2, 0:P]).then_inc(s_("n5_aTc"), 1)

            def n5_fc1_out(b, r, turn):
                act.wait_ge(s_("n5_f1"), b + 1)
                wait_old(act, s_("n5_fT"), b)
                act.copy(KV[:, 0:DF], PS[1][:, 0:DF]).then_inc(s_("n5_f1c"), 1)

            def n5_fc1_turned(b, r, turn):
                act.wait_ge(s_("n5_fT"), b + 1)
                wait_old(act, s_("n5_f2"), b)
                act.copy(XT[:, 0, :], PS[2][:, 0:P]).then_inc(s_("n5_fTc"), 1)

            staged(act, NB, 2, (2, norm_std("n5")), (5, n5_a_turned), (4, n5_fc1_out), (3, n5_fc1_turned))

        @block.tensor
        def _(pe):
            pe.wait_ge(consts, 6)
            pe.wait_ge(ld_w, 16 * 19)
            for r in range(NWT):
                if r >= 4:
                    pe.wait_ge(wt_c, r - 3)
                pe.transpose(PS[r % 4][:, 0:P], wnat[:, r, 0:P], ident[:, :])
                pe.transpose(PS[r % 4][:, P:2 * P], wnat[:, r, P:2 * P], ident[:, :]).then_inc(wt_t, 1)
            pe.matmul(PS[4][:, 0:D1], pick[0:3, 2 * P:3 * P], brow[0:3, BO["b1"]:BO["b1"] + D1],
                      start=True, stop=True)
            pe.matmul(PS[4][:, D1:D1 + D2], pick[0:4, 3 * P:4 * P], brow[0:4, 0:D2],
                      start=True, stop=True).then_inc(wt_t, 1)
            for k in range(2):
                pe.wait_ge(s_("v_cnt"), k + 1)
                pe.matmul(PS[5][0:NB, 0:1], cntn[k][:, :], ones[:, 0:1], start=True, stop=True).then_inc(pe_set, 1)
                pe.wait_ge(s_("v_nt"), 2 * k + 1)
                pe.matmul(PS[5][0:NB, 8:9], tri[:, :], small[0:NB, 1:2], start=True, stop=True).then_inc(pe_set, 1)
                pe.wait_ge(s_("v_nt"), 2 * k + 2)
                pe.wait_ge(wt_c, NWT + 1)
                pe.matmul(PS[6][0:1, 0:T], ones[0:NB, 0:1], past, start=True, stop=True)
                pe.matmul(PS[7][0:1, 0:T], small[0:NB, 2:3], past, start=True, stop=True)
                pe.matmul(PS[4][:, 0:T], ones[0:NB, :], past, start=True, stop=True).then_inc(pe_set, 1)
            pe.wait_ge(v_set, 3)
            pe.matmul(PS[4][:, 0:NB], triP[:, :], cntn[1][:, :], start=True, stop=True)
            pe.matmul(PS[5][:, 0:NB], ones[:, :], cntn[1][:, :], start=True, stop=True).then_inc(pe_set, 1)

            def bias(ps, name, n, off=0):
                k = BP[name]
                pe.matmul(ps, pick[0:k + 1, k * P:(k + 1) * P], brow[0:k + 1, BO[name] + off:BO[name] + off + n], start=True, stop=False)

            def times(ps, aT, name, off, n, start, stop=True):
                c0 = WCOL[name] + off
                for c in range(2):
                    last = pe.matmul(ps, aT[:, c, :], WT[:, c, c0:c0 + n],
                                     start=(start and c == 0), stop=(stop and c == 1))
                return last

            def turn2(ps, a):
                pe.transpose(ps[:, 0:P], a[:, 0:P], ident[:, :])
                return pe.transpose(ps[:, P:2 * P], a[:, P:2 * P], ident[:, :])

            def sums(p, types=False):
                def add(t, r, turn):
                    pe.wait_ge(p.oh, t * 2 + 2 if types else t + 1)
                    pe.wait_ge(p.rows[r], turn * 16 + (p.base + 16))
                    pe.wait_ge(p.added, t + 1)
                    w = p.w + (NREL if types else 0)
                    pe.matmul(PS[4 + r % PR][:, 0:w], oh[:, r % U, :], G[:, r, 0:w], start=True, stop=True
                              ).then_inc(p.used, 1)

                pe.sem_inc(p.used, AHEAD)
                staged(pe, T, p.ring, (0, add))

            def turns(name):
                def stage(t, r, turn):
                    pe.wait_ge(s_(name + "_1h"), t + 1)
                    pe.wait_ge(s_(name + "_ohTc"), t + 1)
                    pe.transpose(PS[r % 2][:, 0:P], oh[:, r, :], ident[:, :]).then_inc(s_(name + "_ohT"), 1)
                return stage

            def tile_at(t):
                return node_tile(pe, 0, t)

            def pick_rows(t, r, turn):
                tile = tile_at(t)
                pe.wait_ge(s_("send_ohTc"), t + 3)
                pe.wait_ge(pm.added, t + 1)
                pe.matmul(PS[4 + r % PR][:, 0:D], ohT[:, r % 4, :], X[:, ds(tile * D, D)],
                          start=True, stop=True).then_inc(s_("send_sel"), 1)

            pe.wait_ge(s_("places"), 1)
            pe.wait_ge(ld_x, 32)
            pe.sem_inc(s_("send_sel"), U)
            staged(pe, T, U, (1, turns("send")), (0, pick_rows))
            sums(p0)
            def n1_turn_sums(b, r, turn):
                pe.wait_ge(s_("n1_a"), b + 1)
                wait_old(pe, s_("n1_aTc"), b)
                turn2(PS[0], A).then_inc(s_("n1_aT"), 1)

            def n1_w0(b, r, turn):
                pe.wait_ge(s_("n1_aTc"), b + 1)
                wait_old(pe, s_("n1_y"), b - 1)
                ps = PS[(1, 5)[r]][:, 0:D]
                bias(ps, "b0", D)
                times(ps, AT, "w0", 0, D, False).then_inc(s_("n1_h"), 1)

            def n1_turn_rows(b, r, turn):
                pe.wait_ge(s_("n1_ln"), b + 1)
                wait_old(pe, s_("n1_xTc"), b)
                turn2(PS[2], XS).then_inc(s_("n1_xT"), 1)

            def n1_qkv(b, r, turn):
                pe.wait_ge(s_("n1_xTc"), b + 1)
                wait_old(pe, s_("n1_q"), b)
                wait_old(pe, s_("n1_kv"), b)
                times(PS[3][:, 0:D], XT, "wq", 0, D, True)
                times(PS[4][:, 0:D], XT, "wk", 0, D, True)
                times(PS[4][:, D:2 * D], XT, "wv", 0, D, True).then_inc(s_("n1_qkv"), 1)

            staged(pe, NB, 2, (1, n1_qkv), (3, n1_w0), (4, n1_turn_sums), (2, n1_turn_rows))

            pe.wait_ge(s_("n1_kv"), NB)
            def pick_queries(t, r, turn):
                tile = tile_at(t)
                pe.wait_ge(s_("keys_ohTc"), t + 3)
                pe.wait_ge(pk.used, t + (1 + AHEAD - PR))
                pe.matmul(PS[4 + r % PR][:, 0:D], ohT[:, r % 4, :], Q[:, ds(tile * D, D)],
                          start=True, stop=True).then_inc(s_("keys_sel"), 1)

            pe.sem_inc(s_("keys_sel"), U)
            staged(pe, T, U, (1, turns("keys")), (0, pick_queries))
            def turn_scores(g):
                pe.wait_ge(s_("m_sg"), g + 1)
                if not isinstance(g, int) or g > 0:
                    pe.wait_ge(s_("m_Tc"), g * 3)
                pe.transpose(PS[0][:, 0:P], sg[:, :], ident[:, :])
                pe.transpose(PS[1][:, 0:P], dg[:, :], ident[:, :]).then_inc(s_("m_T1"), 1)

            def turn_maxima(g):
                pe.wait_ge(s_("m_ms"), g + 1)
                if not isinstance(g, int) or g > 0:
                    pe.wait_ge(s_("m_row"), g * 2)
                pe.transpose(PS[2][:, 0:P], ms[:, :], ident[:, :])
                pe.transpose(PS[3][:, 0:P], la[:, :], ident[:, :]).then_inc(s_("m_T2"), 1)

            def m_pe(c, r, turn):
                g = turn * 2 + r // 4
                if r % 4 == 1 and not (isinstance(g, int) and g + 1 >= GROUPS):
                    turn_maxima(g + 1)
                if r % 4 == 3 and not (isinstance(g, int) and g + 2 >= GROUPS):
                    turn_scores(g + 2)
                if r % 4 == 0:
                    pe.wait_ge(s_("m_row"), g * 2 + 2)
                pe.wait_ge(s_("m_oh"), c + 1)
                pe.wait_ge(s_("m_added"), c + 1)
                for k in range(4):
                    last = pe.matmul(PS[4 + r % PR][:, k * (H + 1):(k + 1) * (H + 1)], oh[:, r % 2 * 4 + k, :],
                                     mrow[:, r // 4, r % 4 * 4 + k, :], start=True, stop=True)
                last.then_inc(s_("m_mm"), 1)

            turn_scores(0)
            turn_maxima(0)
            turn_scores(1)
            pe.sem_inc(s_("m_mm"), 2)
            staged(pe, T // 4, 8, (0, m_pe), tail=1)
            def pick_max(t, r, turn):
                pe.wait_ge(s_("vals_ohTc"), t + 3)
                pe.wait_ge(s_("vals_d"), t + 1)
                pe.matmul(PS[2 + r % 2][:, 0:H], ohT[:, r % 4, :], column(top, t, H, 0, H),
                          start=True, stop=True).then_inc(s_("vals_sel"), 1)

            def sum_values(t, r, turn):
                pe.wait_ge(s_("vals_vp"), t + 1)
                pe.wait_ge(pv.added, t + 1)
                pe.matmul(PS[4 + r % PR][:, 0:D + H], oh[:, r, :], work[:, r % 4, :],
                          start=True, stop=True).then_inc(pv.used, 1)

            pe.sem_inc(s_("vals_sel"), U)
            pe.sem_inc(pv.used, AHEAD)
            staged(pe, T, U, (3, turns("vals")), (2, pick_max), (0, sum_values))
            def n2_wo(b, r, turn):
                pe.wait_ge(s_("n2_aTc"), b + 1)
                wait_old(pe, s_("n2_y"), b - 1)
                times(PS[1 + r][:, 0:D], AT, "wo", 0, D, True).then_inc(s_("n2_h"), 1)

            def n2_turn(b, r, turn):
                pe.wait_ge(s_("n2_a"), b + 1)
                wait_old(pe, s_("n2_aTc"), b)
                turn2(PS[0], A).then_inc(s_("n2_aT"), 1)

            staged(pe, NB, 2, (2, n2_wo), (3, n2_turn))
            sums(p2, types=True)
            def n3_gates(b, r, turn):
                pe.wait_ge(s_("n3_aTc"), b * 2 + 2)
                wait_old(pe, s_("n3_n"), b - 1)
                rz, nn = PS[(3, 6)[r]], PS[(4, 7)[r]]
                pe.matmul(rz[:, 0:2 * D], ones[0:2, :], brow[0:2, 0:2 * D], start=True, stop=False)
                times(rz[:, 0:2 * D], AT, "ih", 0, 2 * D, False, stop=False)
                times(rz[:, 0:2 * D], XT, "hh", 0, 2 * D, False)
                bias(nn[:, 0:D], "ih", D, 2 * D)
                times(nn[:, 0:D], AT, "ih", 2 * D, D, False)
                bias(nn[:, D:2 * D], "hh", D, 2 * D)
                times(nn[:, D:2 * D], XT, "hh", 2 * D, D, False).then_inc(s_("n3_g"), 1)

            def n3_turn_counts(b, r, turn):
                pe.wait_ge(s_("n3_c"), b + 1)
                wait_old(pe, s_("n3_cTc"), b)
                pe.transpose(PS[0][0:NREL, 0:P], cn, ident[:, :]).then_inc(s_("n3_cT"), 1)

            def n3_turn_in(b, r, turn):
                pe.wait_ge(s_("n3_cTc"), b + 1)
                pe.wait_ge(s_("n3_a"), b * 2 + 2)
                wait_old(pe, s_("n3_aTc"), b * 2)
                for c in range(2):
                    pe.matmul(PS[1][:, c * P:(c + 1) * P], A[:, c * P:(c + 1) * P], ident[:, :],
                              start=True, stop=False)
                    pe.matmul(PS[1][:, c * P:(c + 1) * P], REL[:, c * P:(c + 1) * P], cT, start=False, stop=True)
                turn2(PS[1][:, D:2 * D], XI).then_inc(s_("n3_aT"), 1)

            def n3_turn_rows(b, r, turn):
                pe.wait_ge(s_("n3_ln"), b + 1)
                wait_old(pe, s_("n3_xTc"), b)
                turn2(PS[5], XS).then_inc(s_("n3_xT"), 1)

            def n3_w1(b, r, turn):
                pe.wait_ge(s_("n3_xTc"), b + 1)
                wait_old(pe, s_("n3_h"), b)
                for c in range(2):
                    last = pe.matmul(PS[2][:, 0:D1], XT2[:, c, :], W1[:, c, :],
                                     start=(c == 0), stop=(c == 1))
                last.then_inc(s_("n3_h1"), 1)

            pe.wait_ge(s_("n3_degs"), 1)
            staged(pe, NB, 2, (3, n3_gates), (5, n3_turn_counts), (4, n3_turn_in), (2, n3_turn_rows), (1, n3_w1))
            sums(pc1)
            with pe.Fori(0, NB) as b:
                pe.wait_ge(s_("n4_a"), b + 1)
                pe.transpose(PS[0][:, 0:P], A[:, 0:D1], ident[:, :]).then_inc(s_("n4_aT"), 1)
                pe.wait_ge(s_("n4_aTc"), b + 1)
                pe.matmul(PS[1][:, 0:D2], AT[:, 0, :], W2[:, :], start=True, stop=True).then_inc(s_("n4_h2"), 1)
            sums(pc2)
            def n5_turn_a(b, r, turn):
                pe.wait_ge(s_("n5_a"), b + 1)
                wait_old(pe, s_("n5_aTc"), b)
                settle(pe)
                pe.transpose(PS[0][0:D2, 0:P], A[:, 0:D2], ident[:, :]).then_inc(s_("n5_aT"), 1)

            def n5_fc1(b, r, turn):
                pe.wait_ge(s_("n5_aTc"), b + 1)
                wait_old(pe, s_("n5_f1c"), b)
                bias(PS[1][:, 0:DF], "fc1", DF)
                pe.matmul(PS[1][:, 0:DF], AT[0:D2, 0, :], FC1[:, :], start=False, stop=True).then_inc(s_("n5_f1"), 1)

            def n5_turn_fc1(b, r, turn):
                pe.wait_ge(s_("n5_f1c"), b + 1)
                wait_old(pe, s_("n5_fTc"), b)
                pe.transpose(PS[2][:, 0:P], KV[:, 0:DF], ident[:, :]).then_inc(s_("n5_fT"), 1)

            def n5_fc2(b, r, turn):
                pe.wait_ge(s_("n5_fTc"), b + 1)
                wait_old(pe, s_("n5_y"), b - 1)
                bias(PS[3 + r][:, 0:D], "fc2", D)
                pe.matmul(PS[3 + r][:, 0:D], XT[:, 0, :], FC2[:, :], start=False, stop=True).then_inc(s_("n5_f2"), 1)

            staged(pe, NB, 2, (2, n5_fc2), (3, n5_turn_fc1), (4, n5_fc1), (5, n5_turn_a))

        @block.vector
        def _(dve):
            lk = s_("v_link")
            link = Link(dve, lk)
            NOEDGE = 1 << 20
            link(dve.memset(in_dst[:, EC:EC + 1], NOEDGE))
            link(dve.memset(in_src[:, EC:EC + 1], NOEDGE))
            link(dve.memset(in_typ[:, EC:EC + 1], 0))
            link(dve.memset(in_w[:, EC:EC + 1], 0.0))
            link(dve.memset(in_att[:, EC * H:(EC + 1) * H], 0.0))
            link(dve.memset(padr[:, :], 0))
            link(dve.memset(padr[:, R_DST:R_DST + 1].bitcast(F32), float(NOEDGE)))
            link(dve.memset(epsb[:, :], EPS))
            link(dve.memset(dT[:, :], -1.0))
            dve.memset(X[:, (NB - 1) * D:NB * D], 0.0).then_inc(v_set, 1)
            dve.wait_ge(ld_e, 160)
            link(dve.tensor_copy(recs[:, :, R_SRC], in_src))
            link(dve.tensor_copy(recsf[:, :, R_DST], in_dst))
            link(dve.tensor_copy(recsf[:, :, R_TYPE], in_typ))
            link(dve.tensor_copy(recsf[:, :, R_W], in_w))
            dve.tensor_copy(recsf[:, :, R_BIAS:], in_att.rearrange("p (t h) -> p t h", h=H)).then_inc(recs_done, 1)
            dve.wait_ge(recs_done, 1)
            for k, field in ((0, in_dst), (1, in_src)):
                link(dve.tensor_copy(in_it, field))
                link(dve.tensor_scalar(in_it, in_it, 7, None, ALU.arith_shift_right))
                link(dve.tensor_copy(tile_of, in_it))
                for b in range(NB):
                    link(dve.tensor_scalar(junk, tile_of, float(b), None, ALU.is_equal, ALU.add,
                                           accum_out=cntn[k][:, b:b + 1]))
                dve.sem_inc(s_("v_cnt"), 1)
            link(dve.memset(G[:, 0, :], float(NOEDGE)))
            dve.sem_inc(s_("pad_m"), 1)
            for k in range(2):
                dve.wait_ge(pe_set, 3 * k + 1)
                link(dve.tensor_scalar(smalli[0:NB, 0:1], PS[5][0:NB, 0:1], float(P - 1), None, ALU.add))
                link(dve.tensor_scalar(smalli[0:NB, 1:2], smalli[0:NB, 0:1], 7, None, ALU.arith_shift_right))
                link(dve.tensor_copy(small[0:NB, 1:2], smalli[0:NB, 1:2]))
                dve.scalar_tensor_tensor(small[0:NB, 2:3], small[0:NB, 1:2], float(-P), PS[5][0:NB, 0:1],
                                         ALU.mult, ALU.add).then_inc(s_("v_nt"), 1)
                dve.wait_ge(pe_set, 3 * k + 2)
                dve.wait_ge(consts, 6)
                link(dve.tensor_copy(small[0:NB, 3:4], PS[5][0:NB, 8:9]))
                dve.tensor_scalar(past, iota_f[0:NB, 0:T], small[0:NB, 3:4], None, ALU.is_ge
                                  ).then_inc(s_("v_nt"), 1)
                dve.wait_ge(pe_set, 3 * k + 3)
                link(dve.tensor_scalar(bs_row[k][:, :], PS[6][0:1, 0:T], float(NB - 1), None, ALU.min))
                link(dve.scalar_tensor_tensor(sg_row[:, :], iota_f[0:1, 0:T], float(P), PS[7][0:1, 0:T],
                                              ALU.mult, ALU.add))
                link(dve.tensor_scalar(as_row[k][:, :], sg_row[:, :], float(E), None, ALU.min))
                link(dve.tensor_scalar((dstl, offs)[k][:, :], PS[4][:, 0:T], float(NB - 1), -float(P),
                                       ALU.min, ALU.mult))
            dve.sem_inc(v_set, 2)
            dve.wait_ge(pe_set, 7)
            link(dve.tensor_copy(cnt[:, :], PS[5][:, 0:NB]))
            link(dve.tensor_tensor_scan(place[:, :], ones[:, 0:NB], cnt[:, :], -1.0, ALU.mult, ALU.add))
            link(dve.tensor_tensor(place[:, :], place[:, :], cnt[:, :], ALU.subtract))
            link(dve.tensor_tensor(place[:, :], place[:, :], PS[4][:, 0:NB], ALU.add))
            link(dve.memset(ones_t, 1.0))
            link(dve.memset(pos, 0.0))
            for b in range(NB):
                link(dve.tensor_scalar(junk, tile_of, float(b), None, ALU.is_equal))
                link(dve.tensor_tensor_scan(run_to, ones_t, junk, place[:, b:b + 1], ALU.mult, ALU.add))
                link(dve.tensor_tensor(run_to, run_to, junk, ALU.mult))
                link(dve.tensor_tensor(pos, pos, run_to, ALU.add))
            dve.tensor_copy(recs[:, :, R_POS], pos).then_inc(recs_done, 1)
            dve.wait_ge(rec_in, 16 * T)
            dve.wait_ge(v_set, 3)
            link(dve.tensor_tensor(dstl[:, :], dstl[:, :], recf3[:, :, R_DST], ALU.add))
            link(dve.memset(acc[:, :], 0.0))
            link(dve.tensor_scalar(small_t[:, :], dstl[:, :], 0.0, None, ALU.is_ge))
            link(dve.scalar_tensor_tensor(small_t[:, :], dstl[:, :], float(P), small_t[:, :], ALU.is_lt, ALU.mult))
            link(dve.tensor_tensor(recf3[:, :, R_BIAS:], recf3[:, :, R_BIAS:],
                                   small_t[:, :, None].to_broadcast([P, T, H]), ALU.mult))
            link(dve.tensor_scalar(small_t[:, :], small_t[:, :], -float(NOEDGE), float(NOEDGE), ALU.mult, ALU.add))
            link(dve.tensor_tensor(rec3[:, :, R_POS], rec3[:, :, R_POS], small_t[:, :], ALU.add))
            link(dve.memset(posi[:, T:], 0))
            link(dve.tensor_copy(posi[:, 0:T], rec3[:, :, R_POS]))
            link(dve.tensor_copy(srci[:, 0:T], rec3[:, :, R_SRC]))
            dve.sem_inc(s_("places"), 1)
            done = link.n

            def onehot(ready):
                def stage(t, r, turn):
                    dve.tensor_scalar(oh[:, r % U, :], iota_f[:, 0:P], column(dstl, t), None,
                                      ALU.is_equal).then_inc(ready, 1)
                return stage

            def add_up(p, w, k=0):
                def stage(t, r, turn):
                    tile = node_tile(dve, k, t)
                    to = acc[:, ds(tile * ACCW, w)]
                    dve.wait_ge(p.used, t + (1 + AHEAD))
                    dve.wait_ge(p.added, t + PR)
                    dve.tensor_tensor(to, to, PS[4 + r % PR][:, 0:w], ALU.add).then_inc(p.added, 1)
                return stage

            def types(t, r, turn):
                dve.tensor_scalar(G[:, r, D:D + NREL], iota_f[:, 0:NREL],
                                  column(recf, t, RECW, R_TYPE), None, ALU.is_equal).then_inc(p2.oh, 1)

            def sums(p):
                dve.sem_inc(p.added, PR)
                staged(dve, T, U, (4, onehot(p.oh)), (0, add_up(p, p.w)))

            def norm(name, b, lkn, to):
                lkn(dve.bn_stats(stats[:, 0:6], Y[:, :]))
                settle(dve)
                dve.bn_aggr(mv[:, 0:2], stats[:, 0:6]).then_inc(s_("var"), 1)
                dve.wait_ge(s_("std"), b + (NORMS.index(name) * NB + 1))
                lkn(dve.reciprocal(mv[:, 3:4], mv[:, 2:3]))
                return dve.tensor_scalar(to, Y[:, :], mv[:, 0:1], mv[:, 3:4], ALU.subtract, ALU.mult)

            def message(t, r, turn):
                dve.wait_ge(pm.used, t + (1 + AHEAD - GR))
                dve.wait_ge(s_("send_sel"), t + (1 + U))
                dve.tensor_scalar(G[:, r, 0:D], PS[4 + r % PR][:, 0:D], column(recf, t, RECW, R_W),
                                  None, ALU.mult).then_inc(pm.added, 1)
                dve.tensor_scalar(G[:, r, D:MW], column(rec, t, RECW, R_SRC),
                                  1.0, None, ALU.mult).then_inc(pm.oh, 1)

            dve.sem_inc(pm.added, PR)
            staged(dve, T, GR, (4, onehot(s_("send_1h"))), (0, message))

            dve.wait_ge(pm.oh, T)
            dve.sem_inc(p0.added, PR)
            staged(dve, T, U, (0, add_up(p0, D, 1)))
            dve.wait_ge(ld_x, 32)
            dve.wait_ge(p0.added, T + PR)
            dve.sem_inc(s_("n1_free"), 1)
            k1 = s_("n1_link")
            def n1_rows(b, r, turn):
                ln = Link(dve, k1, 0, b, 4)
                dve.wait_ge(s_("n1_h"), b + 1)
                dve.tensor_tensor(Y[:, :], X[:, ds(b * D, D)], PS[(1, 5)[r]][:, 0:D], ALU.add
                                  ).then_inc(s_("n1_y"), 1)
                dve.wait_ge(s_("n1_y"), b + 1)
                wait_old(dve, s_("n1_xT"), b)
                ln(norm("n1", b, ln, XS[:, :]))
                dve.sem_inc(s_("n1_ln"), 1)
                settle(dve)
                ln(dve.tensor_copy(X[:, ds(b * D, D)], XS[:, :]))
                ln.end()

            staged(dve, NB, 2, (2, n1_rows))
            dve.wait_ge(s_("n1_qkv"), NB)
            link2 = Link(dve, lk, done)
            def product(t, r, turn):
                dve.wait_ge(s_("keys_sel"), t + (1 + U))
                dve.wait_ge(pk.rows[r], turn * 16 + (pk.base + 16))
                dve.wait_ge(s_("keys_red"), t + 1)
                dve.tensor_tensor(prod[:, r % 4, :], G[:, r, 0:D], PS[4 + r % PR][:, 0:D], ALU.mult
                                  ).then_inc(pk.used, 1)

            def score(t, r, turn):
                dve.wait_ge(pk.used, t + (1 + AHEAD))
                dve.tensor_reduce(column(S, t, H, 0, H),
                                  prod[:, r % 4, :].rearrange("p (h d) -> p h d", h=H), AX.X, ALU.add
                                  ).then_inc(s_("keys_red"), 1)

            dve.sem_inc(pk.used, AHEAD)
            dve.sem_inc(s_("keys_red"), 4)
            staged(dve, T, GR, (4, onehot(s_("keys_1h"))), (1, product), (0, score))
            dve.wait_ge(s_("keys_red"), T + 4)
            def group_scores(g):
                settle(dve)
                dve.tensor_copy(dg[:, :].rearrange("p (t h) -> p t h", h=H),
                                recf[:, ds(g * (GRP * RECW), GRP * RECW)]
                                .rearrange("p (t c) -> p t c", c=RECW)[:, :, R_DST:R_DST + 1]
                                .to_broadcast([P, GRP, H])).then_inc(s_("m_dg"), 1)
                dve.tensor_tensor(sg[:, :].rearrange("p (t h) -> p t h", h=H),
                                  S[:, ds(g * P, P)].rearrange("p (t h) -> p t h", h=H),
                                  recf[:, ds(g * (GRP * RECW), GRP * RECW)]
                                  .rearrange("p (t c) -> p t c", c=RECW)[:, :, R_BIAS:], ALU.add
                                  ).then_inc(s_("m_dg"), 1)
                dve.wait_ge(s_("m_dg"), g * 2 + 2)
                dve.sem_inc(s_("m_sg"), 1)

            def group_maxima(g):
                ln = Link(dve, s_("m_link"), 0, g, 4)
                dve.wait_ge(s_("m_Tc"), g * 3 + 3)
                if not isinstance(g, int) or g > 0:
                    dve.wait_ge(s_("m_row"), g * 2)
                ln(dve.tensor_tensor(fl[:, :], dT[:, 1:P + 1], dT[:, 0:P], ALU.not_equal))
                ln(dve.tensor_scalar(fl[:, :], fl[:, :], -BIG, None, ALU.mult))
                dve.tensor_tensor(la[:, :], dT[:, 1:P + 1], dT[:, 2:P + 2], ALU.not_equal).then_inc(s_("m_la"), 1)
                ln(dve.tensor_tensor_scan(ms[:, :], fl[:, :], sT[:, :], -BIG, ALU.add, ALU.max))
                dve.wait_ge(s_("m_la"), g + 1)
                ln(dve.tensor_tensor(ms[:, :], ms[:, :], la[:, :], ALU.mult))
                dve.sem_inc(s_("m_ms"), 1)
                ln.end()

            def m_groups(c, r, turn):
                g = turn * 2 + r // 4
                if r % 4 == 0 and not (isinstance(g, int) and g + 1 >= GROUPS):
                    group_maxima(g + 1)
                if r % 4 == 2 and not (isinstance(g, int) and g + 2 >= GROUPS):
                    group_scores(g + 2)

            def m_onehot(c, r, turn):
                dve.wait_ge(s_("m_mm"), c + 1)
                dve.tensor_tensor(oh[:, r % 2 * 4:r % 2 * 4 + 4, :],
                                  iota_f[:, None, 0:P].to_broadcast([P, 4, P]),
                                  column(dstl, c, 4, 0, 4)[:, :, None].to_broadcast([P, 4, P]), ALU.is_equal
                                  ).then_inc(s_("m_oh"), 1)

            def m_keep(c, r, turn):
                dve.wait_ge(s_("m_off"), c + 1)
                dve.tensor_tensor(column(top, c, 4 * H, 0, 4 * H).rearrange("p (t h) -> p t h", h=H),
                                  PS[4 + r % PR][:, 0:4 * (H + 1)].rearrange("p (t h) -> p t h", h=H + 1)[:, :, 0:H],
                                  off[:, r % 4, :, None].to_broadcast([P, 4, H]), ALU.add
                                  ).then_inc(s_("m_added"), 1)

            begins = gru[:, 0:T + 1]
            link2(dve.tensor_tensor(offs[:, :], dstl[:, :], recf3[:, :, R_DST], ALU.subtract))
            link2(dve.memset(begins, 0.0))
            link2(dve.tensor_tensor(begins[:, 1:T], offs[:, 1:T], offs[:, 0:T - 1], ALU.not_equal))
            link2(dve.tensor_scalar(begins, begins, -BIG, None, ALU.mult))
            group_scores(0)
            group_maxima(0)
            group_scores(1)
            dve.sem_inc(s_("m_added"), 4)
            staged(dve, T // 4, 8, (0, m_groups), (1, m_onehot), (0, m_keep), tail=1)
            dve.wait_ge(s_("m_added"), T // 4 + 4)
            top3 = top.rearrange("p (t h) -> p t h", h=H)
            run3 = acc[:, 0:T * H].rearrange("p (t h) -> p t h", h=H)
            for h in range(H):
                dve.tensor_tensor_scan(run3[:, :, h], begins[:, 0:T], top3[:, :, h], -BIG, ALU.add, ALU.max
                                       ).then_inc(s_("m_run"), 1)
            dve.wait_ge(s_("m_run"), H)
            for h in range(H):
                dve.tensor_tensor_scan(top3[:, ::-1, h], begins[:, 1:T + 1][:, ::-1], run3[:, ::-1, h], -BIG,
                                       ALU.add, ALU.max).then_inc(s_("m_run"), 1)
            dve.wait_ge(s_("m_run"), 2 * H)
            link2(dve.memset(acc[:, :], 0.0))
            def below(t, r, turn):
                dve.wait_ge(s_("vals_sel"), t + (1 + U))
                dve.wait_ge(pv.used, t + (1 + AHEAD - 4))
                dve.tensor_tensor(work[:, r % 4, D:D + H], column(S, t, H, 0, H), PS[2 + r % 2][:, 0:H],
                                  ALU.subtract).then_inc(s_("vals_d"), 1)

            def weigh(t, r, turn):
                dve.wait_ge(s_("vals_e"), t + 1)
                dve.wait_ge(pv.rows[r], turn * 16 + (pv.base + 16))
                dve.tensor_tensor(work[:, r % 4, 0:D].rearrange("p (h d) -> p h d", h=H),
                                  G[:, r, 0:D].rearrange("p (h d) -> p h d", h=H),
                                  work[:, r % 4, D:D + H, None].to_broadcast([P, H, DH]), ALU.mult
                                  ).then_inc(s_("vals_vp"), 1)

            dve.sem_inc(pv.added, PR)
            dve.sem_inc(s_("vals_d"), 2)
            staged(dve, T, GR, (6, onehot(s_("vals_1h"))), (3, below), (2, weigh),
                   (0, add_up(pv, D + H)))
            dve.wait_ge(pv.added, T + PR)
            def n2_divide(b, r, turn):
                ln = Link(dve, s_("m_la"), GROUPS, b, 2)
                ln(dve.tensor_scalar(small[:, 0:H], acc[:, ds(b * ACCW + D, H)], 1e-30, None, ALU.max))
                ln(dve.reciprocal(small[:, 8:8 + H], small[:, 0:H]))
                ln.end()
                wait_old(dve, s_("n2_aT"), b)
                settle(dve)
                dve.tensor_tensor(A[:, :].rearrange("p (h d) -> p h d", h=H),
                                  acc[:, ds(b * ACCW, D)].rearrange("p (h d) -> p h d", h=H),
                                  small[:, 8:8 + H, None].to_broadcast([P, H, DH]), ALU.mult
                                  ).then_inc(s_("n2_a"), 1)

            def n2_rows(b, r, turn):
                ln = Link(dve, s_("n2_link"), 0, b, 3)
                dve.wait_ge(s_("n2_h"), b + 1)
                dve.tensor_tensor(Y[:, :], X[:, ds(b * D, D)], PS[1 + r][:, 0:D], ALU.add
                                  ).then_inc(s_("n2_y"), 1)
                dve.wait_ge(s_("n2_y"), b + 1)
                dve.wait_ge(tabs, b * 16 + 16 * 2 * NB)
                norm("n2", b, ln, XS[:, :]).then_inc(s_("n2_x"), 1)
                dve.wait_ge(s_("n2_x"), b + 1)
                settle(dve)
                ln(dve.tensor_copy(X[:, ds(b * D, D)], XS[:, :]))
                ln.end()

            staged(dve, NB, 2, (1, n2_rows), (4, n2_divide))
            link2(dve.memset(acc[:, :], 0.0))
            dve.sem_inc(p2.added, PR)
            staged(dve, T, GR, (4, types), (4, onehot(p2.oh)), (0, add_up(p2, D + NREL)))
            dve.wait_ge(p2.added, T + PR)
            acc3 = acc[:, :].rearrange("p (b w) -> p b w", w=ACCW)
            link2(dve.tensor_reduce(dinv[:, :], acc3[:, :, D:D + NREL], AX.X, ALU.add))
            dve.tensor_scalar(dinv[:, :], dinv[:, :], 1.0, None, ALU.add).then_inc(s_("n3_deg"), 1)
            dve.wait_ge(s_("n3_degs"), 1)
            link2(dve.reciprocal(dinv[:, :], dinv[:, :]))
            dve.wait_ge(tabs, 16 * 3 * NB)
            def n3_rows(b, r, turn):
                ln = Link(dve, s_("n3_link"), 0, b, 8)
                xb = X[:, ds(b * D, D)]
                nn = PS[(4, 7)[r]]
                dve.wait_ge(s_("n3_rz"), b + 1)
                ln(dve.tensor_tensor(TG, gru[:, 0:D], nn[:, D:2 * D], ALU.mult))
                dve.tensor_tensor(TG, TG, nn[:, 0:D], ALU.add).then_inc(s_("n3_t"), 1)
                dve.wait_ge(s_("n3_n"), b + 1)
                ln(dve.tensor_tensor(Y[:, :], xb, gru[:, 2 * D:3 * D], ALU.subtract))
                ln(dve.tensor_tensor(Y[:, :], Y[:, :], gru[:, D:2 * D], ALU.mult))
                ln(dve.tensor_tensor(Y[:, :], Y[:, :], gru[:, 2 * D:3 * D], ALU.add))
                ln(dve.tensor_tensor(Y[:, :], Y[:, :], xb, ALU.add))
                wait_old(dve, s_("n3_xT"), b)
                norm("n3", b, ln, XS[:, :]).then_inc(s_("n3_ln"), 1)
                dve.wait_ge(s_("n3_ln"), b + 1)
                settle(dve)
                ln(dve.tensor_copy(xb, XS[:, :]))
                ln.end()

            def n3_features(b, r, turn):
                dve.wait_ge(s_("n3_h1"), b + 1)
                dve.wait_ge(tabs, b * 16 + 16 * 3 * NB)
                wait_old(dve, s_("n3_hs"), b)
                dve.tensor_scalar(KV[:, 0:D1], PS[2][:, 0:D1], dinv[:, ds(b, 1)], None, ALU.mult
                                  ).then_inc(s_("n3_h"), 1)
                dve.wait_ge(s_("n3_h"), b + 1)
                settle(dve)
                dve.tensor_copy(Q[:, ds(b * D, D1)], KV[:, 0:D1]).then_inc(s_("n3_hs"), 1)

            staged(dve, NB, 2, (2, n3_rows), (1, n3_features))
            link2(dve.memset(acc[:, :], 0.0))
            sums(pc1)
            dve.wait_ge(pc1.added, T + PR)

            def gcn(name, b, ln, w, boff):
                ln(dve.tensor_tensor(A[:, 0:w], acc[:, ds(b * ACCW, w)], Q[:, ds(b * D, w)], ALU.add))
                ln(dve.scalar_tensor_tensor(A[:, 0:w], A[:, 0:w], dinv[:, ds(b, 1)],
                                            b12[:, boff:boff + w], ALU.mult, ALU.add))
                dve.tensor_scalar(A[:, 0:w], A[:, 0:w], 0.0, None, ALU.max).then_inc(s_(name + "_a"), 1)

            dve.wait_ge(tabs, 16 * 4 * NB)
            dve.wait_ge(s_("n3_hs"), NB)
            with dve.Fori(0, NB) as b:
                ln = Link(dve, s_("n4_link"), 0, b, 2)
                gcn("n4", b, ln, D1, 0)
                dve.wait_ge(s_("n4_h2"), b + 1)
                dve.wait_ge(tabs, b * 16 + 16 * 4 * NB)
                dve.tensor_scalar(KV[:, 0:D2], PS[1][:, 0:D2], dinv[:, ds(b, 1)], None, ALU.mult
                                  ).then_inc(s_("n4_h"), 1)
                dve.wait_ge(s_("n4_h"), b + 1)
                settle(dve)
                dve.tensor_copy(Q[:, ds(b * D, D2)], KV[:, 0:D2]).then_inc(s_("n4_hs"), 1)
                ln.end()
            link2(dve.memset(acc[:, :], 0.0))
            sums(pc2)
            dve.wait_ge(pc2.added, T + PR)
            dve.wait_ge(tabs, 16 * 5 * NB)
            dve.wait_ge(s_("n4_hs"), NB)
            def n5_in(b, r, turn):
                wait_old(dve, s_("n5_aT"), b)
                gcn("n5", b, Link(dve, s_("n5_alink"), 0, b, 2), D2, D1)

            def n5_rows(b, r, turn):
                ln = Link(dve, s_("n5_link"), 0, b, 3)
                dve.wait_ge(s_("n5_f2"), b + 1)
                dve.tensor_tensor(Y[:, :], X[:, ds(b * D, D)], PS[3 + r][:, 0:D], ALU.add
                                  ).then_inc(s_("n5_y"), 1)
                dve.wait_ge(s_("n5_y"), b + 1)
                ln(norm("n5", b, ln, X[:, ds(b * D, D)]))
                ln.end()

            staged(dve, NB, 2, (2, n5_rows), (6, n5_in))
            dve.sem_inc(s_("n5_done"), 1)


_INS = ['x', 'src', 'dst', 'edge_attr_8', 'edge_type_16', 'edge_weight', 'L0_gnn_W', 'L0_gnn_b', 'L1_gnn_Wq',
        'L1_gnn_Wk', 'L1_gnn_Wv', 'L1_gnn_Wo', 'L2_gnn_relvectors', 'L2_gnn_w_ih', 'L2_gnn_w_hh', 'L2_gnn_b_ih',
        'L2_gnn_b_hh', 'L3_gnn_W1', 'L3_gnn_b1', 'L3_gnn_W2', 'L3_gnn_b2', 'L3_gnn_fc1_w', 'L3_gnn_fc1_b',
        'L3_gnn_fc2_w', 'L3_gnn_fc2_b']


def kernel(**inputs):
    import numpy as _np
    import concourse.bacc as _bacc
    from concourse import mybir as _mybir
    from concourse.bass_utils import run_bass_kernel_spmd as _run

    nc = _bacc.Bacc("TRN2", target_bir_lowering=False, num_devices=1)
    arrays, args = {}, []
    for name in _INS:
        a = _np.ascontiguousarray(inputs[name])
        arrays[f"in_{name}_dram"] = a
        args.append(nc.dram_tensor(f"in_{name}_dram", a.shape, _mybir.dt.from_np(a.dtype), kind="ExternalInput").ap())
    out = nc.dram_tensor("out_0_dram", tuple(inputs['x'].shape), _mybir.dt.float32, kind="ExternalOutput").ap()
    gnn_kernel(nc, *args, out)
    r = _run(nc, [arrays], core_ids=[0])
    return r.results[0]["out_0_dram"]
```
